# Optimizing a Trainium2 kernel written in Bass

```python
import numpy as np
import jax
import jax.numpy as jnp

def _softmax(x, axis=-1):
    return jax.nn.softmax(x, axis=axis)

def _gelu(x):
    return jax.nn.gelu(x, approximate=True)

def _silu(x):
    return jax.nn.silu(x)

def _sigmoid(x):
    return jax.nn.sigmoid(x)

def _layernorm(x, axis=-1, eps=1e-05):
    m = jnp.mean(x, axis=axis, keepdims=True)
    v = jnp.var(x, axis=axis, keepdims=True)
    return (x - m) / jnp.sqrt(v + eps)

def _scatter_add(tgt, idx, src, axis=0):
    return tgt.at[idx].add(src)

def _segment_sum(src, seg, n):
    return jax.ops.segment_sum(src, seg, n)
kernel_name = 'mk_decoder_preln_d1_seqx_r4_2eb16f'

def setup_inputs(seed: int=0):
    np.random.seed(seed)
    _w = jnp.asarray

    def _rec_inputs():
        import jax
        import jax.numpy as jnp
        _rk = jax.random.key(seed)
        x = -0.0003929 + 0.9999 * jax.random.normal(jax.random.fold_in(_rk, 1), (4, 512, 1024), jnp.float32)
        _lenS = 512 - jax.random.randint(jax.random.fold_in(_rk, 7), (4,), 0, max(1, 512 // 4) + 1, jnp.int32)
        _lenS2 = 64 - jax.random.randint(jax.random.fold_in(_rk, 8), (4,), 0, max(1, 64 // 4) + 1, jnp.int32)
        _ctx_1024P = jax.random.normal(jax.random.fold_in(_rk, 11), (4, 16, 256), jnp.float32)
        _ctx_1024c = jax.random.dirichlet(jax.random.fold_in(_rk, 511), 0.3 * jnp.ones((16,), jnp.float32), (4, 64))
        _ctx_1024t = jnp.einsum('bsk,bkd->bsd', _ctx_1024c, _ctx_1024P)
        _ctx_1024t = _ctx_1024t * jax.lax.rsqrt(jnp.mean(jnp.square(_ctx_1024t)) + 1e-12) * 0.953939
        ctx_1024 = -1.39393e-06 + 0.999914 * (_ctx_1024t + 0.3 * jax.random.normal(jax.random.fold_in(_rk, 611), (4, 64, 256), jnp.float32))
        _validS = jnp.arange(512)[None, :] < _lenS[:, None]
        _validS2 = jnp.arange(64)[None, :] < _lenS2[:, None]
        _causal = jnp.tril(jnp.ones((512, 512), dtype=bool))
        mask_SxS2_ff0 = jnp.where(jnp.ones((512, 64), dtype=bool), 0.0, -1000000000.0).astype(jnp.float32)
        return (x, ctx_1024, mask_SxS2_ff0)
    x, ctx_1024, mask_SxS2_ff0 = _rec_inputs()

    def _L0_attn_setup():
        import jax, jax.numpy as jnp
        import numpy as np
        N_HEADS = 32
        N_KV_HEADS = 16
        N_EMBD = 1024
        HEAD_DIM = N_EMBD // N_HEADS
        GROUPS = N_HEADS // N_KV_HEADS
        KV_DIM = N_KV_HEADS * HEAD_DIM
        SCALE = 1.0 / np.sqrt(np.float32(N_HEADS))
        key = jax.random.key(seed)
        ks = jax.random.split(key, 4)
        B, T, C = (1, 512, N_EMBD)
        s = 1.0 / np.sqrt(np.float32(C))
        return {'x': jax.random.normal(ks[0], (B, T, C), dtype=jnp.float32), 'Wq': jax.random.normal(ks[1], (C, C), dtype=jnp.float32) * s, 'bq': jnp.zeros((C,), dtype=jnp.float32), 'Wk': jax.random.normal(ks[2], (KV_DIM, C), dtype=jnp.float32) * s, 'bk': jnp.zeros((KV_DIM,), dtype=jnp.float32), 'Wv': jax.random.normal(ks[3], (KV_DIM, C), dtype=jnp.float32) * s, 'bv': jnp.zeros((KV_DIM,), dtype=jnp.float32)}
    _L0_attn_all = _L0_attn_setup()
    _L0_attn_in = {k: v for k, v in _L0_attn_all.items() if k in ('Wq', 'bq', 'Wk', 'bk', 'Wv', 'bv')}
    del _L0_attn_all

    def _L0_xattn_setup():
        import math
        import jax, jax.numpy as jnp
        import numpy as np
        N_HEADS = 32
        N_KV_HEADS = 8
        N_REP = N_HEADS // N_KV_HEADS
        HEAD_DIM = 1024 // N_HEADS
        key = jax.random.key(seed)
        kq, kk, kv = jax.random.split(key, 3)
        B, S, T = (2, 512, 512)
        q = jax.random.normal(kq, (B, S, N_HEADS * HEAD_DIM), dtype=jnp.float32)
        k = jax.random.normal(kk, (B, T, N_KV_HEADS * HEAD_DIM), dtype=jnp.float32)
        v = jax.random.normal(kv, (B, T, N_KV_HEADS * HEAD_DIM), dtype=jnp.float32)
        mask = jnp.zeros((S, T), dtype=jnp.float32)
        return {'q': q, 'k': k, 'v': v, 'start_pos': 0, 'mask': mask}
    _L0_xattn_all = _L0_xattn_setup()
    _L0_xattn_in = {k: v for k, v in _L0_xattn_all.items() if k in ()}
    del _L0_xattn_all

    def _L0_ffn_setup():
        import jax, jax.numpy as jnp
        import numpy as np
        BLOCK = 64
        NF4_CODE = jnp.array([-1.0, -0.6961928009986877, -0.5250730514526367, -0.39491748809814453, -0.28444138169288635, -0.18477343022823334, -0.09105003625154495, 0.0, 0.07958029955625534, 0.16093020141124725, 0.24611230194568634, 0.33791524171829224, 0.44070982933044434, 0.5626170039176941, 0.7229568362236023, 1.0], dtype=jnp.float32)

        def dequant_nf4(q, absmax, shape):
            w = NF4_CODE[q.reshape(-1)]
            w = w.reshape(-1, BLOCK) * absmax[:, None]
            return w.reshape(shape)
        key = jax.random.key(seed)
        ks = jax.random.split(key, 7)
        HD, M = (1024, 3584)
        nblk = HD * M // BLOCK
        x = jax.random.normal(ks[0], (2, 512, HD), dtype=jnp.float32)
        gate_q = jax.random.randint(ks[1], (M, HD), 0, 16, dtype=jnp.int32)
        up_q = jax.random.randint(ks[2], (M, HD), 0, 16, dtype=jnp.int32)
        down_q = jax.random.randint(ks[3], (HD, M), 0, 16, dtype=jnp.int32)
        gate_absmax = jax.random.uniform(ks[4], (nblk,), dtype=jnp.float32) * 0.05
        up_absmax = jax.random.uniform(ks[5], (nblk,), dtype=jnp.float32) * 0.05
        down_absmax = jax.random.uniform(ks[6], (nblk,), dtype=jnp.float32) * 0.05
        return {'x': x, 'gate_q': gate_q, 'gate_absmax': gate_absmax, 'up_q': up_q, 'up_absmax': up_absmax, 'down_q': down_q, 'down_absmax': down_absmax}
    _L0_ffn_all = _L0_ffn_setup()
    _L0_ffn_in = {k: v for k, v in _L0_ffn_all.items() if k in ('gate_q', 'gate_absmax', 'up_q', 'up_absmax', 'down_q', 'down_absmax')}
    del _L0_ffn_all
    return {'x': x, 'ctx_1024': ctx_1024, 'mask_SxS2_ff0': mask_SxS2_ff0, 'L0_attn_Wq': _L0_attn_in['Wq'], 'L0_attn_bq': _L0_attn_in['bq'], 'L0_attn_Wk': _L0_attn_in['Wk'], 'L0_attn_bk': _L0_attn_in['bk'], 'L0_attn_Wv': _L0_attn_in['Wv'], 'L0_attn_bv': _L0_attn_in['bv'], 'L0_ffn_gate_q': _L0_ffn_in['gate_q'], 'L0_ffn_gate_absmax': _L0_ffn_in['gate_absmax'], 'L0_ffn_up_q': _L0_ffn_in['up_q'], 'L0_ffn_up_absmax': _L0_ffn_in['up_absmax'], 'L0_ffn_down_q': _L0_ffn_in['down_q'], 'L0_ffn_down_absmax': _L0_ffn_in['down_absmax']}

def reference(x, ctx_1024, mask_SxS2_ff0, L0_attn_Wq, L0_attn_bq, L0_attn_Wk, L0_attn_bk, L0_attn_Wv, L0_attn_bv, L0_ffn_gate_q, L0_ffn_gate_absmax, L0_ffn_up_q, L0_ffn_up_absmax, L0_ffn_down_q, L0_ffn_down_absmax):
    import jax
    import jax.numpy as jnp

    def _L0_attn_ref(x, Wq, bq, Wk, bk, Wv, bv):
        import jax, jax.numpy as jnp
        import numpy as np
        N_HEADS = 32
        N_KV_HEADS = 16
        N_EMBD = 1024
        HEAD_DIM = N_EMBD // N_HEADS
        GROUPS = N_HEADS // N_KV_HEADS
        KV_DIM = N_KV_HEADS * HEAD_DIM
        SCALE = 1.0 / np.sqrt(np.float32(N_HEADS))
        B, T, C = x.shape
        q = (x @ Wq.T + bq).reshape(B, T, N_HEADS, HEAD_DIM)
        k = (x @ Wk.T + bk).reshape(B, T, N_KV_HEADS, HEAD_DIM)
        v = (x @ Wv.T + bv).reshape(B, T, N_KV_HEADS, HEAD_DIM)
        q = q.transpose(0, 2, 1, 3).reshape(B, GROUPS, N_KV_HEADS, T, HEAD_DIM)
        k = k.transpose(0, 2, 1, 3)
        v = v.transpose(0, 2, 1, 3)
        scores = jnp.einsum('bgkqd,bkld->bgkql', q, k) * SCALE
        causal = jnp.tril(jnp.ones((T, T), dtype=bool))
        scores = jnp.where(causal, scores, jnp.float32(-jnp.inf))
        w = jax.nn.softmax(scores, axis=-1)
        out = jnp.einsum('bgkql,bkld->bgkqd', w, v)
        out = out.reshape(B, N_HEADS, T, HEAD_DIM).transpose(0, 2, 1, 3).reshape(B, T, C)
        return out

    def _L0_xattn_ref(q, k, v, start_pos, mask):
        import math
        import jax, jax.numpy as jnp
        import numpy as np
        N_HEADS = 32
        N_KV_HEADS = 8
        N_REP = N_HEADS // N_KV_HEADS
        HEAD_DIM = 1024 // N_HEADS
        b, s, _ = q.shape
        t = k.shape[1]
        xq = q.reshape(b, s, N_KV_HEADS, N_REP, HEAD_DIM)
        xk = k.reshape(b, t, N_KV_HEADS, HEAD_DIM)
        xv = v.reshape(b, t, N_KV_HEADS, HEAD_DIM)
        scores = jnp.einsum('bsgrd,btgd->bgrst', xq, xk) / math.sqrt(HEAD_DIM)
        scores = scores + mask
        probs = jax.nn.softmax(scores.astype(jnp.float32), axis=-1).astype(q.dtype)
        out = jnp.einsum('bgrst,btgd->bsgrd', probs, xv)
        return out.reshape(b, s, N_HEADS * HEAD_DIM)

    def _L0_ffn_ref(x, gate_q, gate_absmax, up_q, up_absmax, down_q, down_absmax):
        import jax, jax.numpy as jnp
        import numpy as np
        BLOCK = 64
        NF4_CODE = jnp.array([-1.0, -0.6961928009986877, -0.5250730514526367, -0.39491748809814453, -0.28444138169288635, -0.18477343022823334, -0.09105003625154495, 0.0, 0.07958029955625534, 0.16093020141124725, 0.24611230194568634, 0.33791524171829224, 0.44070982933044434, 0.5626170039176941, 0.7229568362236023, 1.0], dtype=jnp.float32)

        def dequant_nf4(q, absmax, shape):
            w = NF4_CODE[q.reshape(-1)]
            w = w.reshape(-1, BLOCK) * absmax[:, None]
            return w.reshape(shape)
        HD = x.shape[-1]
        M = gate_q.shape[0]
        Wg = dequant_nf4(gate_q, gate_absmax, (M, HD))
        Wu = dequant_nf4(up_q, up_absmax, (M, HD))
        Wd = dequant_nf4(down_q, down_absmax, (HD, M))
        g = jnp.einsum('bsh,mh->bsm', x, Wg)
        u = jnp.einsum('bsh,mh->bsm', x, Wu)
        h = jax.nn.silu(g) * u
        return jnp.einsum('bsm,hm->bsh', h, Wd)
    x = x + _L0_attn_ref(_layernorm(x, axis=-1), L0_attn_Wq, L0_attn_bq, L0_attn_Wk, L0_attn_bk, L0_attn_Wv, L0_attn_bv)
    x = x + _L0_xattn_ref(_layernorm(x, axis=-1), ctx_1024, ctx_1024, 0, mask_SxS2_ff0)
    x = x + _L0_ffn_ref(_layernorm(x, axis=-1), L0_ffn_gate_q, L0_ffn_gate_absmax, L0_ffn_up_q, L0_ffn_up_absmax, L0_ffn_down_q, L0_ffn_down_absmax)
    return x

_drawn_inputs = setup_inputs


def setup_inputs(seed=0):
    import zlib

    import numpy as np

    out = dict(_drawn_inputs(seed))
    spreads = {'mask_SxS2_ff0': (0.0, 0.648),
     'L0_attn_bq': (0.0, 0.635),
     'L0_attn_bk': (0.0, 0.8),
     'L0_attn_bv': (0.0, 0.1)}
    factors = {}
    for name, (base, spread) in spreads.items():
        noise = np.random.default_rng([zlib.crc32(name.encode()), seed]).standard_normal(out[name].shape)
        drawn = base * np.exp(spread * noise) if base else spread * noise
        out[name] = jnp.asarray(drawn.astype(out[name].dtype))
    for name, factor in factors.items():
        out[name] = (out[name] * factor).astype(out[name].dtype)
    return out
```

```python
import math

import numpy as np

import concourse.bass as bass
from concourse import mybir
from contextlib import ExitStack

FP32 = mybir.dt.float32
FP16 = mybir.dt.float16
BF16 = mybir.dt.bfloat16
INT32 = mybir.dt.int32
ALU = mybir.AluOpType
ACT = mybir.ActivationFunctionType
AX_X = mybir.AxisListType.X

B, T, C = 4, 512, 1024
H, KV, D = 32, 16, 32
TC, KVX = 64, 8
M = 3584
P = 128
CT = C // P
QT = T // P
RT = B * QT
UNITS = KV // 4
PAIRS = 4
CHUNKS = 5
MC = M // P
GROUPS = MC // 2
HALF = 512
EPS = 1e-5

W_SCALE = 256.0
F_SCALE = 512.0
H_SCALE = 16.0
NEG = -1.0e30
SELF_SCALE = 1.0 / math.sqrt(H)
CROSS_SCALE = 1.0 / math.sqrt(D)

NF4 = [-1.0, -0.6961928009986877, -0.5250730514526367, -0.39491748809814453, -0.28444138169288635,
       -0.18477343022823334, -0.09105003625154495, 0.0, 0.07958029955625534, 0.16093020141124725,
       0.24611230194568634, 0.33791524171829224, 0.44070982933044434, 0.5626170039176941,
       0.7229568362236023, 1.0]


def code_line(lo, hi):
    slope = np.float32(F_SCALE * (NF4[hi] - NF4[lo]) / (hi - lo))
    return float(slope), float(np.float32(F_SCALE * NF4[lo] - float(slope) * lo))


LOWER_LINES = [code_line(5, 6), code_line(3, 4), code_line(1, 2), code_line(0, 1)]
UPPER_LINES = [code_line(7, 8), code_line(9, 10), code_line(11, 12), code_line(13, 14), code_line(14, 15)]
LINES = LOWER_LINES + UPPER_LINES
NL = len(LINES)


def prepare(nc, t, dram):
    with ExitStack() as ctx:
        def sem(name):
            return ctx.enter_context(nc.semaphore(name))

        raw = ctx.enter_context(nc.sbuf_tensor("w_raw", [P, 2, 4 * HALF], FP32))
        w_loaded = [sem(f"w_loaded{i}") for i in range(2)]
        small_loaded = sem("small_loaded")
        w_high = sem("w_high")
        w_low = sem("w_low")
        zeroed = sem("zeroed")
        selected = sem("selected")
        block = ctx.enter_context(nc.Block())

        @block.sync
        def _(sp):
            for c in range(CT):
                if c >= 2:
                    sp.wait_ge(w_low, c - 1)
                sp.dma_start(raw[:, c % 2, :], dram["w"][c, :, :]).then_inc(w_loaded[c % 2], 16)
            sp.dma_start(t.bias_qk[:, :, :], dram["bias_qk"]).then_inc(small_loaded, 16)
            sp.dma_start(t.bias_v[:, :], dram["bias_v"].broadcast_to([P, KV * D])).then_inc(small_loaded, 16)
            sp.dma_start(t.mask[:, :, :], dram["mask"].rearrange("(r p) t -> p r t", p=P)).then_inc(small_loaded, 16)
            sp.wait_ge(small_loaded, 48)

        @block.scalar
        def _(act):
            for c in range(CT):
                act.wait_ge(w_loaded[c % 2], 16 * (c // 2 + 1))
                nc.scalar.activation(t.w_h[:, c, :], raw[:, c % 2, :], ACT.Copy, scale=W_SCALE).then_inc(w_high, 1)

        @block.vector
        def _(dve):
            for c in range(CT):
                dve.wait_ge(w_high, c + 1)
                nc.vector.scalar_tensor_tensor(t.w_l[:, c, :], raw[:, c % 2, :], W_SCALE, t.w_h[:, c, :],
                                               ALU.mult, ALU.subtract).then_inc(w_low, 1)

        @block.gpsimd
        def _(pool):
            cleared = [t.ident, t.ident_b, t.mask_qk, t.mask_kq, t.kx_h, t.kx_l, t.vx_h, t.vx_l, t.v_parts]
            for buf in cleared:
                nc.gpsimd.memset(buf[:], 0.0).then_inc(zeroed, 1)
            nc.gpsimd.memset(t.minus_half[:], -0.5).then_inc(zeroed, 1)
            pool.wait_ge(zeroed, len(cleared) + 1)
            for eye in (t.ident, t.ident_b):
                nc.gpsimd.affine_select(out=eye[:, :], in_=eye[:, :], compare_op=ALU.not_equal, fill=1.0, base=0,
                                        pattern=[[-1, P]], channel_multiplier=1).then_inc(selected, 1)
            nc.gpsimd.affine_select(out=t.mask_qk[:, :], in_=t.mask_qk[:, :], compare_op=ALU.is_ge, fill=NEG, base=0,
                                    pattern=[[-1, P]], channel_multiplier=1).then_inc(selected, 1)
            nc.gpsimd.affine_select(out=t.mask_kq[:, :], in_=t.mask_kq[:, :], compare_op=ALU.is_ge, fill=NEG, base=0,
                                    pattern=[[1, P]], channel_multiplier=-1).then_inc(selected, 1)
            nc.gpsimd.memset(t.v_parts[:, :, :, :, D:D + 1], 1.0).then_inc(selected, 1)
            pool.wait_ge(selected, 5)
            nc.gpsimd.memset(t.k_rows[96:97, :, :, :], 1.0).then_inc(selected, 1)
            for j in range(2):
                pool.wait_ge(selected, 6 + j)
                nc.gpsimd.memset(t.vx_h[TC * j:TC * j + TC, :, (D + 1) * j + D:(D + 1) * j + D + 1], 1.0)\
                    .then_inc(selected, 1)
            pool.wait_ge(selected, 8)


class Attention:

    def __init__(self, nc, ctx):
        def sb(name, shape, dt):
            return ctx.enter_context(nc.sbuf_tensor(name, shape, dt))

        self.w_h = sb("w_h", [P, CT, 4 * HALF], FP16)
        self.w_l = sb("w_l", [P, CT, 4 * HALF], FP16)
        self.ident = sb("ident", [P, P], FP32)
        self.ident_b = sb("ident_b", [P, P], BF16)
        self.mask_qk = sb("mask_qk", [P, P], BF16)
        self.mask_kq = sb("mask_kq", [P, P], BF16)
        self.minus_half = sb("minus_half", [P, 1], FP32)
        self.bias_qk = sb("bias_qk", [P, UNITS, 3], FP32)
        self.bias_v = sb("bias_v", [P, KV * D], FP32)
        self.mask = sb("mask_x", [P, QT, TC], FP32)
        self.kx_h = sb("kx_h", [P, KVX, 4 * TC], FP16)
        self.kx_l = sb("kx_l", [P, KVX, 4 * TC], FP16)
        self.vx_h = sb("vx_h", [P, KVX, 2 * (D + 1)], FP16)
        self.vx_l = sb("vx_l", [P, KVX, 2 * (D + 1)], FP16)
        self.q_rows = sb("q_rows", [97, 2, 2 * PAIRS, T], FP16)
        self.k_rows = sb("k_rows", [97, 2, PAIRS, T], FP16)
        self.v_parts = sb("v_parts", [P, 2, QT, PAIRS, 2 * D + 1], FP16)


def attention(nc, t, dram):
    with ExitStack() as ctx:
        def sb(name, shape, dt):
            return ctx.enter_context(nc.sbuf_tensor(name, shape, dt))

        def sem(name):
            return ctx.enter_context(nc.semaphore(name))

        x_in = sb("x_in", [P, QT, C], FP32)
        x_mid = sb("x_mid", [P, QT, C], FP32)
        xT_h = sb("xT_h", [P, CT, T], FP16)
        xT_l = sb("xT_l", [P, CT, T], FP16)
        stats = sb("stats", [P, 2, 2, 6], FP32)
        mean_var = sb("mean_var", [P, 2, 2], FP32)
        var_eps = sb("var_eps", [P, 2], FP32)
        rstd = sb("rstd", [P, 2], FP32)
        xn = sb("xn", [P, 2, C], FP32)
        proj32 = sb("proj32", [P, 2, HALF], FP32)
        nat_h = sb("nat_h", [P, 3, T], FP16)
        nat_l = sb("nat_l", [P, 3, T], FP16)
        v32 = sb("v32", [P, QT, PAIRS, D], FP32)
        block_max = sb("block_max", [P, PAIRS, CHUNKS, 4], FP32)
        row_max = sb("row_max", [P, PAIRS, 2, QT], FP32)
        neg_max = sb("neg_max", [2 * PAIRS * QT, P], FP16)
        p32 = sb("p32", [P, 4, HALF], FP32)
        p_h = sb("p_h", [P, 2, CHUNKS, HALF], FP16)
        p_l = sb("p_l", [P, 2, CHUNKS, HALF], FP16)
        r_sum = sb("r_sum", [P, 2, 2 * QT], FP32)
        o32 = sb("o32", [P, 2, QT, 2, D], FP32)
        k_raw = v32[:, :, :, :].rearrange("p q j d -> p (q j d)").rearrange("p (g t) -> p g t", t=TC)
        v_raw = o32[:, 1, :, :, :].rearrange("p q a d -> p (q a) d")
        s_top = sb("s_top", [P, 2, 8], FP32)
        s32 = p32[:, 0:2, :].rearrange("p s (a t) -> p s a t", t=TC)
        e32 = p32[:, 2:4, :]
        px_h, px_l = p_h[:, 0, 0:2, :], p_l[:, 0, 0:2, :]
        bank = [ctx.enter_context(nc.psum_tensor(f"bank{i}", [P, HALF], FP32)) for i in range(8)]
        LN_BANK, PROJ_BANK, T_BANK, O_BANK = 0, 2, 4, 7

        x_loaded = sem("x_loaded")
        ctx_loaded = sem("ctx_loaded")
        ctx_step = sem("ctx_step")
        ln_stat = sem("ln_stat")
        ln_rstd = sem("ln_rstd")
        ln_xn = sem("ln_xn")
        ln_turned = sem("ln_turned")
        ln_high = sem("ln_high")
        ln_low = sem("ln_low")
        proj_done = sem("proj_done")
        proj_out = sem("proj_out")
        proj_high = sem("proj_high")
        proj_low = sem("proj_low")
        rows_stacked = sem("rows_stacked")
        v_out = sem("v_out")
        v_high = sem("v_high")
        v_low = sem("v_low")
        scored = sem("scored")
        maxed = sem("maxed")
        rows_maxed = sem("rows_maxed")
        max_turned = sem("max_turned")
        max_out = sem("max_out")
        max_stacked = sem("max_stacked")
        t_scored = sem("t_scored")
        t_exp = sem("t_exp")
        p_high = sem("p_high")
        p_low = sem("p_low")
        o_done = sem("o_done")
        o_recip = sem("o_recip")
        o_read = sem("o_read")
        o_added = sem("o_added")
        x_scored = sem("x_scored")
        x_step = sem("x_step")
        x_exp = sem("x_exp")
        x_turned = sem("x_turned")
        x_high = sem("x_high")
        x_low = sem("x_low")
        x_done = sem("x_done")
        x_recip = sem("x_recip")
        x_read = sem("x_read")
        x_added = sem("x_added")
        stored = sem("stored")
        dve_tick = sem("dve_tick")
        sp_tick = sem("sp_tick")
        pool_tick = sem("pool_tick")
        block = ctx.enter_context(nc.Block())

        STACKS = 3 * 3 * 4
        NP = UNITS * PAIRS
        NCH = NP * CHUNKS
        NX = QT * 4

        def score_parts(k):
            if k < 2:
                return [(0, k, 3, 512)]
            if k < 4:
                return [(0, k - 2, 0, 128), (128, k - 2, 2, 384)]
            return [(0, 0, 1, 256), (256, 1, 1, 256)]

        def t_parts(k):
            if k < 2:
                return [(0, k, 0)]
            if k < 4:
                return [(0, k - 2, 3), (128, k - 2, 1)]
            return [(0, 0, 2), (256, 1, 2)]

        def t_place(hh, kt, qt):
            if kt == 0:
                return hh, P * qt
            if kt == 1:
                return 2 + hh, P + P * (qt - 1)
            if kt == 2:
                return 4, 256 * hh + P * (qt - 2)
            return 2 + hh, 0

        @block.sync
        def _(sp):
            def held(ge_sem, value):
                sp.wait_ge(ge_sem, value)
                sp.sem_inc(sp_tick, 1)

            def load_x(b):
                sp.dma_start(x_in[:, :, :], dram["x"][bass.ds(b, 1), :, :].rearrange("b (r p) c -> p (b r) c", p=P))\
                    .then_inc(x_loaded, 16)

            def batch(b, last):
                kT = dram["ctx_kT"][bass.ds(b, 1), :, :].rearrange("b d n -> d (b n)")
                v = dram["ctx_v"][bass.ds(b, 1), :, :].rearrange("b t n -> t (b n)")
                for r in range(4):
                    sp.dma_start(k_raw[D * r:D * r + D, :, :].rearrange("p g t -> p (g t)"), kT)\
                        .then_inc(ctx_loaded, 16)
                for j in range(2):
                    sp.dma_start(v_raw[TC * j:TC * j + TC, :, :].rearrange("p g d -> p (g d)"), v)\
                        .then_inc(ctx_loaded, 16)
                for g in range(UNITS):
                    for kind in range(3):
                        held(proj_low, 3 * UNITS * b + 3 * g + kind + 1)
                        for j in range(4):
                            for r in range(3):
                                if kind == 0:
                                    src = (nat_h, nat_h, nat_l)[r]
                                    dst = t.k_rows[D * r:D * r + D, g % 2, j, :]
                                else:
                                    src = (nat_h, nat_l, nat_h)[r]
                                    dst = t.q_rows[D * r:D * r + D, g % 2, 2 * j + kind - 1, :]
                                sp.dma_start(dst, src[D * j:D * j + D, kind, :]).then_inc(rows_stacked, 16)
                    held(max_out, UNITS * b + g + 1)
                    sp.dma_start(t.q_rows[96:97, g % 2, :, :].rearrange("o s (q n) -> o (s q) n", n=P),
                                 neg_max[:, :]).then_inc(max_stacked, 16)
                if not last:
                    held(o_added, NP * (b + 1))
                    load_x(b + 1)
                held(x_added, NX * (b + 1))
                sp.dma_start(dram["x2"][bass.ds(b, 1), :, :].rearrange("b (r p) c -> p (b r) c", p=P), x_mid[:, :, :])\
                    .then_inc(stored, 16)
                held(stored, 16 * (b + 1))

            load_x(0)
            with sp.Fori(0, B - 1) as b:
                batch(b, False)
            batch(B - 1, True)

        @block.gpsimd
        def _(pool):
            def held(ge_sem, value):
                pool.wait_ge(ge_sem, value)
                pool.sem_inc(pool_tick, 1)

            def ln_root(b, i):
                held(ln_stat, 4 * (8 * b + i) + 4)
                nc.gpsimd.tensor_tensor(rstd[:, i % 2:i % 2 + 1], var_eps[:, i % 2:i % 2 + 1], t.minus_half[:, :],
                                        ALU.pow).then_inc(ln_rstd, 1)

            def low_parts(b, n):
                held(p_high, NCH * b + n + 1)
                dst = (n // CHUNKS % 2, n % CHUNKS)
                nc.gpsimd.tensor_tensor(p_l[:, dst[0], dst[1], :], p32[:, n % 4, :], p_h[:, dst[0], dst[1], :],
                                        ALU.subtract).then_inc(p_low, 1)

            def add_pair(b, n):
                g, j = n // PAIRS, n % PAIRS
                held(o_read, NP * b + n + 1)
                cols = slice(D * (4 * g + j), D * (4 * g + j) + D)
                view = "p q (two r) -> p q two r"
                nc.gpsimd.tensor_tensor(x_mid[:, :, :].rearrange(view, two=2)[:, :, :, cols], o32[:, n % 2, :, :, :],
                                        x_in[:, :, :].rearrange(view, two=2)[:, :, :, cols], ALU.add)\
                    .then_inc(o_added, 1)

            def add_cross(b, n):
                held(x_read, NX * b + n + 1)
                cols = x_mid[:, n // 4, 8 * D * (n % 4):8 * D * (n % 4 + 1)]
                nc.gpsimd.tensor_tensor(cols, o32[:, n % 2, :, :, :].rearrange("p q a d -> p (q a d)"), cols, ALU.add)\
                    .then_inc(x_added, 1)

            with pool.Fori(0, B) as b:
                for i in range(4):
                    ln_root(b, i)
                for n in range(NP):
                    for k in range(CHUNKS):
                        low_parts(b, CHUNKS * n + k)
                    if n >= 1:
                        add_pair(b, n - 1)
                add_pair(b, NP - 1)
                for i in range(4, 8):
                    ln_root(b, i)
                for n in range(NX):
                    add_cross(b, n)

        @block.tensor
        def _(pe):
            def ln_turn(b, i):
                pe.wait_ge(ln_xn, 8 * b + i + 1)
                for half in range(2):
                    if i % 4:
                        pe.wait_ge(ln_low, 2 * (8 * b + i) + half - 1)
                    for c in range(4):
                        mm = nc.tensor.transpose(bank[LN_BANK + half][:, P * c:P * c + P],
                                                 xn[:, i % 2, P * (4 * half + c):P * (4 * half + c + 1)],
                                                 t.ident[:, :])
                    mm.then_inc(ln_turned, 1)

            def project(b, g):
                for kind in range(4):
                    dst = bank[PROJ_BANK + (5 * g + kind) % 2]
                    cols = slice(HALF * g + P * kind, HALF * g + P * kind + P)
                    if kind == 0 and g == 0:
                        pe.wait_ge(ln_low, 16 * b + 8)
                    if kind == 1 and g:
                        pe.wait_ge(max_out, UNITS * b + g)
                    if kind == 0 and g:
                        pe.wait_ge(v_out, UNITS * b + g)
                    if kind >= 2:
                        pe.wait_ge(proj_out, 3 * (UNITS * b + g) + kind - 1)
                    terms = [(w, x) for c in range(CT) for w, x in
                             ((t.w_h[:, c, cols], xT_h[:, c, :]), (t.w_h[:, c, cols], xT_l[:, c, :]),
                              (t.w_l[:, c, cols], xT_h[:, c, :]))]
                    if kind < 3:
                        for n, (w, x) in enumerate(terms):
                            mm = nc.tensor.matmul(dst[:, :], w, x, start=(n == 0), stop=(n == len(terms) - 1))
                    else:
                        for q in range(QT):
                            for n, (w, x) in enumerate(terms):
                                mm = nc.tensor.matmul(dst[:, P * q:P * q + P], x[:, P * q:P * q + P], w,
                                                      start=(n == 0), stop=(n == len(terms) - 1))
                    mm.then_inc(proj_done, 1)

            def score(b, n):
                g, j = n // PAIRS, n % PAIRS
                if j == 0:
                    pe.wait_ge(rows_stacked, 16 * STACKS * (UNITS * b + g + 1))
                for k in range(CHUNKS):
                    m = CHUNKS * n + k
                    if m >= 2:
                        pe.wait_ge(maxed, NCH * b + m - 1)
                    for col, hh, qt, keys in score_parts(k):
                        nc.tensor.matmul(bank[LN_BANK + m % 2][:, col:col + keys],
                                         t.q_rows[0:96, g % 2, 2 * j + hh, P * qt:P * qt + P],
                                         t.k_rows[0:96, g % 2, j, 0:keys], start=True, stop=False)
                        mm = nc.tensor.matmul(bank[LN_BANK + m % 2][:, col + P * qt:col + P * qt + P],
                                              t.ident_b[:, :], t.mask_qk[:, :], start=False, stop=True)
                    mm.then_inc(scored, 1)

            def turn_max(b, g):
                pe.wait_ge(rows_maxed, 4 * (UNITS * b + g + 1))
                pe.wait_ge(proj_out, 3 * (UNITS * b + g + 1))
                nc.tensor.transpose(bank[PROJ_BANK + (5 * g + 4) % 2][0:2 * PAIRS * QT, 0:P],
                                    row_max[:, :, :, :].rearrange("p j a q -> p (j a q)"), t.ident[:, :])\
                    .then_inc(max_turned, 1)

            def t_score(b, n):
                g, j = n // PAIRS, n % PAIRS
                if j == 0:
                    pe.wait_ge(max_stacked, 16 * (UNITS * b + g + 1))
                for k in range(CHUNKS):
                    m = CHUNKS * n + k
                    if m >= 3:
                        pe.wait_ge(t_exp, NCH * b + m - 2)
                    for col, hh, kt in t_parts(k):
                        nc.tensor.matmul(bank[T_BANK + m % 3][:, col:col + T - P * kt],
                                         t.k_rows[0:97, g % 2, j, P * kt:P * kt + P],
                                         t.q_rows[0:97, g % 2, 2 * j + hh, P * kt:T], start=True, stop=False)
                        mm = nc.tensor.matmul(bank[T_BANK + m % 3][:, col:col + P],
                                              t.ident_b[:, :], t.mask_kq[:, :], start=False, stop=True)
                    mm.then_inc(t_scored, 1)

            def weigh(b, n):
                g, j = n // PAIRS, n % PAIRS
                if j == 0:
                    pe.wait_ge(v_low, UNITS * b + g + 1)
                pe.wait_ge(p_low, CHUNKS * (NP * b + n + 1))
                if n >= 1:
                    pe.wait_ge(o_read, NP * b + n)
                for qt in range(QT):
                    for hh in range(2):
                        col = (D + 1) * (2 * qt + hh)
                        for kt in range(qt + 1):
                            k, at = t_place(hh, kt, qt)
                            high = p_h[:, n % 2, k, at:at + P]
                            low = p_l[:, n % 2, k, at:at + P]
                            v = t.v_parts[:, g % 2, kt, j, :]
                            out = bank[O_BANK]
                            nc.tensor.matmul(out[:, col:col + D + 1], high, v[:, 0:D + 1],
                                             start=(kt == 0), stop=False)
                            nc.tensor.matmul(out[:, col:col + D], high, v[:, D + 1:2 * D + 1],
                                             start=False, stop=False)
                            mm = nc.tensor.matmul(out[:, col:col + D + 1], low, v[:, 0:D + 1],
                                                  start=False, stop=(kt == qt))
                mm.then_inc(o_done, 1)

            def x_score(b, n):
                rt = n // 4
                if n % 4 == 0:
                    pe.wait_ge(ln_low, 16 * b + 8 + 2 * (rt + 1))
                if n == 0:
                    pe.wait_ge(ctx_step, 13 * (b + 1))
                if n >= 2:
                    pe.wait_ge(x_step, 3 * (NX * b + n - 2) + 1)
                for part in range(2):
                    g = 2 * (n % 4) + part
                    rows = slice(P * rt, P * rt + P)
                    for i, (x, k) in enumerate(((xT_h, t.kx_h), (xT_l, t.kx_h), (xT_h, t.kx_l))):
                        mm = nc.tensor.matmul(bank[PROJ_BANK + n % 2][:, 256 * part:256 * part + 256],
                                              x[:, g, rows], k[:, g, :], start=(i == 0), stop=(i == 2))
                mm.then_inc(x_scored, 1)

            def x_turn(b, n):
                pe.wait_ge(x_exp, NX * b + n + 1)
                if n >= 2:
                    pe.wait_ge(x_low, NX * b + n - 1)
                for i in range(4):
                    mm = nc.tensor.transpose(bank[T_BANK + n % 2][:, P * i:P * i + P], e32[:, n % 2, P * i:P * i + P],
                                             t.ident[:, :])
                mm.then_inc(x_turned, 1)

            def x_weigh(b, n):
                pe.wait_ge(x_low, NX * b + n + 1)
                if n >= 1:
                    pe.wait_ge(x_read, NX * b + n)
                W = 2 * (D + 1)
                for i in range(4):
                    g = 2 * (n % 4) + i // 2
                    for m, (p, v) in enumerate(((px_h, t.vx_h), (px_h, t.vx_l), (px_l, t.vx_h))):
                        mm = nc.tensor.matmul(bank[O_BANK][:, W * i:W * i + W], p[:, n % 2, P * i:P * i + P],
                                              v[:, g, :], start=(m == 0), stop=(m == 2))
                mm.then_inc(x_done, 1)

            with pe.Fori(0, B) as b:
                for i in range(4):
                    ln_turn(b, i)
                project(b, 0)
                for j in range(PAIRS):
                    score(b, j)
                turn_max(b, 0)
                for g in range(UNITS):
                    more = g + 1 < UNITS
                    n, nn = PAIRS * g, PAIRS * (g + 1)
                    if more:
                        project(b, g + 1)
                    t_score(b, n)
                    t_score(b, n + 1)
                    weigh(b, n)
                    if more:
                        score(b, nn)
                    t_score(b, n + 2)
                    weigh(b, n + 1)
                    if more:
                        score(b, nn + 1)
                    t_score(b, n + 3)
                    weigh(b, n + 2)
                    if more:
                        score(b, nn + 2)
                        score(b, nn + 3)
                    weigh(b, n + 3)
                    if more:
                        turn_max(b, g + 1)
                for i in range(4, 8):
                    ln_turn(b, i)
                for n in range(NX + 2):
                    if n < NX:
                        x_score(b, n)
                    if 1 <= n <= NX:
                        x_turn(b, n - 1)
                    if n >= 2:
                        x_weigh(b, n - 2)

        @block.scalar
        def _(act):
            def ln_high_parts(b, i):
                for half in range(2):
                    act.wait_ge(ln_turned, 2 * (8 * b + i) + half + 1)
                    nc.scalar.activation(xT_h[:, 4 * half:4 * half + 4, P * (i % 4):P * (i % 4) + P],
                                         bank[LN_BANK + half][:, :].rearrange("p (c n) -> p c n", n=P), ACT.Copy)\
                        .then_inc(ln_high, 1)

            def proj_parts(b, g):
                for kind in range(3):
                    n = 3 * (UNITS * b + g) + kind
                    slot = (3 * g + kind) % 2
                    act.wait_ge(proj_done, 4 * (UNITS * b + g) + kind + 1)
                    if 3 * g + kind >= 2:
                        act.wait_ge(proj_low, n - 1)
                    nc.scalar.activation(proj32[:, slot, :], bank[PROJ_BANK + (5 * g + kind) % 2][:, :], ACT.Identity,
                                         bias=t.bias_qk[:, g, kind:kind + 1], scale=1.0 / W_SCALE)\
                        .then_inc(proj_out, 1)
                    act.wait_ge(proj_out, n + 1)
                    if kind == 0 and g:
                        act.wait_ge(rows_stacked, 16 * STACKS * (UNITS * b + g))
                    nc.scalar.activation(nat_h[:, kind, :], proj32[:, slot, :], ACT.Copy).then_inc(proj_high, 1)
                act.wait_ge(v_out, UNITS * b + g + 1)
                nc.scalar.activation(t.v_parts[:, g % 2, :, :, 0:D], v32[:, :, :, :], ACT.Copy).then_inc(v_high, 1)

            def exps(b, n):
                act.wait_ge(t_scored, NCH * b + n + 1)
                if n >= 4:
                    act.wait_ge(p_low, NCH * b + n - 3)
                nc.scalar.activation(p32[:, n % 4, :], bank[T_BANK + n % 3][:, :], ACT.Exp, scale=SELF_SCALE)\
                    .then_inc(t_exp, 1)

            def high_parts(b, n):
                act.wait_ge(t_exp, NCH * b + n + 1)
                if n % CHUNKS == 0 and n >= 2 * CHUNKS:
                    act.wait_ge(o_done, NP * b + n // CHUNKS - 1)
                nc.scalar.activation(p_h[:, n // CHUNKS % 2, n % CHUNKS, :], p32[:, n % 4, :], ACT.Copy)\
                    .then_inc(p_high, 1)

            def x_exps(b, n):
                act.wait_ge(x_step, 3 * (NX * b + n + 1))
                if n >= 2:
                    act.wait_ge(x_turned, NX * b + n - 1)
                nc.scalar.activation(e32[:, n % 2, :], s32[:, n % 2, :, :].rearrange("p a t -> p (a t)"), ACT.Exp)\
                    .then_inc(x_exp, 1)

            def x_high_parts(b, n):
                act.wait_ge(x_turned, NX * b + n + 1)
                if n >= 2:
                    act.wait_ge(x_done, NX * b + n - 1)
                nc.scalar.activation(px_h[:, n % 2, :], bank[T_BANK + n % 2][:, :], ACT.Copy).then_inc(x_high, 1)

            with act.Fori(0, B) as b:
                for i in range(4):
                    ln_high_parts(b, i)
                proj_parts(b, 0)
                act.wait_ge(max_turned, UNITS * b + 1)
                nc.scalar.activation(neg_max[:, :], bank[PROJ_BANK][0:2 * PAIRS * QT, 0:P], ACT.Copy, scale=-1.0)\
                    .then_inc(max_out, 1)
                for g in range(UNITS):
                    if g + 1 < UNITS:
                        proj_parts(b, g + 1)
                    first = CHUNKS * PAIRS * g
                    for n in range(first, first + CHUNKS * PAIRS):
                        exps(b, n)
                        if n > first:
                            high_parts(b, n - 1)
                    high_parts(b, first + CHUNKS * PAIRS - 1)
                    if g + 1 < UNITS:
                        act.wait_ge(max_turned, UNITS * b + g + 2)
                        act.wait_ge(max_stacked, 16 * (UNITS * b + g + 1))
                        nc.scalar.activation(neg_max[:, :], bank[PROJ_BANK + (5 * g + 9) % 2][0:2 * PAIRS * QT, 0:P],
                                             ACT.Copy, scale=-1.0).then_inc(max_out, 1)
                for i in range(4, 8):
                    ln_high_parts(b, i)
                for n in range(NX + 1):
                    if n < NX:
                        x_exps(b, n)
                    if n >= 1:
                        x_high_parts(b, n - 1)

        @block.vector
        def _(dve):
            def lay_context(b):
                dve.wait_ge(ctx_loaded, 16 * 6 * (b + 1))
                base = 13 * b
                nc.vector.tensor_scalar(k_raw[:, :, :], k_raw[:, :, :], CROSS_SCALE, None, ALU.mult)\
                    .then_inc(ctx_step, 1)
                dve.wait_ge(ctx_step, base + 1)
                for r in range(4):
                    rows, cols = slice(D * r, D * r + D), slice(TC * r, TC * r + TC)
                    nc.vector.tensor_copy(t.kx_h[rows, :, cols], k_raw[rows, :, :]).then_inc(ctx_step, 1)
                for j in range(2):
                    rows, cols = slice(TC * j, TC * j + TC), slice((D + 1) * j, (D + 1) * j + D)
                    nc.vector.tensor_copy(t.vx_h[rows, :, cols], v_raw[rows, :, :]).then_inc(ctx_step, 1)
                dve.wait_ge(ctx_step, base + 7)
                for r in range(4):
                    rows, cols = slice(D * r, D * r + D), slice(TC * r, TC * r + TC)
                    nc.vector.tensor_tensor(t.kx_l[rows, :, cols], k_raw[rows, :, :], t.kx_h[rows, :, cols],
                                            ALU.subtract).then_inc(ctx_step, 1)
                for j in range(2):
                    rows, cols = slice(TC * j, TC * j + TC), slice((D + 1) * j, (D + 1) * j + D)
                    nc.vector.tensor_tensor(t.vx_l[rows, :, cols], v_raw[rows, :, :], t.vx_h[rows, :, cols],
                                            ALU.subtract).then_inc(ctx_step, 1)

            def ln_normal(b, i, src):
                n, s = 8 * b + i, i % 2
                row = src[:, i % 4, :]
                for half in range(2):
                    nc.vector.bn_stats(stats[:, s, half, :], row[:, HALF * half:HALF * half + HALF])\
                        .then_inc(ln_stat, 1)
                dve.wait_ge(ln_stat, 4 * n + 2)
                dve.sem_inc(dve_tick, 1)
                nc.vector.bn_aggr(mean_var[:, s, :], stats[:, s, :, :]).then_inc(ln_stat, 1)
                dve.wait_ge(ln_stat, 4 * n + 3)
                nc.vector.tensor_scalar(var_eps[:, s:s + 1], mean_var[:, s, 1:2], EPS, None, ALU.add)\
                    .then_inc(ln_stat, 1)
                dve.wait_ge(ln_rstd, n + 1)
                if i % 4 >= 2:
                    dve.wait_ge(ln_turned, 2 * n - 2)
                nc.vector.tensor_scalar(xn[:, s, :], row, mean_var[:, s, 0:1], rstd[:, s:s + 1],
                                        ALU.subtract, ALU.mult).then_inc(ln_xn, 1)

            def ln_low_parts(b, i):
                for half in range(2):
                    dve.wait_ge(ln_high, 2 * (8 * b + i) + half + 1)
                    cols = (slice(None), slice(4 * half, 4 * half + 4), slice(P * (i % 4), P * (i % 4) + P))
                    nc.vector.tensor_tensor(xT_l[cols], bank[LN_BANK + half][:, :].rearrange("p (c n) -> p c n", n=P),
                                            xT_h[cols], ALU.subtract).then_inc(ln_low, 1)

            def proj_parts(b, g):
                for kind in range(3):
                    dve.wait_ge(proj_high, 3 * (UNITS * b + g) + kind + 1)
                    nc.vector.tensor_tensor(nat_l[:, kind, :], proj32[:, (3 * g + kind) % 2, :], nat_h[:, kind, :],
                                            ALU.subtract).then_inc(proj_low, 1)
                dve.wait_ge(proj_done, 4 * (UNITS * b + g + 1))
                bias = t.bias_v[:, P * g:P * g + P].unsqueeze(1).broadcast_to([P, QT, P])
                nc.vector.scalar_tensor_tensor(v32[:, :, :, :].rearrange("p q j d -> p q (j d)"),
                                               bank[PROJ_BANK + (5 * g + 3) % 2][:, :]
                                               .rearrange("p (q n) -> p q n", n=P),
                                               1.0 / W_SCALE, bias, ALU.mult, ALU.add).then_inc(v_out, 1)
                dve.wait_ge(v_high, UNITS * b + g + 1)
                nc.vector.tensor_tensor(t.v_parts[:, g % 2, :, :, D + 1:2 * D + 1], v32[:, :, :, :],
                                        t.v_parts[:, g % 2, :, :, 0:D], ALU.subtract).then_inc(v_low, 1)

            def maxima(b, n):
                for k in range(CHUNKS):
                    m = CHUNKS * n + k
                    dve.wait_ge(scored, NCH * b + m + 1)
                    nc.vector.reduce_max(block_max[:, n % PAIRS, k, :],
                                         bank[LN_BANK + m % 2][:, :].rearrange("p (a n) -> p a n", n=P), AX_X)\
                        .then_inc(maxed, 1)

            def row_maxima(b, g):
                dve.wait_ge(maxed, NCH * b + CHUNKS * PAIRS * (g + 1))
                nc.vector.reduce_max(row_max[:, :, :, 3], block_max[:, :, 0:2, :], AX_X).then_inc(rows_maxed, 1)
                nc.vector.reduce_max(row_max[:, :, :, 2], block_max[:, :, 2:4, 1:4], AX_X).then_inc(rows_maxed, 1)
                nc.vector.tensor_copy(row_max[:, :, :, 0], block_max[:, :, 2:4, 0]).then_inc(rows_maxed, 1)
                nc.vector.reduce_max(row_max[:, :, :, 1],
                                     block_max[:, :, 4, :].rearrange("p j (a n) -> p j a n", n=2), AX_X)\
                    .then_inc(rows_maxed, 1)

            def pair_out(b, n):
                dve.wait_ge(o_done, NP * b + n + 1)
                out = bank[O_BANK][:, 0:(D + 1) * 2 * QT].rearrange("p (s d) -> p s d", d=D + 1)
                nc.vector.reciprocal(r_sum[:, n % 2, :], out[:, :, D]).then_inc(o_recip, 1)
                dve.wait_ge(o_recip, NP * b + n + 1)
                if n >= 2:
                    dve.wait_ge(o_added, NP * b + n - 1)
                nc.vector.tensor_tensor(o32[:, n % 2, :, :, :].rearrange("p q a d -> p (q a) d"), out[:, :, 0:D],
                                        r_sum[:, n % 2, :].unsqueeze(2).broadcast_to([P, 2 * QT, D]), ALU.mult)\
                    .then_inc(o_read, 1)

            def x_soft(b, n):
                s = s32[:, n % 2, :, :]
                dve.wait_ge(x_scored, NX * b + n + 1)
                if n >= 2:
                    dve.wait_ge(x_exp, NX * b + n - 1)
                nc.vector.tensor_tensor(s, bank[PROJ_BANK + n % 2][:, :].rearrange("p (a t) -> p a t", t=TC),
                                        t.mask[:, n // 4, :].unsqueeze(1).broadcast_to([P, 8, TC]), ALU.add)\
                    .then_inc(x_step, 1)
                dve.wait_ge(x_step, 3 * (NX * b + n) + 1)
                nc.vector.reduce_max(s_top[:, n % 2, :], s, AX_X).then_inc(x_step, 1)
                dve.wait_ge(x_step, 3 * (NX * b + n) + 2)
                nc.vector.tensor_tensor(s, s, s_top[:, n % 2, :].unsqueeze(2).broadcast_to([P, 8, TC]), ALU.subtract)\
                    .then_inc(x_step, 1)

            def x_low_parts(b, n):
                dve.wait_ge(x_high, NX * b + n + 1)
                nc.vector.tensor_tensor(px_l[:, n % 2, :], bank[T_BANK + n % 2][:, :], px_h[:, n % 2, :],
                                        ALU.subtract).then_inc(x_low, 1)

            def x_out(b, n):
                dve.wait_ge(x_done, NX * b + n + 1)
                out = bank[O_BANK][:, 0:(D + 1) * 8].rearrange("p (s d) -> p s d", d=D + 1)
                nc.vector.reciprocal(r_sum[:, n % 2, :], out[:, :, D]).then_inc(x_recip, 1)
                dve.wait_ge(x_recip, NX * b + n + 1)
                if n >= 2:
                    dve.wait_ge(x_added, NX * b + n - 1)
                nc.vector.tensor_tensor(o32[:, n % 2, :, :, :].rearrange("p q a d -> p (q a) d"), out[:, :, 0:D],
                                        r_sum[:, n % 2, :].unsqueeze(2).broadcast_to([P, 8, D]), ALU.mult)\
                    .then_inc(x_read, 1)

            with dve.Fori(0, B) as b:
                dve.wait_ge(x_loaded, 16 * (b + 1))
                for i in range(5):
                    if i < 4:
                        ln_normal(b, i, x_in)
                    if i >= 1:
                        ln_low_parts(b, i - 1)
                lay_context(b)
                proj_parts(b, 0)
                for j in range(PAIRS):
                    maxima(b, j)
                row_maxima(b, 0)
                for g in range(UNITS):
                    more = g + 1 < UNITS
                    n, nn = PAIRS * g, PAIRS * (g + 1)
                    if more:
                        proj_parts(b, g + 1)
                    pair_out(b, n)
                    if more:
                        maxima(b, nn)
                    pair_out(b, n + 1)
                    if more:
                        maxima(b, nn + 1)
                    pair_out(b, n + 2)
                    if more:
                        maxima(b, nn + 2)
                        maxima(b, nn + 3)
                        row_maxima(b, g + 1)
                    pair_out(b, n + 3)
                dve.wait_ge(o_added, NP * (b + 1))
                for i in range(4, 9):
                    if i < 8:
                        ln_normal(b, i, x_mid)
                    if i >= 5:
                        ln_low_parts(b, i - 1)
                for n in range(NX + 2):
                    if n < NX:
                        x_soft(b, n)
                    if 1 <= n <= NX:
                        x_low_parts(b, n - 1)
                    if n >= 2:
                        x_out(b, n - 2)


def feed_forward(nc, dram):
    with ExitStack() as ctx:
        def sb(name, shape, dt):
            return ctx.enter_context(nc.sbuf_tensor(name, shape, dt))

        def sem(name):
            return ctx.enter_context(nc.semaphore(name))

        y = sb("y", [P, RT, C], FP32)
        xT_h = sb("fT_h", [P, CT, B * T], FP16)
        xT_l = sb("fT_l", [P, CT, B * T], FP16)
        hT_h = sb("hT_h", [P, 2, B * T], FP16)
        hT_l = sb("hT_l", [P, 2, B * T], FP16)
        up_h = sb("up_h", [P, 2, 2, C], FP16)
        up_l = sb("up_l", [P, 2, 2, C], FP16)
        dn_h = sb("dn_h", [P, 2, C], FP16)
        dn_l = sb("dn_l", [P, 2, C], FP16)
        codes = sb("codes", [P, 2, HALF], INT32)
        scales = sb("scales", [P, 2, HALF], FP32)
        line = sb("line", [P, 4, HALF], FP32)
        lower = sb("lower", [P, HALF], FP32)
        upper = sb("upper", [P, HALF], FP32)
        w32 = sb("w32", [P, 2, HALF], FP32)
        silu = sb("silu", [P, 2, HALF], FP32)
        h32 = sb("h32", [P, 2, HALF], FP32)
        xn = sb("f_xn", [P, C], FP32)
        ident = sb("f_ident", [P, P], FP32)
        minus_half = sb("f_minus_half", [P, 1], FP32)
        stats = sb("f_stats", [P, 2, 2, 6], FP32)
        mean_var = sb("f_mean_var", [P, 2, 2], FP32)
        var_eps = sb("f_var_eps", [P, 2], FP32)
        rstd = sb("f_rstd", [P, 2], FP32)
        bank = [ctx.enter_context(nc.psum_tensor(f"f_bank{i}", [P, HALF], FP32)) for i in range(8)]
        GATE, UP, DOWN = 0, 2, 4

        y_loaded = [sem(f"y_loaded{i}") for i in range(4)]
        consts = sem("consts")
        ln_stat = sem("f_ln_stat")
        ln_rstd = sem("f_ln_rstd")
        ln_xn = sem("f_ln_xn")
        ln_turned = sem("f_ln_turned")
        ln_high = sem("f_ln_high")
        ln_low = sem("f_ln_low")
        codes_loaded = [sem(f"codes_loaded{i}") for i in range(2)]
        lined = sem("lined")
        lut = sem("lut")
        w_high = sem("fw_high")
        w_low = sem("fw_low")
        gate_done = sem("gate_done")
        up_done = sem("up_done")
        silu_done = sem("silu_done")
        h_done = sem("h_done")
        h_high = sem("h_high")
        h_low = sem("h_low")
        down_done = sem("down_done")
        y_added = sem("y_added")
        stored = sem("y_stored")
        sp_tick = sem("f_sp_tick")
        pool_tick = sem("f_pool_tick")
        block = ctx.enter_context(nc.Block())

        NB = B
        NQ = 2 * NB
        ND = 2 * RT
        AHEAD = 4
        PER = 12

        def tile_of(k):
            if k < 4:
                return 1, k // 2, k % 2
            if k < 8:
                return (k - 4) // 2, 2, k % 2
            return 2, (k - 8) // 2, k % 2

        STEPS = [[0, 1], [2], [3, 4], [5], [6], [7, 8], [9], [10], [], [11], [], []]

        def last_k(last):
            return 8 if last else PER

        USED_BY = [1, 1, 2, 3, 4, 4, 5, 6, 7]

        def weights(chunk, kind, half):
            cols = slice(HALF * half, HALF * half + HALF)
            if kind == 2:
                return dn_h[:, chunk % 2, cols], dn_l[:, chunk % 2, cols]
            return up_h[:, chunk % 2, kind, cols], up_l[:, chunk % 2, kind, cols]

        @block.sync
        def _(sp):
            def load(i, k, t):
                chunk, kind, half = tile_of(k) if k >= 0 else (0, (k + 4) // 2, k % 2)
                cols = slice(HALF * half, HALF * half + HALF)
                code = dram["codes"][bass.ds(2 * i + chunk, 1), kind, :, cols].rearrange("a p n -> p (a n)")
                scale = [dram["scales"][bass.ds(2 * i + chunk, 1), kind, s, cols].broadcast_to([P // 2, HALF])
                         for s in range(2)]
                if k > -3:
                    sp.wait_ge(lut, NL * (t - 1))
                    sp.sem_inc(sp_tick, 1)
                slot = k % 2
                sp.dma_start(codes[:, slot, :], code).then_inc(codes_loaded[slot], 16)
                for s in range(2):
                    sp.dma_start(scales[P // 2 * s:P // 2 * (s + 1), slot, :], scale[s])\
                        .then_inc(codes_loaded[slot], 16)

            def group(i, last):
                for k in range(last_k(last)):
                    load(i, k, AHEAD + PER * i + k)

            for q in range(4):
                sp.dma_start(y[:, 4 * q:4 * q + 4, :], dram["x2"][q, :, :].rearrange("(r p) c -> p r c", p=P))\
                    .then_inc(y_loaded[q], 16)
            for k in range(-4, 0):
                load(0, k, AHEAD + k)
            with sp.Fori(0, GROUPS - 1) as i:
                group(i, False)
            group(GROUPS - 1, True)
            for r in range(RT):
                sp.wait_ge(y_added, ND * (GROUPS - 1) + 2 * (r + 1))
                sp.dma_start(dram["out"][P * r:P * r + P, :], y[:, r, :]).then_inc(stored, 16)
            sp.wait_ge(stored, 16 * RT)

        @block.gpsimd
        def _(pool):
            nc.gpsimd.memset(ident[:, :], 0.0).then_inc(consts, 1)
            nc.gpsimd.memset(minus_half[:, :], -0.5).then_inc(consts, 1)
            pool.wait_ge(consts, 2)
            nc.gpsimd.affine_select(out=ident[:, :], in_=ident[:, :], compare_op=ALU.not_equal, fill=1.0, base=0,
                                    pattern=[[-1, P]], channel_multiplier=1).then_inc(consts, 1)

            def low_parts(w_h, w_l, t, slot):
                pool.wait_ge(w_high, t + 1)
                pool.sem_inc(pool_tick, 1)
                nc.gpsimd.tensor_tensor(w_l, w32[:, slot, :], w_h, ALU.subtract).then_inc(w_low, 1)

            def group(i, last):
                for k in range(last_k(last)):
                    low_parts(*weights(*tile_of(k)), AHEAD + PER * i + k, k % 2)

            for r in range(RT):
                pool.wait_ge(ln_stat, 4 * r + 4)
                nc.gpsimd.tensor_tensor(rstd[:, r % 2:r % 2 + 1], var_eps[:, r % 2:r % 2 + 1], minus_half[:, :],
                                        ALU.pow).then_inc(ln_rstd, 1)
            for k in range(AHEAD):
                low_parts(*weights(0, k // 2, k % 2), k, k % 2)
            with pool.Fori(0, GROUPS - 1) as i:
                group(i, False)
            group(GROUPS - 1, True)

        @block.tensor
        def _(pe):
            def gate_up(i, chunk):
                pe.wait_ge(w_low, AHEAD + PER * i + 4 * chunk)
                for nb in range(NB):
                    n = NB * chunk + nb
                    cols = slice(T * nb, T * nb + T)
                    for kind in range(2):
                        if n >= 2:
                            pe.wait_ge((silu_done, h_done)[kind], NQ * i + n - 1)
                        for m in range(3 * CT):
                            c = m // 3
                            w, x = ((up_h, xT_h), (up_h, xT_l), (up_l, xT_h))[m % 3]
                            mm = nc.tensor.matmul(bank[(GATE, UP)[kind] + n % 2][:, :],
                                                  w[:, chunk, kind, P * c:P * c + P], x[:, c, cols],
                                                  start=(m == 0), stop=(m == 3 * CT - 1))
                        mm.then_inc((gate_done, up_done)[kind], 1)

            def down(i):
                pe.wait_ge(w_low, AHEAD + PER * i + 8)
                for d in range(ND):
                    r, half = d // 2, d % 2
                    if d % 8 == 0:
                        pe.wait_ge(h_low, NQ * i + NB + d // 8 + 1)
                    if d >= 4:
                        pe.wait_ge(y_added, ND * i + d - 3)
                    rows, cols = slice(P * r, P * r + P), slice(HALF * half, HALF * half + HALF)
                    for m in range(6):
                        h, w = ((hT_h, dn_h), (hT_h, dn_l), (hT_l, dn_h))[m % 3]
                        mm = nc.tensor.matmul(bank[DOWN + d % 4][:, :], h[:, m // 3, rows], w[:, m // 3, cols],
                                              start=(m == 0), stop=(m == 5))
                    mm.then_inc(down_done, 1)

            pe.wait_ge(consts, 3)
            for r in range(RT):
                pe.wait_ge(ln_xn, r + 1)
                for half in range(2):
                    if r:
                        pe.wait_ge(ln_low, 2 * r + half - 1)
                    for c in range(4):
                        mm = nc.tensor.transpose(bank[GATE + half][:, P * c:P * c + P],
                                                 xn[:, P * (4 * half + c):P * (4 * half + c + 1)], ident[:, :])
                    mm.then_inc(ln_turned, 1)
            pe.wait_ge(ln_low, 2 * RT)
            with pe.Fori(0, GROUPS) as i:
                gate_up(i, 0)
                gate_up(i, 1)
                down(i)

        @block.scalar
        def _(act):
            def draw_lines(i, k):
                t, slot = AHEAD + PER * i + k, k % 2
                act.wait_ge(codes_loaded[slot], 48 * (PER // 2 * i + (AHEAD + k) // 2 + 1))
                for m, (slope, intercept) in enumerate(LINES):
                    at = (NL * (k % 4) + m) % 4
                    if k != -4 or m >= 4:
                        back = NL * (t - 1) + USED_BY[m + NL - 4] if m < 4 else NL * t + USED_BY[m - 4]
                        act.wait_ge(lut, back)
                    nc.scalar.activation(line[:, at, :], codes[:, slot, :], ACT.Copy, scale=slope, bias=intercept)\
                        .then_inc(lined, 1)

            def cut_high(t, k, dst):
                act.wait_ge(lut, NL * (t + 1))
                nc.scalar.activation(dst, w32[:, k % 2, :], ACT.Copy).then_inc(w_high, 1)

            def group(i, last):
                for q, ks in enumerate(STEPS):
                    if q < NQ:
                        act.wait_ge(gate_done, NQ * i + q + 1)
                        nc.scalar.activation(silu[:, q % 2, :], bank[GATE + q % 2][:, :], ACT.Silu,
                                             scale=1.0 / F_SCALE).then_inc(silu_done, 1)
                    for k in ks:
                        if k < last_k(last):
                            draw_lines(i, k)
                    if q < NQ:
                        act.wait_ge(h_done, NQ * i + q + 1)
                        nc.scalar.activation(hT_h[:, q // NB, T * (q % NB):T * (q % NB) + T], h32[:, q % 2, :],
                                             ACT.Copy).then_inc(h_high, 1)
                    for k in ks:
                        if k < last_k(last):
                            cut_high(AHEAD + PER * i + k, k, weights(*tile_of(k))[0])

            for r in range(RT):
                for half in range(2):
                    act.wait_ge(ln_turned, 2 * r + half + 1)
                    nc.scalar.activation(xT_h[:, 4 * half:4 * half + 4, P * r:P * r + P],
                                         bank[GATE + half][:, :].rearrange("p (c n) -> p c n", n=P), ACT.Copy)\
                        .then_inc(ln_high, 1)
            for k in range(-4, 0):
                draw_lines(0, k)
                cut_high(AHEAD + k, k, weights(0, (k + 4) // 2, k % 2)[0])
            with act.Fori(0, GROUPS - 1) as i:
                group(i, False)
            group(GROUPS - 1, True)

        @block.vector
        def _(dve):
            def look_up(t, k):
                def at(m):
                    return line[:, (NL * (k % 4) + m) % 4, :]

                def step(m, done):
                    dve.wait_ge(lined, NL * t + m)
                    if done:
                        dve.wait_ge(lut, NL * t + done)

                step(2, 0)
                nc.vector.scalar_tensor_tensor(lower[:, :], at(0), 0.0, at(1), ALU.min, ALU.min).then_inc(lut, 1)
                step(3, 1)
                nc.vector.tensor_tensor(lower[:, :], lower[:, :], at(2), ALU.min).then_inc(lut, 1)
                step(4, 2)
                nc.vector.tensor_tensor(lower[:, :], lower[:, :], at(3), ALU.min).then_inc(lut, 1)
                step(6, 3)
                nc.vector.scalar_tensor_tensor(upper[:, :], at(4), 0.0, at(5), ALU.max, ALU.max).then_inc(lut, 1)
                for m in range(6, 9):
                    step(m + 1, m - 2)
                    nc.vector.tensor_tensor(upper[:, :], upper[:, :], at(m), ALU.max).then_inc(lut, 1)
                dve.wait_ge(lut, NL * t + 7)
                nc.vector.tensor_tensor(upper[:, :], upper[:, :], lower[:, :], ALU.add).then_inc(lut, 1)
                dve.wait_ge(lut, NL * t + 8)
                if k >= -2:
                    dve.wait_ge(w_low, t - 1)
                nc.vector.tensor_tensor(w32[:, k % 2, :], upper[:, :], scales[:, k % 2, :], ALU.mult)\
                    .then_inc(lut, 1)

            def group(i, last):
                for q, ks in enumerate(STEPS):
                    if q < NQ:
                        dve.wait_ge(silu_done, NQ * i + q + 1)
                        dve.wait_ge(up_done, NQ * i + q + 1)
                        nc.vector.scalar_tensor_tensor(h32[:, q % 2, :], bank[UP + q % 2][:, :], H_SCALE / F_SCALE,
                                                       silu[:, q % 2, :], ALU.mult, ALU.mult).then_inc(h_done, 1)
                    for k in ks:
                        if k < last_k(last):
                            look_up(AHEAD + PER * i + k, k)
                    if q < NQ:
                        dve.wait_ge(h_high, NQ * i + q + 1)
                        cols = slice(T * (q % NB), T * (q % NB) + T)
                        nc.vector.tensor_tensor(hT_l[:, q // NB, cols], h32[:, q % 2, :], hT_h[:, q // NB, cols],
                                                ALU.subtract).then_inc(h_low, 1)
                    else:
                        for d in range(8 * (q - NQ), 8 * (q - NQ) + 8):
                            cols = y[:, d // 2, HALF * (d % 2):HALF * (d % 2) + HALF]
                            dve.wait_ge(down_done, ND * i + d + 1)
                            nc.vector.scalar_tensor_tensor(cols, bank[DOWN + d % 4][:, :], 1.0 / (H_SCALE * F_SCALE),
                                                           cols, ALU.mult, ALU.add).then_inc(y_added, 1)

            def ln_low_parts(r):
                for half in range(2):
                    dve.wait_ge(ln_high, 2 * r + half + 1)
                    cols = (slice(None), slice(4 * half, 4 * half + 4), slice(P * r, P * r + P))
                    nc.vector.tensor_tensor(xT_l[cols], bank[GATE + half][:, :].rearrange("p (c n) -> p c n", n=P),
                                            xT_h[cols], ALU.subtract).then_inc(ln_low, 1)

            for r in range(RT + 1):
                if r < RT:
                    s = r % 2
                    if r % 4 == 0:
                        dve.wait_ge(y_loaded[r // 4], 16)
                    for half in range(2):
                        nc.vector.bn_stats(stats[:, s, half, :], y[:, r, HALF * half:HALF * half + HALF])\
                            .then_inc(ln_stat, 1)
                    dve.wait_ge(ln_stat, 4 * r + 2)
                    nc.vector.bn_aggr(mean_var[:, s, :], stats[:, s, :, :]).then_inc(ln_stat, 1)
                    dve.wait_ge(ln_stat, 4 * r + 3)
                    nc.vector.tensor_scalar(var_eps[:, s:s + 1], mean_var[:, s, 1:2], EPS, None, ALU.add)\
                        .then_inc(ln_stat, 1)
                    dve.wait_ge(ln_rstd, r + 1)
                    if r >= 1:
                        dve.wait_ge(ln_turned, 2 * r)
                    nc.vector.tensor_scalar(xn[:, :], y[:, r, :], mean_var[:, s, 0:1], rstd[:, s:s + 1],
                                            ALU.subtract, ALU.mult).then_inc(ln_xn, 1)
                if r >= 1:
                    ln_low_parts(r - 1)
            for k in range(-4, 0):
                look_up(AHEAD + k, k)
            with dve.Fori(0, GROUPS - 1) as i:
                group(i, False)
            group(GROUPS - 1, True)


def decoder_layer(nc, dram):
    with ExitStack() as ctx:
        t = Attention(nc, ctx)
        prepare(nc, t, dram)
        attention(nc, t, dram)
    feed_forward(nc, dram)


def kernel(x, ctx_1024, mask_SxS2_ff0, L0_attn_Wq, L0_attn_bq, L0_attn_Wk, L0_attn_bk, L0_attn_Wv, L0_attn_bv,
           L0_ffn_gate_q, L0_ffn_gate_absmax, L0_ffn_up_q, L0_ffn_up_absmax, L0_ffn_down_q, L0_ffn_down_absmax):
    import concourse.bacc as bacc
    from concourse.bass_utils import run_bass_kernel_spmd

    def arr(a):
        return np.asarray(a)

    wk = arr(L0_attn_Wk).T.reshape(CT, P, UNITS, 1, P)
    wv = arr(L0_attn_Wv).T.reshape(CT, P, UNITS, 1, P)
    wq = arr(L0_attn_Wq).T.reshape(CT, P, 2, UNITS, P).transpose(0, 1, 3, 2, 4)
    w = np.concatenate([wk, wq, wv], axis=3).reshape(CT, P, 4 * HALF)
    bq = arr(L0_attn_bq).reshape(2, UNITS, P)
    bias_qk = np.stack([arr(L0_attn_bk).reshape(UNITS, P), bq[0], bq[1]], axis=2).transpose(1, 0, 2)
    ctx4 = arr(ctx_1024).reshape(B, TC, KVX, D)

    def gate_codes(q):
        return arr(q).reshape(MC, P, CT, P).transpose(0, 3, 2, 1).reshape(MC, P, C)

    def gate_scales(s):
        return arr(s).reshape(MC, P, CT, 2).transpose(0, 3, 2, 1).reshape(MC, 2, C)

    codes = np.stack([gate_codes(L0_ffn_gate_q), gate_codes(L0_ffn_up_q),
                      arr(L0_ffn_down_q).reshape(C, MC, P).transpose(1, 2, 0)], axis=1)
    scales = np.stack([gate_scales(L0_ffn_gate_absmax), gate_scales(L0_ffn_up_absmax),
                       arr(L0_ffn_down_absmax).reshape(C, MC, 2).transpose(1, 2, 0)], axis=1)
    arrays = {
        "x": arr(x),
        "w": w,
        "bias_qk": bias_qk,
        "bias_v": arr(L0_attn_bv).reshape(1, KV * D),
        "mask": arr(mask_SxS2_ff0),
        "ctx_kT": ctx4.transpose(0, 3, 2, 1).reshape(B, D, KVX * TC),
        "ctx_v": ctx4.reshape(B, TC, KVX * D),
        "codes": codes,
        "scales": scales,
    }
    arrays = {name: np.ascontiguousarray(a) for name, a in arrays.items()}
    nc = bacc.Bacc("TRN2", target_bir_lowering=False, num_devices=1)
    dram = {name: nc.dram_tensor("in_" + name, a.shape, mybir.dt.from_np(a.dtype), kind="ExternalInput").ap()
            for name, a in arrays.items()}
    dram["x2"] = nc.dram_tensor("x2", [B, T, C], FP32, kind="Internal").ap()
    dram["out"] = nc.dram_tensor("out", [B * T, C], FP32, kind="ExternalOutput").ap()
    decoder_layer(nc, dram)
    result = run_bass_kernel_spmd(nc, [{"in_" + name: a for name, a in arrays.items()}], core_ids=[0])
    return result.results[0]["out"].reshape(B, T, C)
```

```python
import math

import numpy as np

import concourse.bass as bass
from concourse import mybir
from contextlib import ExitStack

FP32 = mybir.dt.float32
FP16 = mybir.dt.float16
BF16 = mybir.dt.bfloat16
INT32 = mybir.dt.int32
ALU = mybir.AluOpType
ACT = mybir.ActivationFunctionType
AX_X = mybir.AxisListType.X

B, T, C = 4, 512, 1024
H, KV, D = 32, 16, 32
TC, KVX = 64, 8
M = 3584
P = 128
CT = C // P
QT = T // P
RT = B * QT
UNITS = KV // 4
PAIRS = 4
CHUNKS = 5
MC = M // P
GROUPS = MC // 2
HALF = 512
EPS = 1e-5

W_SCALE = 256.0
F_SCALE = 512.0
H_SCALE = 16.0
NEG = -1.0e30
SELF_SCALE = 1.0 / math.sqrt(H)
CROSS_SCALE = 1.0 / math.sqrt(D)

NF4 = [-1.0, -0.6961928009986877, -0.5250730514526367, -0.39491748809814453, -0.28444138169288635,
       -0.18477343022823334, -0.09105003625154495, 0.0, 0.07958029955625534, 0.16093020141124725,
       0.24611230194568634, 0.33791524171829224, 0.44070982933044434, 0.5626170039176941,
       0.7229568362236023, 1.0]


def code_line(lo, hi):
    slope = np.float32(F_SCALE * (NF4[hi] - NF4[lo]) / (hi - lo))
    return float(slope), float(np.float32(F_SCALE * NF4[lo] - float(slope) * lo))


LOWER_LINES = [code_line(5, 6), code_line(3, 4), code_line(1, 2), code_line(0, 1)]
UPPER_LINES = [code_line(7, 8), code_line(9, 10), code_line(11, 12), code_line(13, 14), code_line(14, 15)]
LINES = [UPPER_LINES[0], UPPER_LINES[1], LOWER_LINES[0], LOWER_LINES[1],
         UPPER_LINES[2], LOWER_LINES[2], UPPER_LINES[3], LOWER_LINES[3], UPPER_LINES[4]]
USED_BY = [1, 3, 2, 4, 5, 6, 7, 8, 8]
NL = len(LINES)
LUT = 8


class Attention:

    def __init__(self, nc, ctx):
        def sb(name, shape, dt):
            return ctx.enter_context(nc.sbuf_tensor(name, shape, dt))

        self.w_h = sb("w_h", [P, CT, 4 * HALF], FP16)
        self.w_l = sb("w_l", [P, CT, 4 * HALF], FP16)
        self.ident = sb("ident", [P, P], FP32)
        self.ident_b = sb("ident_b", [P, P], BF16)
        self.mask_qk = sb("mask_qk", [P, P], BF16)
        self.mask_kq = sb("mask_kq", [P, P], BF16)
        self.minus_half = sb("minus_half", [P, 1], FP32)
        self.bias_qk = sb("bias_qk", [P, UNITS, 3], FP32)
        self.bias_v = sb("bias_v", [P, KV * D], FP32)
        self.mask = sb("mask_x", [P, QT, TC], FP32)
        self.kx_h = sb("kx_h", [P, KVX, 4 * TC], FP16)
        self.kx_l = sb("kx_l", [P, KVX, 4 * TC], FP16)
        self.vx_h = sb("vx_h", [P, KVX, 2 * (D + 1)], FP16)
        self.vx_l = sb("vx_l", [P, KVX, 2 * (D + 1)], FP16)
        self.q_rows = sb("q_rows", [97, 2, 2 * PAIRS, T], FP16)
        self.k_rows = sb("k_rows", [97, 2, PAIRS, T], FP16)
        self.v_parts = sb("v_parts", [P, 2, QT, PAIRS, 2 * D + 1], FP16)


def attention(nc, t, dram):
    with ExitStack() as ctx:
        def sb(name, shape, dt):
            return ctx.enter_context(nc.sbuf_tensor(name, shape, dt))

        def sem(name):
            return ctx.enter_context(nc.semaphore(name))

        x_sb = sb("x_sb", [P, QT, C], FP32)
        xT_h = sb("xT_h", [P, CT, T], FP16)
        xT_l = sb("xT_l", [P, CT, T], FP16)
        x2T_h = sb("x2T_h", [P, 2, CT, P], FP16)
        x2T_l = sb("x2T_l", [P, 2, CT, P], FP16)
        stats = sb("stats", [P, 2, 2, 6], FP32)
        mean_var = sb("mean_var", [P, 2, 2], FP32)
        var_eps = sb("var_eps", [P, 2], FP32)
        rstd = sb("rstd", [P, 2], FP32)
        xn = sb("xn", [P, 2, C], FP32)
        proj32 = sb("proj32", [P, 2, HALF], FP32)
        nat_h = sb("nat_h", [P, 3, T], FP16)
        nat_l = sb("nat_l", [P, 3, T], FP16)
        v32 = sb("v32", [P, QT, PAIRS, D], FP32)
        block_max = sb("block_max", [P, PAIRS, CHUNKS, 4], FP32)
        row_max = sb("row_max", [P, PAIRS, 2, QT], FP32)
        neg_max = sb("neg_max", [2 * PAIRS * QT, P], FP16)
        p32 = sb("p32", [P, 4, HALF], FP32)
        p_h = sb("p_h", [P, 2, CHUNKS, HALF], FP16)
        p_l = sb("p_l", [P, 2, CHUNKS, HALF], FP16)
        r_sum = sb("r_sum", [P, 2, 2 * QT], FP32)
        o32 = sb("o32", [P, 2, QT, 2, D], FP32)
        k_raw = sb("k_raw", [P, KVX, TC], FP32)
        v_raw = sb("v_raw", [P, KVX, D], FP32)
        s_top = sb("s_top", [P, 2, 8], FP32)
        s32 = p32[:, 0:2, :].rearrange("p s (a t) -> p s a t", t=TC)
        e32 = p32[:, 2:4, :]
        px_h, px_l = p_h[:, 0, 0:2, :], p_l[:, 0, 0:2, :]
        w_raw = p32[:, :, :].rearrange("p (s c) n -> p s c n", c=2)
        bank = [ctx.enter_context(nc.psum_tensor(f"bank{i}", [P, HALF], FP32)) for i in range(8)]
        LN_BANK, PROJ_BANK, T_BANK, O_BANK = 0, 2, 4, 7

        zeroed = sem("zeroed")
        selected = sem("selected")
        small_loaded = sem("small_loaded")
        w_loaded = [sem(f"w_loaded{i}") for i in range(2)]
        w_high = sem("w_high")
        w_low = sem("w_low")
        row_loaded = [sem(f"row_loaded{i}") for i in range(2)]
        x_loaded = sem("x_loaded")
        ctx_loaded = sem("ctx_loaded")
        ctx_step = sem("ctx_step")
        ln_stat = sem("ln_stat")
        ln_rstd = sem("ln_rstd")
        ln_xn = sem("ln_xn")
        ln_turned = sem("ln_turned")
        ln_high = sem("ln_high")
        ln_low = sem("ln_low")
        proj_done = sem("proj_done")
        proj_out = sem("proj_out")
        proj_high = sem("proj_high")
        proj_low = sem("proj_low")
        rows_stacked = sem("rows_stacked")
        v_out = sem("v_out")
        v_high = sem("v_high")
        v_low = sem("v_low")
        scored = sem("scored")
        maxed = sem("maxed")
        rows_maxed = sem("rows_maxed")
        max_turned = sem("max_turned")
        max_out = sem("max_out")
        max_stacked = sem("max_stacked")
        t_scored = sem("t_scored")
        t_exp = sem("t_exp")
        p_high = sem("p_high")
        p_low = sem("p_low")
        o_done = sem("o_done")
        o_recip = sem("o_recip")
        o_read = sem("o_read")
        o_added = sem("o_added")
        x_scored = sem("x_scored")
        x_masked = sem("x_masked")
        x_topped = sem("x_topped")
        x_shifted = sem("x_shifted")
        x_exp = sem("x_exp")
        x_turned = sem("x_turned")
        x_high = sem("x_high")
        x_low = sem("x_low")
        x_done = sem("x_done")
        x_recip = sem("x_recip")
        x_read = sem("x_read")
        x_added = sem("x_added")
        stored = sem("stored")
        dve_tick = sem("dve_tick")
        sp_tick = sem("sp_tick")
        pool_tick = sem("pool_tick")
        block = ctx.enter_context(nc.Block())

        STACKS = 3 * 3 * 4
        NP = UNITS * PAIRS
        NCH = NP * CHUNKS
        NX = QT * 4
        NW = UNITS * CT // 2

        def ln_first(b, first):
            return 0 if first else 8 * b - 4

        def ln_cross(b, last):
            return 8 * b + (4 if last else 8)

        def score_parts(k):
            if k < 2:
                return [(0, k, 3, 512)]
            if k < 4:
                return [(0, k - 2, 0, 128), (128, k - 2, 2, 384)]
            return [(0, 0, 1, 256), (256, 1, 1, 256)]

        def t_parts(k):
            if k < 2:
                return [(0, k, 0)]
            if k < 4:
                return [(0, k - 2, 3), (128, k - 2, 1)]
            return [(0, 0, 2), (256, 1, 2)]

        def t_place(hh, kt, qt):
            if kt == 0:
                return hh, P * qt
            if kt == 1:
                return 2 + hh, P + P * (qt - 1)
            if kt == 2:
                return 4, 256 * hh + P * (qt - 2)
            return 2 + hh, 0

        @block.sync
        def _(sp):
            def held(ge_sem, value):
                sp.wait_ge(ge_sem, value)
                sp.sem_inc(sp_tick, 1)

            def load_row(b, i, at, first=False):
                src = dram["x"][bass.ds(b, 1), P * i:P * i + P, :].rearrange("b p c -> p (b c)")
                if not (first and i < 2):
                    held(ln_turned, 2 * at - 2)
                sp.dma_start(xn[:, i % 2, :], src).then_inc(row_loaded[i % 2], 16)

            def load_x(b, rt):
                src = dram["x"][bass.ds(b, 1), P * rt:P * rt + P, :].rearrange("b p c -> p (b c)")
                sp.dma_start(x_sb[:, rt, :], src).then_inc(x_loaded, 16)

            def load_w(n):
                g, c = n // 4, 2 * (n % 4)
                if n >= 2:
                    sp.wait_ge(w_low, n - 1)
                sp.dma_start(w_raw[:, n % 2, :, :],
                             dram["w"][c:c + 2, :, HALF * g:HALF * g + HALF].rearrange("c p n -> p c n"))\
                    .then_inc(w_loaded[n % 2], 16)

            def stack_rows(b, g, kind):
                held(proj_low, 3 * (UNITS * b + g) + kind + 1)
                for j in range(4):
                    for r in range(3):
                        if kind == 0:
                            src = (nat_h, nat_h, nat_l)[r]
                            dst = t.k_rows[D * r:D * r + D, g % 2, j, :]
                        else:
                            src = (nat_h, nat_l, nat_h)[r]
                            dst = t.q_rows[D * r:D * r + D, g % 2, 2 * j + kind - 1, :]
                        sp.dma_start(dst, src[D * j:D * j + D, kind, :]).then_inc(rows_stacked, 16)

            def stack_max(b, g):
                held(max_out, UNITS * b + g + 1)
                sp.dma_start(t.q_rows[96:97, g % 2, :, :].rearrange("o s (q n) -> o (s q) n", n=P),
                             neg_max[:, :]).then_inc(max_stacked, 16)

            def load_context(b):
                kT = dram["ctx_kT"][bass.ds(b, 1), :, :].rearrange("b d n -> d (b n)")
                v = dram["ctx_v"][bass.ds(b, 1), :, :].rearrange("b t n -> t (b n)")
                for r in range(4):
                    sp.dma_start(k_raw[D * r:D * r + D, :, :].rearrange("p g t -> p (g t)"), kT)\
                        .then_inc(ctx_loaded, 16)
                for j in range(2):
                    sp.dma_start(v_raw[TC * j:TC * j + TC, :, :].rearrange("p g d -> p (g d)"), v)\
                        .then_inc(ctx_loaded, 16)

            def store_x(b, rt):
                dst = dram["x2"][bass.ds(b, 1), P * rt:P * rt + P, :].rearrange("b p c -> p (b c)")
                held(x_added, NX * b + 4 * (rt + 1))
                sp.dma_start(dst, x_sb[:, rt, :]).then_inc(stored, 16)
                held(stored, 16 * (QT * b + rt + 1))

            def batch(b, last):
                load_context(b)
                for g in range(1, UNITS):
                    for kind in range(3):
                        stack_rows(b, g, kind)
                    stack_max(b, g)
                if not last:
                    for i in range(4):
                        load_row(b + 1, i, ln_first(b + 1, False) + i)
                for rt in range(QT):
                    if not last and rt < 3:
                        stack_rows(b + 1, 0, rt)
                    store_x(b, rt)
                    if not last:
                        load_x(b + 1, rt)
                if not last:
                    stack_max(b + 1, 0)

            sp.wait_ge(zeroed, 1)
            for i in range(2):
                load_row(0, i, i, True)
            for n in range(4):
                load_w(n)
                if n < 2:
                    load_row(0, 2 + n, 2 + n, True)
            sp.dma_start(t.bias_qk[:, :, :], dram["bias_qk"]).then_inc(small_loaded, 16)
            sp.dma_start(t.bias_v[:, :], dram["bias_v"].broadcast_to([P, KV * D])).then_inc(small_loaded, 16)
            sp.dma_start(t.mask[:, :, :], dram["mask"].rearrange("(r p) t -> p r t", p=P)).then_inc(small_loaded, 16)
            for n in range(4, NW):
                load_w(n)
                if n in (7, 8, 9):
                    stack_rows(0, 0, n - 7)
            for rt in range(QT):
                load_x(0, rt)
            stack_max(0, 0)
            with sp.Fori(0, B - 1) as b:
                batch(b, False)
            batch(B - 1, True)

        @block.gpsimd
        def _(pool):
            def held(ge_sem, value):
                pool.wait_ge(ge_sem, value)
                pool.sem_inc(pool_tick, 1)

            def ln_root(at, s):
                held(ln_stat, 4 * at + 4)
                nc.gpsimd.tensor_tensor(rstd[:, s:s + 1], var_eps[:, s:s + 1], t.minus_half[:, :],
                                        ALU.pow).then_inc(ln_rstd, 1)

            def low_parts(b, n):
                held(p_high, NCH * b + n + 1)
                dst = (n // CHUNKS % 2, n % CHUNKS)
                nc.gpsimd.tensor_tensor(p_l[:, dst[0], dst[1], :], p32[:, n % 4, :], p_h[:, dst[0], dst[1], :],
                                        ALU.subtract).then_inc(p_low, 1)

            def add_pair(b, n):
                g, j = n // PAIRS, n % PAIRS
                if n == 0:
                    held(x_loaded, 16 * QT * (b + 1))
                held(o_read, NP * b + n + 1)
                cols = slice(D * (4 * g + j), D * (4 * g + j) + D)
                x = x_sb[:, :, :].rearrange("p q (two r) -> p q two r", two=2)[:, :, :, cols]
                nc.gpsimd.tensor_tensor(x, o32[:, n % 2, :, :, :], x, ALU.add).then_inc(o_added, 1)

            def shift(b, n):
                s = s32[:, n % 2, :, :]
                held(x_topped, NX * b + n + 1)
                nc.gpsimd.tensor_tensor(s, s, s_top[:, n % 2, :].unsqueeze(2).broadcast_to([P, 8, TC]), ALU.subtract)\
                    .then_inc(x_shifted, 1)

            def add_cross(b, n):
                held(x_read, NX * b + n + 1)
                cols = x_sb[:, n // 4, 8 * D * (n % 4):8 * D * (n % 4 + 1)]
                nc.gpsimd.tensor_tensor(cols, o32[:, n % 2, :, :, :].rearrange("p q a d -> p (q a d)"), cols, ALU.add)\
                    .then_inc(x_added, 1)

            def batch(b, last):
                for n in range(NP):
                    j = n % PAIRS
                    turn = n // PAIRS == UNITS - 1 and not last
                    if turn and j == 0:
                        for i in range(2):
                            ln_root(ln_first(b + 1, False) + i, i)
                    for k in range(CHUNKS):
                        low_parts(b, CHUNKS * n + k)
                    if turn and j in (0, 1):
                        ln_root(ln_first(b + 1, False) + 2 + j, j)
                    if n >= 1:
                        add_pair(b, n - 1)
                add_pair(b, NP - 1)
                ln_root(ln_cross(b, last), 0)
                ln_root(ln_cross(b, last) + 1, 1)
                for n in range(NX + 2):
                    if n in (2, 6):
                        ln_root(ln_cross(b, last) + 2 + n // 4, n // 4)
                    if n < NX:
                        shift(b, n)
                    if n >= 2:
                        add_cross(b, n - 2)

            nc.gpsimd.memset(t.minus_half[:], -0.5).then_inc(zeroed, 1)
            nc.gpsimd.memset(t.ident[:], 0.0).then_inc(zeroed, 1)
            pool.wait_ge(zeroed, 2)
            nc.gpsimd.affine_select(out=t.ident[:, :], in_=t.ident[:, :], compare_op=ALU.not_equal, fill=1.0, base=0,
                                    pattern=[[-1, P]], channel_multiplier=1).then_inc(selected, 1)
            for i in range(4):
                ln_root(i, i % 2)
            cleared = [t.ident_b, t.mask_qk, t.mask_kq, t.v_parts, t.kx_h, t.kx_l, t.vx_h, t.vx_l]
            for buf in cleared:
                nc.gpsimd.memset(buf[:], 0.0).then_inc(zeroed, 1)
            pool.wait_ge(zeroed, len(cleared) + 2)
            nc.gpsimd.affine_select(out=t.ident_b[:, :], in_=t.ident_b[:, :], compare_op=ALU.not_equal, fill=1.0,
                                    base=0, pattern=[[-1, P]], channel_multiplier=1).then_inc(selected, 1)
            nc.gpsimd.affine_select(out=t.mask_qk[:, :], in_=t.mask_qk[:, :], compare_op=ALU.is_ge, fill=NEG, base=0,
                                    pattern=[[-1, P]], channel_multiplier=1).then_inc(selected, 1)
            nc.gpsimd.affine_select(out=t.mask_kq[:, :], in_=t.mask_kq[:, :], compare_op=ALU.is_ge, fill=NEG, base=0,
                                    pattern=[[1, P]], channel_multiplier=-1).then_inc(selected, 1)
            nc.gpsimd.memset(t.v_parts[:, :, :, :, D:D + 1], 1.0).then_inc(selected, 1)
            pool.wait_ge(selected, 5)
            nc.gpsimd.memset(t.k_rows[96:97, :, :, :], 1.0).then_inc(selected, 1)
            for j in range(2):
                pool.wait_ge(selected, 6 + j)
                nc.gpsimd.memset(t.vx_h[TC * j:TC * j + TC, :, (D + 1) * j + D:(D + 1) * j + D + 1], 1.0)\
                    .then_inc(selected, 1)
            pool.wait_ge(selected, 8)
            with pool.Fori(0, B - 1) as b:
                batch(b, False)
            batch(B - 1, True)

        @block.tensor
        def _(pe):
            def ln_turn(at, i, first=False):
                pe.wait_ge(ln_xn, at + 1)
                for half in range(2):
                    if not (first and i == 0):
                        pe.wait_ge(ln_low, 2 * at + half - 1)
                    for c in range(4):
                        mm = nc.tensor.transpose(bank[LN_BANK + half][:, P * c:P * c + P],
                                                 xn[:, i % 2, P * (4 * half + c):P * (4 * half + c + 1)],
                                                 t.ident[:, :])
                    mm.then_inc(ln_turned, 1)

            def project(b, g, kind, pieces=range(4), first=False):
                dst = bank[PROJ_BANK + (5 * g + kind) % 2]
                cols = slice(HALF * g + P * kind, HALF * g + P * kind + P)
                if 0 in pieces:
                    if kind == 0 and g == 0:
                        pe.wait_ge(ln_low, 2 * ln_first(b, first) + 8)
                    if kind == 0 and not first:
                        pe.wait_ge(v_out, UNITS * b + g)
                    if kind == 1 and not first:
                        pe.wait_ge(max_out, UNITS * b + g)
                    if kind >= 2:
                        pe.wait_ge(proj_out, 3 * (UNITS * b + g) + kind - 1)
                for piece in pieces:
                    if kind < 3:
                        for c in (2 * piece, 2 * piece + 1):
                            if first and kind == 0:
                                pe.wait_ge(w_low, piece + 1)
                            for m, (w, x) in enumerate(((t.w_h, xT_h), (t.w_h, xT_l), (t.w_l, xT_h))):
                                mm = nc.tensor.matmul(dst[:, :], w[:, c, cols], x[:, c, :],
                                                      start=(c == 0 and m == 0), stop=(c == CT - 1 and m == 2))
                    else:
                        rows = slice(P * piece, P * piece + P)
                        for c in range(CT):
                            for m, (w, x) in enumerate(((t.w_h, xT_h), (t.w_h, xT_l), (t.w_l, xT_h))):
                                mm = nc.tensor.matmul(dst[:, rows], x[:, c, rows], w[:, c, cols],
                                                      start=(c == 0 and m == 0), stop=(c == CT - 1 and m == 2))
                if 3 in pieces:
                    mm.then_inc(proj_done, 1)

            def score(b, n, first=False):
                g, j = n // PAIRS, n % PAIRS
                if j == 0:
                    pe.wait_ge(rows_stacked, 16 * STACKS * (UNITS * b + g + 1))
                for k in range(CHUNKS):
                    m = CHUNKS * n + k
                    if m >= 2:
                        pe.wait_ge(maxed, NCH * b + m - 1)
                    for col, hh, qt, keys in score_parts(k):
                        nc.tensor.matmul(bank[LN_BANK + m % 2][:, col:col + keys],
                                         t.q_rows[0:96, g % 2, 2 * j + hh, P * qt:P * qt + P],
                                         t.k_rows[0:96, g % 2, j, 0:keys], start=True, stop=False)
                        mm = nc.tensor.matmul(bank[LN_BANK + m % 2][:, col + P * qt:col + P * qt + P],
                                              t.ident_b[:, :], t.mask_qk[:, :], start=False, stop=True)
                    mm.then_inc(scored, 1)

            def turn_max(b, g):
                pe.wait_ge(rows_maxed, 4 * (UNITS * b + g + 1))
                pe.wait_ge(proj_out, 3 * (UNITS * b + g + 1))
                nc.tensor.transpose(bank[PROJ_BANK + (5 * g + 4) % 2][0:2 * PAIRS * QT, 0:P],
                                    row_max[:, :, :, :].rearrange("p j a q -> p (j a q)"), t.ident[:, :])\
                    .then_inc(max_turned, 1)

            def t_score(b, n):
                g, j = n // PAIRS, n % PAIRS
                if j == 0:
                    pe.wait_ge(max_stacked, 16 * (UNITS * b + g + 1))
                for k in range(CHUNKS):
                    m = CHUNKS * n + k
                    if m >= 3:
                        pe.wait_ge(t_exp, NCH * b + m - 2)
                    for col, hh, kt in t_parts(k):
                        nc.tensor.matmul(bank[T_BANK + m % 3][:, col:col + T - P * kt],
                                         t.k_rows[0:97, g % 2, j, P * kt:P * kt + P],
                                         t.q_rows[0:97, g % 2, 2 * j + hh, P * kt:T], start=True, stop=False)
                        mm = nc.tensor.matmul(bank[T_BANK + m % 3][:, col:col + P],
                                              t.ident_b[:, :], t.mask_kq[:, :], start=False, stop=True)
                    mm.then_inc(t_scored, 1)

            def weigh(b, n):
                g, j = n // PAIRS, n % PAIRS
                if j == 0:
                    pe.wait_ge(v_low, UNITS * b + g + 1)
                pe.wait_ge(p_low, CHUNKS * (NP * b + n + 1))
                if n >= 1:
                    pe.wait_ge(o_read, NP * b + n)
                for qt in range(QT):
                    for hh in range(2):
                        col = (D + 1) * (2 * qt + hh)
                        for kt in range(qt + 1):
                            k, at = t_place(hh, kt, qt)
                            high = p_h[:, n % 2, k, at:at + P]
                            low = p_l[:, n % 2, k, at:at + P]
                            v = t.v_parts[:, g % 2, kt, j, :]
                            out = bank[O_BANK]
                            nc.tensor.matmul(out[:, col:col + D + 1], high, v[:, 0:D + 1],
                                             start=(kt == 0), stop=False)
                            nc.tensor.matmul(out[:, col:col + D], high, v[:, D + 1:2 * D + 1],
                                             start=False, stop=False)
                            mm = nc.tensor.matmul(out[:, col:col + D + 1], low, v[:, 0:D + 1],
                                                  start=False, stop=(kt == qt))
                mm.then_inc(o_done, 1)

            def x_score(b, n, last):
                rt = n // 4
                if n % 4 == 0:
                    pe.wait_ge(ln_low, 2 * (ln_cross(b, last) + rt + 1))
                if n == 0:
                    pe.wait_ge(ctx_step, 13 * (b + 1))
                if n >= 2:
                    pe.wait_ge(x_masked, NX * b + n - 1)
                for part in range(2):
                    g = 2 * (n % 4) + part
                    for i, (x, k) in enumerate(((x2T_h, t.kx_h), (x2T_l, t.kx_h), (x2T_h, t.kx_l))):
                        mm = nc.tensor.matmul(bank[T_BANK + n % 2][:, 256 * part:256 * part + 256],
                                              x[:, rt % 2, g, :], k[:, g, :], start=(i == 0), stop=(i == 2))
                mm.then_inc(x_scored, 1)

            def x_weigh(b, n):
                pe.wait_ge(x_low, NX * b + n + 1)
                if n >= 1:
                    pe.wait_ge(x_read, NX * b + n)
                W = 2 * (D + 1)
                for i in range(4):
                    g = 2 * (n % 4) + i // 2
                    for m, (p, v) in enumerate(((px_h, t.vx_h), (px_h, t.vx_l), (px_l, t.vx_h))):
                        mm = nc.tensor.matmul(bank[O_BANK][:, W * i:W * i + W], p[:, n % 2, P * i:P * i + P],
                                              v[:, g, :], start=(m == 0), stop=(m == 2))
                mm.then_inc(x_done, 1)

            def x_turn(b, n):
                pe.wait_ge(x_exp, NX * b + n + 1)
                for i in range(4):
                    mm = nc.tensor.transpose(bank[T_BANK + 2][:, P * i:P * i + P], e32[:, n % 2, P * i:P * i + P],
                                             t.ident[:, :])
                mm.then_inc(x_turned, 1)

            def unit(b, g, last):
                n, nn = PAIRS * g, PAIRS * (g + 1)
                more = g + 1 < UNITS
                turns = not more and not last
                at = ln_first(b + 1, False)
                for j in range(PAIRS):
                    if more and j < 3:
                        project(b, g + 1, j)
                    t_score(b, n + j)
                    if j >= 1:
                        weigh(b, n + j - 1)
                    if turns:
                        ln_turn(at + j, j)
                for j in range(PAIRS):
                    if more:
                        score(b, nn + j)
                        project(b, g + 1, 3, (j,))
                    if j == 1:
                        weigh(b, n + 3)
                if more:
                    turn_max(b, g + 1)

            def tail(b, last):
                at = ln_cross(b, last)
                ln_turn(at, 0)
                ln_turn(at + 1, 1)
                for n in range(NX + 2):
                    if n in (3, 7):
                        ln_turn(at + 2 + n // 4, n // 4)
                    if n < NX:
                        x_score(b, n, last)
                        if not last:
                            project(b + 1, 0, n // 4, (n % 4,))
                    if n >= 2:
                        x_weigh(b, n - 2)
                    if 1 <= n <= NX:
                        x_turn(b, n - 1)
                if not last:
                    for j in range(PAIRS):
                        score(b + 1, j)
                    turn_max(b + 1, 0)

            pe.wait_ge(selected, 1)
            for i in range(4):
                ln_turn(i, i, True)
            for kind in range(4):
                project(0, 0, kind, first=True)
            pe.wait_ge(selected, 8)
            for j in range(PAIRS):
                score(0, j)
            turn_max(0, 0)
            pe.wait_ge(w_low, NW)
            with pe.Fori(0, B - 1) as b:
                for g in range(UNITS):
                    unit(b, g, False)
                tail(b, False)
            for g in range(UNITS):
                unit(B - 1, g, True)
            tail(B - 1, True)

        @block.scalar
        def _(act):
            def cut_w(n):
                act.wait_ge(w_loaded[n % 2], 16 * (n // 2 + 1))
                g, c = n // 4, 2 * (n % 4)
                nc.scalar.activation(t.w_h[:, c:c + 2, HALF * g:HALF * g + HALF], w_raw[:, n % 2, :, :], ACT.Copy,
                                     scale=W_SCALE).then_inc(w_high, 1)

            def ln_high_parts(at, dst):
                for half in range(2):
                    act.wait_ge(ln_turned, 2 * at + half + 1)
                    nc.scalar.activation(dst[:, 4 * half:4 * half + 4, :],
                                         bank[LN_BANK + half][:, :].rearrange("p (c n) -> p c n", n=P), ACT.Copy)\
                        .then_inc(ln_high, 1)

            def proj_parts(b, g, kind, first=False):
                n = 3 * (UNITS * b + g) + kind
                slot = (3 * g + kind) % 2
                act.wait_ge(proj_done, 4 * (UNITS * b + g) + kind + 1)
                if not (first and kind < 2):
                    act.wait_ge(proj_low, n - 1)
                nc.scalar.activation(proj32[:, slot, :], bank[PROJ_BANK + (5 * g + kind) % 2][:, :], ACT.Identity,
                                     bias=t.bias_qk[:, g, kind:kind + 1], scale=1.0 / W_SCALE)\
                    .then_inc(proj_out, 1)
                act.wait_ge(proj_out, n + 1)
                if kind == 0 and not first:
                    act.wait_ge(rows_stacked, 16 * STACKS * (UNITS * b + g))
                nc.scalar.activation(nat_h[:, kind, :], proj32[:, slot, :], ACT.Copy).then_inc(proj_high, 1)

            def v_parts(b, g):
                act.wait_ge(v_out, UNITS * b + g + 1)
                nc.scalar.activation(t.v_parts[:, g % 2, :, :, 0:D], v32[:, :, :, :], ACT.Copy).then_inc(v_high, 1)

            def max_rows(b, g, first=False):
                act.wait_ge(max_turned, UNITS * b + g + 1)
                if not first:
                    act.wait_ge(max_stacked, 16 * (UNITS * b + g))
                nc.scalar.activation(neg_max[:, :], bank[PROJ_BANK + (5 * g + 4) % 2][0:2 * PAIRS * QT, 0:P],
                                     ACT.Copy, scale=-1.0).then_inc(max_out, 1)

            def exps(b, n):
                act.wait_ge(t_scored, NCH * b + n + 1)
                if n >= 4:
                    act.wait_ge(p_low, NCH * b + n - 3)
                nc.scalar.activation(p32[:, n % 4, :], bank[T_BANK + n % 3][:, :], ACT.Exp, scale=SELF_SCALE)\
                    .then_inc(t_exp, 1)

            def high_parts(b, n):
                act.wait_ge(t_exp, NCH * b + n + 1)
                if n % CHUNKS == 0 and n >= 2 * CHUNKS:
                    act.wait_ge(o_done, NP * b + n // CHUNKS - 1)
                nc.scalar.activation(p_h[:, n // CHUNKS % 2, n % CHUNKS, :], p32[:, n % 4, :], ACT.Copy)\
                    .then_inc(p_high, 1)

            def x_exps(b, n):
                act.wait_ge(x_shifted, NX * b + n + 1)
                if n >= 2:
                    act.wait_ge(x_turned, NX * b + n - 1)
                nc.scalar.activation(e32[:, n % 2, :], s32[:, n % 2, :, :].rearrange("p a t -> p (a t)"), ACT.Exp)\
                    .then_inc(x_exp, 1)

            def x_high_parts(b, n):
                act.wait_ge(x_turned, NX * b + n + 1)
                if n >= 2:
                    act.wait_ge(x_done, NX * b + n - 1)
                nc.scalar.activation(px_h[:, n % 2, :], bank[T_BANK + 2][:, :], ACT.Copy).then_inc(x_high, 1)

            def unit(b, g, last):
                more = g + 1 < UNITS
                for j in range(PAIRS):
                    if more and j < 3:
                        proj_parts(b, g + 1, j)
                    first = CHUNKS * (PAIRS * g + j)
                    for n in range(first, first + CHUNKS):
                        exps(b, n)
                        if n > first:
                            high_parts(b, n - 1)
                    high_parts(b, first + CHUNKS - 1)
                    if not more and not last:
                        ln_high_parts(ln_first(b + 1, False) + j, xT_h[:, :, P * j:P * j + P])
                if more:
                    v_parts(b, g + 1)
                    max_rows(b, g + 1)

            def tail(b, last):
                at = ln_cross(b, last)
                ln_high_parts(at, x2T_h[:, 0, :, :])
                ln_high_parts(at + 1, x2T_h[:, 1, :, :])
                for n in range(NX + 1):
                    if n < NX:
                        x_exps(b, n)
                    if n >= 1:
                        x_high_parts(b, n - 1)
                    if n in (3, 7):
                        act.wait_ge(x_scored, NX * b + n + 1)
                        ln_high_parts(at + 2 + n // 4, x2T_h[:, n // 4, :, :])
                    if n in (4, 8, 12) and not last:
                        proj_parts(b + 1, 0, n // 4 - 1)
                if not last:
                    v_parts(b + 1, 0)
                    max_rows(b + 1, 0)

            for i in range(4):
                cut_w(i)
                ln_high_parts(i, xT_h[:, :, P * i:P * i + P])
            act.wait_ge(small_loaded, 48)
            for n in range(4, NW):
                if n in (7, 8, 9):
                    proj_parts(0, 0, n - 7, True)
                cut_w(n)
            act.wait_ge(selected, 8)
            v_parts(0, 0)
            max_rows(0, 0, True)
            with act.Fori(0, B - 1) as b:
                for g in range(UNITS):
                    unit(b, g, False)
                tail(b, False)
            for g in range(UNITS):
                unit(B - 1, g, True)
            tail(B - 1, True)

        @block.vector
        def _(dve):
            def cut_w(n):
                g, c = n // 4, 2 * (n % 4)
                cols = (slice(None), slice(c, c + 2), slice(HALF * g, HALF * g + HALF))
                dve.wait_ge(w_high, n + 1)
                nc.vector.scalar_tensor_tensor(t.w_l[cols], w_raw[:, n % 2, :, :], W_SCALE, t.w_h[cols],
                                               ALU.mult, ALU.subtract).then_inc(w_low, 1)

            def lay_context(b):
                dve.wait_ge(ctx_loaded, 16 * 6 * (b + 1))
                base = 13 * b
                nc.vector.tensor_scalar(k_raw[:, :, :], k_raw[:, :, :], CROSS_SCALE, None, ALU.mult)\
                    .then_inc(ctx_step, 1)
                dve.wait_ge(ctx_step, base + 1)
                for r in range(4):
                    rows, cols = slice(D * r, D * r + D), slice(TC * r, TC * r + TC)
                    nc.vector.tensor_copy(t.kx_h[rows, :, cols], k_raw[rows, :, :]).then_inc(ctx_step, 1)
                for j in range(2):
                    rows, cols = slice(TC * j, TC * j + TC), slice((D + 1) * j, (D + 1) * j + D)
                    nc.vector.tensor_copy(t.vx_h[rows, :, cols], v_raw[rows, :, :]).then_inc(ctx_step, 1)
                dve.wait_ge(ctx_step, base + 7)
                for r in range(4):
                    rows, cols = slice(D * r, D * r + D), slice(TC * r, TC * r + TC)
                    nc.vector.tensor_tensor(t.kx_l[rows, :, cols], k_raw[rows, :, :], t.kx_h[rows, :, cols],
                                            ALU.subtract).then_inc(ctx_step, 1)
                for j in range(2):
                    rows, cols = slice(TC * j, TC * j + TC), slice((D + 1) * j, (D + 1) * j + D)
                    nc.vector.tensor_tensor(t.vx_l[rows, :, cols], v_raw[rows, :, :], t.vx_h[rows, :, cols],
                                            ALU.subtract).then_inc(ctx_step, 1)

            def ln_stats(at, s, row):
                for half in range(2):
                    nc.vector.bn_stats(stats[:, s, half, :], row[:, HALF * half:HALF * half + HALF])\
                        .then_inc(ln_stat, 1)
                dve.wait_ge(ln_stat, 4 * at + 2)
                dve.sem_inc(dve_tick, 1)
                nc.vector.bn_aggr(mean_var[:, s, :], stats[:, s, :, :]).then_inc(ln_stat, 1)
                dve.wait_ge(ln_stat, 4 * at + 3)
                nc.vector.tensor_scalar(var_eps[:, s:s + 1], mean_var[:, s, 1:2], EPS, None, ALU.add)\
                    .then_inc(ln_stat, 1)

            def ln_normal(at, s, row):
                dve.wait_ge(ln_rstd, at + 1)
                nc.vector.tensor_scalar(xn[:, s, :], row, mean_var[:, s, 0:1], rstd[:, s:s + 1],
                                        ALU.subtract, ALU.mult).then_inc(ln_xn, 1)

            def ln_low_parts(at, dst_h, dst_l):
                for half in range(2):
                    dve.wait_ge(ln_high, 2 * at + half + 1)
                    cols = (slice(None), slice(4 * half, 4 * half + 4), slice(None))
                    nc.vector.tensor_tensor(dst_l[cols], bank[LN_BANK + half][:, :].rearrange("p (c n) -> p c n", n=P),
                                            dst_h[cols], ALU.subtract).then_inc(ln_low, 1)

            def first_stats(b, i, first=False):
                dve.wait_ge(row_loaded[i % 2], 16 * (2 * b + i // 2 + 1))
                ln_stats(ln_first(b, first) + i, i % 2, xn[:, i % 2, :])

            def first_normal(b, i, first=False):
                ln_normal(ln_first(b, first) + i, i % 2, xn[:, i % 2, :])

            def first_low(b, i, first=False):
                cols = slice(P * i, P * i + P)
                ln_low_parts(ln_first(b, first) + i, xT_h[:, :, cols], xT_l[:, :, cols])

            def cross_normal(b, i, last):
                at = ln_cross(b, last) + i
                ln_stats(at, i % 2, x_sb[:, i, :])
                dve.wait_ge(ln_turned, 2 * at - 2)
                ln_normal(at, i % 2, x_sb[:, i, :])

            def cross_low(b, i, last):
                ln_low_parts(ln_cross(b, last) + i, x2T_h[:, i % 2, :, :], x2T_l[:, i % 2, :, :])

            def proj_low_parts(b, g, kind):
                dve.wait_ge(proj_high, 3 * (UNITS * b + g) + kind + 1)
                nc.vector.tensor_tensor(nat_l[:, kind, :], proj32[:, (3 * g + kind) % 2, :], nat_h[:, kind, :],
                                        ALU.subtract).then_inc(proj_low, 1)

            def v_parts(b, g):
                dve.wait_ge(proj_done, 4 * (UNITS * b + g + 1))
                bias = t.bias_v[:, P * g:P * g + P].unsqueeze(1).broadcast_to([P, QT, P])
                nc.vector.scalar_tensor_tensor(v32[:, :, :, :].rearrange("p q j d -> p q (j d)"),
                                               bank[PROJ_BANK + (5 * g + 3) % 2][:, :]
                                               .rearrange("p (q n) -> p q n", n=P),
                                               1.0 / W_SCALE, bias, ALU.mult, ALU.add).then_inc(v_out, 1)
                dve.wait_ge(v_high, UNITS * b + g + 1)
                nc.vector.tensor_tensor(t.v_parts[:, g % 2, :, :, D + 1:2 * D + 1], v32[:, :, :, :],
                                        t.v_parts[:, g % 2, :, :, 0:D], ALU.subtract).then_inc(v_low, 1)

            def maxima(b, n):
                for k in range(CHUNKS):
                    m = CHUNKS * n + k
                    dve.wait_ge(scored, NCH * b + m + 1)
                    nc.vector.reduce_max(block_max[:, n % PAIRS, k, :],
                                         bank[LN_BANK + m % 2][:, :].rearrange("p (a n) -> p a n", n=P), AX_X)\
                        .then_inc(maxed, 1)

            def row_maxima(b, g):
                dve.wait_ge(maxed, NCH * b + CHUNKS * PAIRS * (g + 1))
                nc.vector.reduce_max(row_max[:, :, :, 3], block_max[:, :, 0:2, :], AX_X).then_inc(rows_maxed, 1)
                nc.vector.reduce_max(row_max[:, :, :, 2], block_max[:, :, 2:4, 1:4], AX_X).then_inc(rows_maxed, 1)
                nc.vector.tensor_copy(row_max[:, :, :, 0], block_max[:, :, 2:4, 0]).then_inc(rows_maxed, 1)
                nc.vector.reduce_max(row_max[:, :, :, 1],
                                     block_max[:, :, 4, :].rearrange("p j (a n) -> p j a n", n=2), AX_X)\
                    .then_inc(rows_maxed, 1)

            def pair_out(b, n):
                dve.wait_ge(o_done, NP * b + n + 1)
                out = bank[O_BANK][:, 0:(D + 1) * 2 * QT].rearrange("p (s d) -> p s d", d=D + 1)
                nc.vector.reciprocal(r_sum[:, n % 2, :], out[:, :, D]).then_inc(o_recip, 1)
                dve.wait_ge(o_recip, NP * b + n + 1)
                if n >= 2:
                    dve.wait_ge(o_added, NP * b + n - 1)
                nc.vector.tensor_tensor(o32[:, n % 2, :, :, :].rearrange("p q a d -> p (q a) d"), out[:, :, 0:D],
                                        r_sum[:, n % 2, :].unsqueeze(2).broadcast_to([P, 2 * QT, D]), ALU.mult)\
                    .then_inc(o_read, 1)

            def x_soft(b, n):
                s = s32[:, n % 2, :, :]
                dve.wait_ge(x_scored, NX * b + n + 1)
                if n >= 2:
                    dve.wait_ge(x_exp, NX * b + n - 1)
                nc.vector.tensor_tensor(s, bank[T_BANK + n % 2][:, :].rearrange("p (a t) -> p a t", t=TC),
                                        t.mask[:, n // 4, :].unsqueeze(1).broadcast_to([P, 8, TC]), ALU.add)\
                    .then_inc(x_masked, 1)
                dve.wait_ge(x_masked, NX * b + n + 1)
                nc.vector.reduce_max(s_top[:, n % 2, :], s, AX_X).then_inc(x_topped, 1)

            def x_low_parts(b, n):
                dve.wait_ge(x_high, NX * b + n + 1)
                nc.vector.tensor_tensor(px_l[:, n % 2, :], bank[T_BANK + 2][:, :], px_h[:, n % 2, :],
                                        ALU.subtract).then_inc(x_low, 1)

            def x_out(b, n):
                dve.wait_ge(x_done, NX * b + n + 1)
                out = bank[O_BANK][:, 0:(D + 1) * 8].rearrange("p (s d) -> p s d", d=D + 1)
                nc.vector.reciprocal(r_sum[:, n % 2, :], out[:, :, D]).then_inc(x_recip, 1)
                dve.wait_ge(x_recip, NX * b + n + 1)
                if n >= 2:
                    dve.wait_ge(x_added, NX * b + n - 1)
                nc.vector.tensor_tensor(o32[:, n % 2, :, :, :].rearrange("p q a d -> p (q a) d"), out[:, :, 0:D],
                                        r_sum[:, n % 2, :].unsqueeze(2).broadcast_to([P, 8, D]), ALU.mult)\
                    .then_inc(x_read, 1)

            def unit(b, g, last):
                n, nn = PAIRS * g, PAIRS * (g + 1)
                if g == 0:
                    lay_context(b)
                if g + 1 < UNITS:
                    for j in range(3):
                        proj_low_parts(b, g + 1, j)
                        if j >= 1:
                            pair_out(b, n + j - 1)
                    maxima(b, nn)
                    pair_out(b, n + 2)
                    maxima(b, nn + 1)
                    maxima(b, nn + 2)
                    pair_out(b, n + 3)
                    maxima(b, nn + 3)
                    row_maxima(b, g + 1)
                    v_parts(b, g + 1)
                elif last:
                    for j in range(PAIRS):
                        pair_out(b, n + j)
                else:
                    first_stats(b + 1, 0)
                    first_stats(b + 1, 1)
                    first_normal(b + 1, 0)
                    first_normal(b + 1, 1)
                    for j in range(PAIRS):
                        first_low(b + 1, j)
                        if j < 2:
                            first_stats(b + 1, j + 2)
                            first_normal(b + 1, j + 2)
                        pair_out(b, n + j)

            def tail(b, last):
                dve.wait_ge(o_added, NP * (b + 1))
                cross_normal(b, 0, last)
                cross_normal(b, 1, last)
                cross_low(b, 0, last)
                cross_low(b, 1, last)
                for n in range(NX + 2):
                    if n in (2, 6):
                        cross_normal(b, 2 + n // 4, last)
                    if n < NX:
                        x_soft(b, n)
                    if 1 <= n <= NX:
                        x_low_parts(b, n - 1)
                    if n >= 2:
                        x_out(b, n - 2)
                    if n in (3, 7):
                        cross_low(b, 2 + n // 4, last)
                    if n in (4, 8, 12) and not last:
                        proj_low_parts(b + 1, 0, n // 4 - 1)
                if not last:
                    v_parts(b + 1, 0)
                    for j in range(PAIRS):
                        maxima(b + 1, j)
                    row_maxima(b + 1, 0)

            for i in range(4):
                first_stats(0, i, True)
                first_normal(0, i, True)
                if i:
                    cut_w(i - 1)
                    first_low(0, i - 1, True)
            cut_w(3)
            first_low(0, 3, True)
            for n in range(4, NW):
                if n in (7, 8, 9):
                    proj_low_parts(0, 0, n - 7)
                cut_w(n)
            dve.wait_ge(small_loaded, 48)
            v_parts(0, 0)
            for j in range(PAIRS):
                maxima(0, j)
            row_maxima(0, 0)
            dve.wait_ge(selected, 8)
            with dve.Fori(0, B - 1) as b:
                for g in range(UNITS):
                    unit(b, g, False)
                tail(b, False)
            for g in range(UNITS):
                unit(B - 1, g, True)
            tail(B - 1, True)


def feed_forward(nc, dram):
    with ExitStack() as ctx:
        def sb(name, shape, dt):
            return ctx.enter_context(nc.sbuf_tensor(name, shape, dt))

        def sem(name):
            return ctx.enter_context(nc.semaphore(name))

        y = sb("y", [P, RT, C], FP32)
        xT_h = sb("fT_h", [P, CT, B * T], FP16)
        xT_l = sb("fT_l", [P, CT, B * T], FP16)
        hT_h = sb("hT_h", [P, 2, B * T], FP16)
        hT_l = sb("hT_l", [P, 2, B * T], FP16)
        up_h = sb("up_h", [P, 2, 2, C], FP16)
        up_l = sb("up_l", [P, 2, 2, C], FP16)
        dn_h = sb("dn_h", [P, 2, C], FP16)
        dn_l = sb("dn_l", [P, 2, C], FP16)
        codes = sb("codes", [P, 2, HALF], INT32)
        scales = sb("scales", [P, 2, HALF], FP32)
        line = sb("line", [P, NL, HALF], FP32)
        w32 = sb("w32", [P, 2, HALF], FP32)
        silu = sb("silu", [P, 2, HALF], FP32)
        h32 = sb("h32", [P, 2, HALF], FP32)
        xn = line[:, 0:2, :].rearrange("p a n -> p (a n)")
        ident = sb("f_ident", [P, P], FP32)
        minus_half = sb("f_minus_half", [P, 1], FP32)
        stats = sb("f_stats", [P, 2, 2, 6], FP32)
        mean_var = sb("f_mean_var", [P, 2, 2], FP32)
        var_eps = sb("f_var_eps", [P, 2], FP32)
        rstd = sb("f_rstd", [P, 2], FP32)
        bank = [ctx.enter_context(nc.psum_tensor(f"f_bank{i}", [P, HALF], FP32)) for i in range(8)]
        GATE, UP, DOWN = 0, 2, 4

        y_loaded = [sem(f"y_loaded{i}") for i in range(4)]
        consts = sem("consts")
        ln_stat = sem("f_ln_stat")
        ln_rstd = sem("f_ln_rstd")
        ln_xn = sem("f_ln_xn")
        ln_turned = sem("f_ln_turned")
        ln_high = sem("f_ln_high")
        ln_low = sem("f_ln_low")
        codes_loaded = [sem(f"codes_loaded{i}") for i in range(2)]
        scales_loaded = [sem(f"scales_loaded{i}") for i in range(2)]
        lined = sem("lined")
        lut = sem("lut")
        scaled = sem("scaled")
        w_high = sem("fw_high")
        w_low = sem("fw_low")
        gate_done = sem("gate_done")
        up_done = sem("up_done")
        silu_done = sem("silu_done")
        h_done = sem("h_done")
        h_high = sem("h_high")
        h_low = sem("h_low")
        down_done = sem("down_done")
        y_added = sem("y_added")
        stored = sem("y_stored")
        sp_tick = sem("f_sp_tick")
        pool_tick = sem("f_pool_tick")
        block = ctx.enter_context(nc.Block())

        NB = B
        NQ = 2 * NB
        ND = 2 * RT
        AHEAD = 4
        PER = 12
        FREE = 2

        def tile_of(k):
            if k < 0:
                return 0, (k + 4) // 2, k % 2
            if k < 4:
                return 1, k // 2, k % 2
            if k < 8:
                return (k - 4) // 2, 2, k % 2
            return 2, (k - 8) // 2, k % 2

        STEPS = [[0, 1], [2, 3], [4], [5], [6], [7], [8], [9], [10, 11]]

        def last_k(last):
            return 8 if last else PER

        def cut_with(k, last):
            if k >= last_k(last):
                return []
            return ([k - 1] if k % 4 else []) + ([k] if k % 4 == 3 else [])

        def weights(chunk, kind, half):
            cols = slice(HALF * half, HALF * half + HALF)
            if kind == 2:
                return dn_h[:, chunk % 2, cols], dn_l[:, chunk % 2, cols]
            return up_h[:, chunk % 2, kind, cols], up_l[:, chunk % 2, kind, cols]

        @block.sync
        def _(sp):
            def load(i, k, t):
                chunk, kind, half = tile_of(k)
                cols = slice(HALF * half, HALF * half + HALF)
                code = dram["codes"][bass.ds(2 * i + chunk, 1), kind, :, cols].rearrange("a p n -> p (a n)")
                scale = [dram["scales"][bass.ds(2 * i + chunk, 1), kind, s, cols].broadcast_to([P // 2, HALF])
                         for s in range(2)]
                slot = k % 2
                if k > -3:
                    sp.wait_ge(lined, NL * (t - 1))
                    sp.sem_inc(sp_tick, 1)
                sp.dma_start(codes[:, slot, :], code).then_inc(codes_loaded[slot], 16)
                if k > -3:
                    sp.wait_ge(scaled, t - 1)
                    sp.sem_inc(sp_tick, 1)
                for s in range(2):
                    sp.dma_start(scales[P // 2 * s:P // 2 * (s + 1), slot, :], scale[s])\
                        .then_inc(scales_loaded[slot], 16)

            def group(i, last):
                for k in range(last_k(last)):
                    load(i, k, AHEAD + PER * i + k)

            for k in range(-4, 0):
                load(0, k, AHEAD + k)
                if k == -3:
                    for q in range(4):
                        sp.dma_start(y[:, 4 * q:4 * q + 4, :], dram["x2"][q, :, :].rearrange("(r p) c -> p r c", p=P))\
                            .then_inc(y_loaded[q], 16)
            with sp.Fori(0, GROUPS - 1) as i:
                group(i, False)
            group(GROUPS - 1, True)
            for r in range(RT):
                sp.wait_ge(y_added, ND * (GROUPS - 1) + 2 * (r + 1))
                sp.dma_start(dram["out"][P * r:P * r + P, :], y[:, r, :]).then_inc(stored, 16)
            sp.wait_ge(stored, 16 * RT)

        @block.gpsimd
        def _(pool):
            nc.gpsimd.memset(ident[:, :], 0.0).then_inc(consts, 1)
            nc.gpsimd.memset(minus_half[:, :], -0.5).then_inc(consts, 1)
            pool.wait_ge(consts, 2)
            nc.gpsimd.affine_select(out=ident[:, :], in_=ident[:, :], compare_op=ALU.not_equal, fill=1.0, base=0,
                                    pattern=[[-1, P]], channel_multiplier=1).then_inc(consts, 1)

            def held(ge_sem, value):
                pool.wait_ge(ge_sem, value)
                pool.sem_inc(pool_tick, 1)

            def scale(i, k):
                t, w = AHEAD + PER * i + k, w32[:, k % 2, :]
                held(scales_loaded[k % 2], 32 * (PER // 2 * i + (AHEAD + k) // 2 + 1))
                held(lut, LUT * (t + 1))
                nc.gpsimd.tensor_tensor(w, w, scales[:, k % 2, :], ALU.mult).then_inc(scaled, 1)

            def cut_low(i, k):
                w_h, w_l = weights(*tile_of(k))
                held(w_high, AHEAD + PER * i + k + 1)
                nc.gpsimd.tensor_tensor(w_l, w32[:, k % 2, :], w_h, ALU.subtract).then_inc(w_low, 1)

            def group(i, last):
                for q, ks in enumerate(STEPS):
                    for n, k in enumerate(ks):
                        if n == 0 and q < NQ:
                            cols = slice(T * (q % NB), T * (q % NB) + T)
                            held(h_high, NQ * i + q + 1)
                            nc.gpsimd.tensor_tensor(hT_l[:, q // NB, cols], h32[:, q % 2, :],
                                                    hT_h[:, q // NB, cols], ALU.subtract).then_inc(h_low, 1)
                        if k < last_k(last):
                            scale(i, k)
                        for c in cut_with(k, last):
                            cut_low(i, c)

            pool.sem_inc(h_low, FREE)
            for k in range(-4, 0):
                scale(0, k)
                cut_low(0, k)
            for r in range(RT):
                pool.wait_ge(ln_stat, 4 * r + 4)
                nc.gpsimd.tensor_tensor(rstd[:, r % 2:r % 2 + 1], var_eps[:, r % 2:r % 2 + 1], minus_half[:, :],
                                        ALU.pow).then_inc(ln_rstd, 1)
            with pool.Fori(0, GROUPS - 1) as i:
                group(i, False)
            group(GROUPS - 1, True)

        @block.tensor
        def _(pe):
            def gate_up(i, chunk):
                pe.wait_ge(w_low, AHEAD + PER * i + 4 * chunk)
                for nb in range(NB):
                    n = NB * chunk + nb
                    cols = slice(T * nb, T * nb + T)
                    for kind in range(2):
                        if n >= 2:
                            pe.wait_ge((silu_done, h_done)[kind], NQ * i + n - 1)
                        for m in range(3 * CT):
                            c = m // 3
                            w, x = ((up_h, xT_h), (up_h, xT_l), (up_l, xT_h))[m % 3]
                            mm = nc.tensor.matmul(bank[(GATE, UP)[kind] + n % 2][:, :],
                                                  w[:, chunk, kind, P * c:P * c + P], x[:, c, cols],
                                                  start=(m == 0), stop=(m == 3 * CT - 1))
                        mm.then_inc((gate_done, up_done)[kind], 1)

            def down(i):
                pe.wait_ge(w_low, AHEAD + PER * i + 8)
                for d in range(ND):
                    r, half = d // 2, d % 2
                    if d % 8 == 0:
                        pe.wait_ge(h_low, FREE + NQ * i + NB + d // 8 + 1)
                    if d >= 4:
                        pe.wait_ge(y_added, ND * i + d - 3)
                    rows, cols = slice(P * r, P * r + P), slice(HALF * half, HALF * half + HALF)
                    for m in range(6):
                        h, w = ((hT_h, dn_h), (hT_h, dn_l), (hT_l, dn_h))[m % 3]
                        mm = nc.tensor.matmul(bank[DOWN + d % 4][:, :], h[:, m // 3, rows], w[:, m // 3, cols],
                                              start=(m == 0), stop=(m == 5))
                    mm.then_inc(down_done, 1)

            pe.wait_ge(consts, 3)
            for r in range(RT):
                pe.wait_ge(ln_xn, r + 1)
                for half in range(2):
                    if r:
                        pe.wait_ge(ln_low, 2 * r + half - 1)
                    for c in range(4):
                        mm = nc.tensor.transpose(bank[GATE + half][:, P * c:P * c + P],
                                                 xn[:, P * (4 * half + c):P * (4 * half + c + 1)], ident[:, :])
                    mm.then_inc(ln_turned, 1)
            pe.wait_ge(ln_low, 2 * RT)
            with pe.Fori(0, GROUPS) as i:
                gate_up(i, 0)
                gate_up(i, 1)
                down(i)

        @block.scalar
        def _(act):
            def draw_lines(i, k):
                t, slot = AHEAD + PER * i + k, k % 2
                act.wait_ge(codes_loaded[slot], 16 * (PER // 2 * i + (AHEAD + k) // 2 + 1))
                for m, (slope, intercept) in enumerate(LINES):
                    if k > -4:
                        act.wait_ge(lut, LUT * (t - 1) + USED_BY[m])
                    nc.scalar.activation(line[:, m, :], codes[:, slot, :], ACT.Copy, scale=slope, bias=intercept)\
                        .then_inc(lined, 1)

            def cut_high(i, k):
                act.wait_ge(scaled, AHEAD + PER * i + k + 1)
                nc.scalar.activation(weights(*tile_of(k))[0], w32[:, k % 2, :], ACT.Copy).then_inc(w_high, 1)

            def group(i, last):
                for q, ks in enumerate(STEPS):
                    if q < NQ:
                        act.wait_ge(gate_done, NQ * i + q + 1)
                        act.wait_ge(h_low, FREE + NQ * i + q - 1)
                        nc.scalar.activation(silu[:, q % 2, :], bank[GATE + q % 2][:, :], ACT.Silu,
                                             scale=1.0 / F_SCALE).then_inc(silu_done, 1)
                    for n, k in enumerate(ks):
                        if k + 1 < (last_k(last) if last else PER + 1):
                            draw_lines(i, k + 1)
                        if n == 0 and q < NQ:
                            act.wait_ge(h_done, NQ * i + q + 1)
                            nc.scalar.activation(hT_h[:, q // NB, T * (q % NB):T * (q % NB) + T], h32[:, q % 2, :],
                                                 ACT.Copy).then_inc(h_high, 1)
                        for c in cut_with(k, last):
                            cut_high(i, c)

            draw_lines(0, -4)
            for k in range(-4, 0):
                if k < -1:
                    draw_lines(0, k + 1)
                cut_high(0, k)
            for r in range(RT):
                for half in range(2):
                    act.wait_ge(ln_turned, 2 * r + half + 1)
                    nc.scalar.activation(xT_h[:, 4 * half:4 * half + 4, P * r:P * r + P],
                                         bank[GATE + half][:, :].rearrange("p (c n) -> p c n", n=P), ACT.Copy)\
                        .then_inc(ln_high, 1)
            draw_lines(0, 0)
            with act.Fori(0, GROUPS - 1) as i:
                group(i, False)
            group(GROUPS - 1, True)

        @block.vector
        def _(dve):
            def look_up(i, k, steps=range(LUT)):
                t = AHEAD + PER * i + k
                for n in steps:
                    if n in (0, 4):
                        dve.wait_ge(lined, NL * t + (6, NL)[n // 4])
                    if n >= 7:
                        dve.wait_ge(lut, LUT * t + n)
                    elif n >= 2:
                        dve.wait_ge(lut, LUT * t + n - 1)
                    w = w32[:, k % 2, :]
                    if n < 2:
                        op = nc.vector.scalar_tensor_tensor(line[:, 2 * n + 1, :], line[:, 2 * n, :], 0.0,
                                                            line[:, 2 * n + 1, :], *((ALU.max,) * 2, (ALU.min,) * 2)[n])
                    elif n < 7:
                        op = nc.vector.tensor_tensor(line[:, n + 2, :], line[:, (1, 3)[n - 2] if n < 4 else n, :],
                                                     line[:, n + 2, :], (ALU.max, ALU.min)[n % 2])
                    else:
                        if k >= -2:
                            dve.wait_ge(w_low, t - 1)
                        op = nc.vector.tensor_tensor(w, line[:, NL - 1, :], line[:, NL - 2, :], ALU.add)
                    op.then_inc(lut, 1)

            def group(i, last):
                for q, ks in enumerate(STEPS):
                    if q < NQ:
                        dve.wait_ge(silu_done, NQ * i + q + 1)
                        dve.wait_ge(up_done, NQ * i + q + 1)
                        nc.vector.scalar_tensor_tensor(h32[:, q % 2, :], bank[UP + q % 2][:, :], H_SCALE / F_SCALE,
                                                       silu[:, q % 2, :], ALU.mult, ALU.mult).then_inc(h_done, 1)
                        for k in ks:
                            if k < last_k(last):
                                look_up(i, k)
                        continue
                    for d in range(ND):
                        cols = y[:, d // 2, HALF * (d % 2):HALF * (d % 2) + HALF]
                        dve.wait_ge(down_done, ND * i + d + 1)
                        nc.vector.scalar_tensor_tensor(cols, bank[DOWN + d % 4][:, :], 1.0 / (H_SCALE * F_SCALE),
                                                       cols, ALU.mult, ALU.add).then_inc(y_added, 1)
                        if d < LUT * len(ks) and not last:
                            k = ks[d // LUT]
                            look_up(i, k, (d % LUT,))

            def ln_low_parts(r):
                for half in range(2):
                    dve.wait_ge(ln_high, 2 * r + half + 1)
                    cols = (slice(None), slice(4 * half, 4 * half + 4), slice(P * r, P * r + P))
                    nc.vector.tensor_tensor(xT_l[cols], bank[GATE + half][:, :].rearrange("p (c n) -> p c n", n=P),
                                            xT_h[cols], ALU.subtract).then_inc(ln_low, 1)

            for k in range(-4, 0):
                look_up(0, k)
            for r in range(RT + 1):
                if r < RT:
                    s = r % 2
                    if r % 4 == 0:
                        dve.wait_ge(y_loaded[r // 4], 16)
                    for half in range(2):
                        nc.vector.bn_stats(stats[:, s, half, :], y[:, r, HALF * half:HALF * half + HALF])\
                            .then_inc(ln_stat, 1)
                    dve.wait_ge(ln_stat, 4 * r + 2)
                    nc.vector.bn_aggr(mean_var[:, s, :], stats[:, s, :, :]).then_inc(ln_stat, 1)
                    dve.wait_ge(ln_stat, 4 * r + 3)
                    nc.vector.tensor_scalar(var_eps[:, s:s + 1], mean_var[:, s, 1:2], EPS, None, ALU.add)\
                        .then_inc(ln_stat, 1)
                    dve.wait_ge(ln_rstd, r + 1)
                    if r >= 1:
                        dve.wait_ge(ln_turned, 2 * r)
                    else:
                        dve.wait_ge(lut, LUT * AHEAD)
                    nc.vector.tensor_scalar(xn, y[:, r, :], mean_var[:, s, 0:1], rstd[:, s:s + 1],
                                            ALU.subtract, ALU.mult).then_inc(ln_xn, 1)
                if r >= 1:
                    ln_low_parts(r - 1)
            with dve.Fori(0, GROUPS - 1) as i:
                group(i, False)
            group(GROUPS - 1, True)


def decoder_layer(nc, dram):
    with ExitStack() as ctx:
        t = Attention(nc, ctx)
        attention(nc, t, dram)
    feed_forward(nc, dram)


def kernel(x, ctx_1024, mask_SxS2_ff0, L0_attn_Wq, L0_attn_bq, L0_attn_Wk, L0_attn_bk, L0_attn_Wv, L0_attn_bv,
           L0_ffn_gate_q, L0_ffn_gate_absmax, L0_ffn_up_q, L0_ffn_up_absmax, L0_ffn_down_q, L0_ffn_down_absmax):
    import concourse.bacc as bacc
    from concourse.bass_utils import run_bass_kernel_spmd

    def arr(a):
        return np.asarray(a)

    wk = arr(L0_attn_Wk).T.reshape(CT, P, UNITS, 1, P)
    wv = arr(L0_attn_Wv).T.reshape(CT, P, UNITS, 1, P)
    wq = arr(L0_attn_Wq).T.reshape(CT, P, 2, UNITS, P).transpose(0, 1, 3, 2, 4)
    w = np.concatenate([wk, wq, wv], axis=3).reshape(CT, P, 4 * HALF)
    bq = arr(L0_attn_bq).reshape(2, UNITS, P)
    bias_qk = np.stack([arr(L0_attn_bk).reshape(UNITS, P), bq[0], bq[1]], axis=2).transpose(1, 0, 2)
    ctx4 = arr(ctx_1024).reshape(B, TC, KVX, D)

    def gate_codes(q):
        return arr(q).reshape(MC, P, CT, P).transpose(0, 3, 2, 1).reshape(MC, P, C)

    def gate_scales(s):
        return arr(s).reshape(MC, P, CT, 2).transpose(0, 3, 2, 1).reshape(MC, 2, C)

    codes = np.stack([gate_codes(L0_ffn_gate_q), gate_codes(L0_ffn_up_q),
                      arr(L0_ffn_down_q).reshape(C, MC, P).transpose(1, 2, 0)], axis=1)
    scales = np.stack([gate_scales(L0_ffn_gate_absmax), gate_scales(L0_ffn_up_absmax),
                       arr(L0_ffn_down_absmax).reshape(C, MC, 2).transpose(1, 2, 0)], axis=1)
    arrays = {
        "x": arr(x),
        "w": w,
        "bias_qk": bias_qk,
        "bias_v": arr(L0_attn_bv).reshape(1, KV * D),
        "mask": arr(mask_SxS2_ff0),
        "ctx_kT": ctx4.transpose(0, 3, 2, 1).reshape(B, D, KVX * TC),
        "ctx_v": ctx4.reshape(B, TC, KVX * D),
        "codes": codes,
        "scales": scales,
    }
    arrays = {name: np.ascontiguousarray(a) for name, a in arrays.items()}
    nc = bacc.Bacc("TRN2", target_bir_lowering=False, num_devices=1)
    dram = {name: nc.dram_tensor("in_" + name, a.shape, mybir.dt.from_np(a.dtype), kind="ExternalInput").ap()
            for name, a in arrays.items()}
    dram["x2"] = nc.dram_tensor("x2", [B, T, C], FP32, kind="Internal").ap()
    dram["out"] = nc.dram_tensor("out", [B * T, C], FP32, kind="ExternalOutput").ap()
    decoder_layer(nc, dram)
    result = run_bass_kernel_spmd(nc, [{"in_" + name: a for name, a in arrays.items()}], core_ids=[0])
    return result.results[0]["out"].reshape(B, T, C)
```

```python
import math

import numpy as np

import concourse.bass as bass
from concourse import mybir
from contextlib import ExitStack

FP32 = mybir.dt.float32
FP16 = mybir.dt.float16
BF16 = mybir.dt.bfloat16
INT32 = mybir.dt.int32
ALU = mybir.AluOpType
ACT = mybir.ActivationFunctionType
AX_X = mybir.AxisListType.X

B, T, C = 4, 512, 1024
H, KV, D = 32, 16, 32
TC, KVX = 64, 8
M = 3584
P = 128
CT = C // P
QT = T // P
RT = B * QT
UNITS = KV // 4
PAIRS = 4
CHUNKS = 5
MC = M // P
GROUPS = MC // 2
HALF = 512
EPS = 1e-5

W_SCALE = 256.0
F_SCALE = 512.0
H_SCALE = 16.0
NEG = -1.0e30
SELF_SCALE = 1.0 / math.sqrt(H)
CROSS_SCALE = 1.0 / math.sqrt(D)

NF4 = [-1.0, -0.6961928009986877, -0.5250730514526367, -0.39491748809814453, -0.28444138169288635,
       -0.18477343022823334, -0.09105003625154495, 0.0, 0.07958029955625534, 0.16093020141124725,
       0.24611230194568634, 0.33791524171829224, 0.44070982933044434, 0.5626170039176941,
       0.7229568362236023, 1.0]


def code_line(lo, hi):
    slope = np.float32(F_SCALE * (NF4[hi] - NF4[lo]) / (hi - lo))
    return float(slope), float(np.float32(F_SCALE * NF4[lo] - float(slope) * lo))


LOWER_LINES = [code_line(5, 6), code_line(3, 4), code_line(1, 2), code_line(0, 1)]
UPPER_LINES = [code_line(7, 8), code_line(9, 10), code_line(11, 12), code_line(13, 14), code_line(14, 15)]
LINES = [UPPER_LINES[0], UPPER_LINES[1], LOWER_LINES[0], LOWER_LINES[1],
         UPPER_LINES[2], LOWER_LINES[2], UPPER_LINES[3], LOWER_LINES[3], UPPER_LINES[4]]
USED_BY = [1, 3, 2, 4, 5, 6, 7, 8, 8]
NL = len(LINES)
LUT = 8


class Attention:

    def __init__(self, nc, ctx):
        def sb(name, shape, dt):
            return ctx.enter_context(nc.sbuf_tensor(name, shape, dt))

        self.w_h = sb("w_h", [P, CT, 4 * HALF], FP16)
        self.w_l = sb("w_l", [P, CT, 4 * HALF], FP16)
        self.ident = sb("ident", [P, P], FP32)
        self.ident_b = sb("ident_b", [P, P], BF16)
        self.mask_qk = sb("mask_qk", [P, P], BF16)
        self.mask_kq = sb("mask_kq", [P, P], BF16)
        self.minus_half = sb("minus_half", [P, 1], FP32)
        self.bias_qk = sb("bias_qk", [P, UNITS, 3], FP32)
        self.bias_v = sb("bias_v", [P, KV * D], FP32)
        self.mask = sb("mask_x", [P, QT, TC], FP32)
        self.kx_h = sb("kx_h", [P, KVX, 4 * TC], FP16)
        self.kx_l = sb("kx_l", [P, KVX, 4 * TC], FP16)
        self.vx_h = sb("vx_h", [P, KVX, 2 * (D + 1)], FP16)
        self.vx_l = sb("vx_l", [P, KVX, 2 * (D + 1)], FP16)
        self.q_rows = sb("q_rows", [97, 2, 2 * PAIRS, T], FP16)
        self.k_rows = sb("k_rows", [97, 2, PAIRS, T], FP16)
        self.v_parts = sb("v_parts", [P, 2, QT, PAIRS, 2 * D + 1], FP16)


def attention(nc, t, dram):
    with ExitStack() as ctx:
        def sb(name, shape, dt):
            return ctx.enter_context(nc.sbuf_tensor(name, shape, dt))

        def sem(name):
            return ctx.enter_context(nc.semaphore(name))

        x_sb = sb("x_sb", [P, QT, C], FP32)
        xT_h = sb("xT_h", [P, CT, T], FP16)
        xT_l = sb("xT_l", [P, CT, T], FP16)
        x2T_h = sb("x2T_h", [P, 2, CT, P], FP16)
        x2T_l = sb("x2T_l", [P, 2, CT, P], FP16)
        stats = sb("stats", [P, 2, 2, 6], FP32)
        mean_var = sb("mean_var", [P, 2, 2], FP32)
        var_eps = sb("var_eps", [P, 2], FP32)
        rstd = sb("rstd", [P, 2], FP32)
        xn = sb("xn", [P, 2, C], FP32)
        proj32 = sb("proj32", [P, 2, HALF], FP32)
        nat_h = sb("nat_h", [P, 3, T], FP16)
        nat_l = sb("nat_l", [P, 3, T], FP16)
        v32 = sb("v32", [P, QT, PAIRS, D], FP32)
        block_max = sb("block_max", [P, PAIRS, CHUNKS, 4], FP32)
        row_max = sb("row_max", [P, PAIRS, 2, QT], FP32)
        neg_max = sb("neg_max", [PAIRS * QT, 2, P], FP16)
        p32 = sb("p32", [P, 4, HALF], FP32)
        p_h = sb("p_h", [P, 2, CHUNKS, HALF], FP16)
        p_l = sb("p_l", [P, 2, CHUNKS, HALF], FP16)
        r_sum = sb("r_sum", [P, 2, 2 * QT], FP32)
        o32 = sb("o32", [P, 2, QT, 2, D], FP32)
        k_raw = sb("k_raw", [P, KVX, TC], FP32)
        v_raw = sb("v_raw", [P, KVX, D], FP32)
        s_top = sb("s_top", [P, 2, 8], FP32)
        s32 = p32[:, 0:2, :].rearrange("p s (a t) -> p s a t", t=TC)
        e32 = p32[:, 2:4, :]
        px_h, px_l = p_h[:, 0, 0:2, :], p_l[:, 0, 0:2, :]
        w_raw = x_sb[:, :, :].rearrange("p s (c n) -> p s c n", c=2)
        bank = [ctx.enter_context(nc.psum_tensor(f"bank{i}", [P, HALF], FP32)) for i in range(8)]
        LN_BANK, PROJ_BANK, T_BANK, MAX_BANK, O_BANK = 0, 2, 4, 6, 7

        zeroed = sem("zeroed")
        selected = sem("selected")
        small_loaded = sem("small_loaded")
        w_loaded = [sem(f"w_loaded{i}") for i in range(QT)]
        w_high = sem("w_high")
        w_low = sem("w_low")
        row_loaded = [sem(f"row_loaded{i}") for i in range(2)]
        x_loaded = sem("x_loaded")
        ctx_loaded = sem("ctx_loaded")
        ctx_step = sem("ctx_step")
        ln_stat = sem("ln_stat")
        ln_rstd = sem("ln_rstd")
        ln_xn = sem("ln_xn")
        ln_turned = sem("ln_turned")
        ln_high = sem("ln_high")
        ln_low = sem("ln_low")
        proj_done = sem("proj_done")
        proj_out = sem("proj_out")
        proj_high = sem("proj_high")
        proj_low = sem("proj_low")
        rows_stacked = sem("rows_stacked")
        v_out = sem("v_out")
        v_high = sem("v_high")
        v_low = sem("v_low")
        scored = sem("scored")
        maxed = sem("maxed")
        rows_maxed = sem("rows_maxed")
        max_turned = sem("max_turned")
        max_out = sem("max_out")
        max_stacked = sem("max_stacked")
        t_scored = sem("t_scored")
        t_exp = sem("t_exp")
        p_high = sem("p_high")
        p_low = sem("p_low")
        p_low_v = sem("p_low_v")
        o_done = sem("o_done")
        o_recip = sem("o_recip")
        o_read = sem("o_read")
        o_added = sem("o_added")
        x_scored = sem("x_scored")
        x_masked = sem("x_masked")
        x_topped = sem("x_topped")
        x_shifted = sem("x_shifted")
        x_exp = sem("x_exp")
        x_turned = sem("x_turned")
        x_high = sem("x_high")
        x_low = sem("x_low")
        x_done = sem("x_done")
        x_recip = sem("x_recip")
        x_read = sem("x_read")
        x_added = sem("x_added")
        stored = sem("stored")
        dve_tick = sem("dve_tick")
        sp_tick = sem("sp_tick")
        pool_tick = sem("pool_tick")
        block = ctx.enter_context(nc.Block())

        STACKS = 3 * 3 * 4
        NP = UNITS * PAIRS
        NCH = NP * CHUNKS
        NX = QT * 4
        NW = UNITS * CT // 2
        LATE = NW - 4
        CUTS_BEFORE = (7, 9, 10)

        def ln_first(b, first):
            return 0 if first else 8 * b - 4

        def ln_cross(b, last):
            return 8 * b + (4 if last else 8)

        BY_VECTOR = (1, 3)

        def low_cut(b, n):
            pair, k = n // CHUNKS, n % CHUNKS
            by_vector = k in BY_VECTOR
            before = sum((kk in BY_VECTOR) == by_vector for kk in range(k + 1))
            each = len(BY_VECTOR) if by_vector else CHUNKS - len(BY_VECTOR)
            return (p_low_v if by_vector else p_low), each * (NP * b + pair) + before

        def score_parts(k):
            if k < 2:
                return [(0, k, 3, 512)]
            if k < 4:
                return [(0, k - 2, 0, 128), (128, k - 2, 2, 384)]
            return [(0, 0, 1, 256), (256, 1, 1, 256)]

        def t_parts(k):
            if k < 2:
                return [(0, k, 0)]
            if k < 4:
                return [(0, k - 2, 3), (128, k - 2, 1)]
            return [(0, 0, 2), (256, 1, 2)]

        def t_place(hh, kt, qt):
            if kt == 0:
                return hh, P * qt
            if kt == 1:
                return 2 + hh, P + P * (qt - 1)
            if kt == 2:
                return 4, 256 * hh + P * (qt - 2)
            return 2 + hh, 0

        @block.sync
        def _(sp):
            def held(ge_sem, value):
                sp.wait_ge(ge_sem, value)
                sp.sem_inc(sp_tick, 1)

            def load_row(b, i, at, first=False):
                src = dram["x"][bass.ds(b, 1), P * i:P * i + P, :].rearrange("b p c -> p (b c)")
                if not (first and i < 2):
                    held(ln_turned, 2 * at - 2)
                sp.dma_start(xn[:, i % 2, :], src).then_inc(row_loaded[i % 2], 16)

            def load_x(b, rt):
                src = dram["x"][bass.ds(b, 1), P * rt:P * rt + P, :].rearrange("b p c -> p (b c)")
                sp.dma_start(x_sb[:, rt, :], src).then_inc(x_loaded, 16)

            def load_w(n):
                g, c = n // 4, 2 * (n % 4)
                if n >= QT:
                    sp.wait_ge(w_low, n - QT + 1)
                sp.dma_start(w_raw[:, n % QT, :, :],
                             dram["w"][c:c + 2, :, HALF * g:HALF * g + HALF].rearrange("c p n -> p c n"))\
                    .then_inc(w_loaded[n % QT], 16)

            def stack_rows(b, g, kind):
                held(proj_low, 3 * (UNITS * b + g) + kind + 1)
                for j in range(4):
                    for r in range(3):
                        if kind == 0:
                            src = (nat_h, nat_h, nat_l)[r]
                            dst = t.k_rows[D * r:D * r + D, g % 2, j, :]
                        else:
                            src = (nat_h, nat_l, nat_h)[r]
                            dst = t.q_rows[D * r:D * r + D, g % 2, 2 * j + kind - 1, :]
                        sp.dma_start(dst, src[D * j:D * j + D, kind, :]).then_inc(rows_stacked, 16)

            def stack_max(b, g, half):
                held(max_out, 2 * (UNITS * b + g) + half + 1)
                sp.dma_start(t.q_rows[96:97, g % 2, PAIRS * half:PAIRS * (half + 1), :]
                             .rearrange("o s (q n) -> o (s q) n", n=P), neg_max[:, half, :])\
                    .then_inc(max_stacked, 16)

            def load_context(b):
                kT = dram["ctx_kT"][bass.ds(b, 1), :, :].rearrange("b d n -> d (b n)")
                v = dram["ctx_v"][bass.ds(b, 1), :, :].rearrange("b t n -> t (b n)")
                for r in range(4):
                    sp.dma_start(k_raw[D * r:D * r + D, :, :].rearrange("p g t -> p (g t)"), kT)\
                        .then_inc(ctx_loaded, 16)
                for j in range(2):
                    sp.dma_start(v_raw[TC * j:TC * j + TC, :, :].rearrange("p g d -> p (g d)"), v)\
                        .then_inc(ctx_loaded, 16)

            def store_x(b, rt):
                dst = dram["x2"][bass.ds(b, 1), P * rt:P * rt + P, :].rearrange("b p c -> p (b c)")
                held(x_added, NX * b + 4 * (rt + 1))
                sp.dma_start(dst, x_sb[:, rt, :]).then_inc(stored, 16)
                held(stored, 16 * (QT * b + rt + 1))

            def batch(b, last):
                for g in range(1, UNITS):
                    if g == UNITS - 1 and not last:
                        for i in range(2):
                            load_row(b + 1, i, ln_first(b + 1, False) + i)
                    stack_rows(b, g, 0)
                    stack_rows(b, g, 1)
                    stack_max(b, g - 1, 1)
                    stack_rows(b, g, 2)
                    stack_max(b, g, 0)
                if not last:
                    for i in range(2, 4):
                        load_row(b + 1, i, ln_first(b + 1, False) + i)
                stack_max(b, UNITS - 1, 1)
                for rt in range(QT):
                    if not last:
                        for kind in range(3 if rt == 0 else 0):
                            stack_rows(b + 1, 0, kind)
                        if rt == 1:
                            load_context(b + 1)
                        if rt == QT - 1:
                            stack_max(b + 1, 0, 0)
                    store_x(b, rt)
                    if not last:
                        load_x(b + 1, rt)

            sp.wait_ge(zeroed, 1)
            for i in range(2):
                load_row(0, i, i, True)
            for n in range(4):
                load_w(n)
                if n < 2:
                    load_row(0, 2 + n, 2 + n, True)
            sp.dma_start(t.bias_qk[:, :, :], dram["bias_qk"]).then_inc(small_loaded, 16)
            sp.dma_start(t.bias_v[:, :], dram["bias_v"].broadcast_to([P, KV * D])).then_inc(small_loaded, 16)
            sp.dma_start(t.mask[:, :, :], dram["mask"].rearrange("(r p) t -> p r t", p=P)).then_inc(small_loaded, 16)
            for n in range(4, LATE):
                load_w(n)
                if n == LATE - 2:
                    stack_rows(0, 0, 0)
            stack_rows(0, 0, 1)
            stack_rows(0, 0, 2)
            for n in range(LATE, NW):
                load_w(n)
            stack_max(0, 0, 0)
            load_context(0)
            held(w_low, NW)
            for rt in range(QT):
                load_x(0, rt)
            with sp.Fori(0, B - 1) as b:
                batch(b, False)
            batch(B - 1, True)

        @block.gpsimd
        def _(pool):
            def held(ge_sem, value):
                pool.wait_ge(ge_sem, value)
                pool.sem_inc(pool_tick, 1)

            def ln_root(at, s):
                held(ln_stat, 4 * at + 4)
                nc.gpsimd.tensor_tensor(rstd[:, s:s + 1], var_eps[:, s:s + 1], t.minus_half[:, :],
                                        ALU.pow).then_inc(ln_rstd, 1)

            def low_parts(b, n):
                held(p_high, NCH * b + n + 1)
                dst = (n // CHUNKS % 2, n % CHUNKS)
                nc.gpsimd.tensor_tensor(p_l[:, dst[0], dst[1], :], p32[:, n % 4, :], p_h[:, dst[0], dst[1], :],
                                        ALU.subtract).then_inc(p_low, 1)

            def add_pair(b, n):
                g, j = n // PAIRS, n % PAIRS
                if n == 0:
                    held(x_loaded, 16 * QT * (b + 1))
                held(o_read, NP * b + n + 1)
                cols = slice(D * (4 * g + j), D * (4 * g + j) + D)
                x = x_sb[:, :, :].rearrange("p q (two r) -> p q two r", two=2)[:, :, :, cols]
                nc.gpsimd.tensor_tensor(x, o32[:, n % 2, :, :, :], x, ALU.add).then_inc(o_added, 1)

            def shift(b, n):
                s = s32[:, n % 2, :, :]
                held(x_topped, NX * b + n + 1)
                nc.gpsimd.tensor_tensor(s, s, s_top[:, n % 2, :].unsqueeze(2).broadcast_to([P, 8, TC]), ALU.subtract)\
                    .then_inc(x_shifted, 1)

            def add_cross(b, n):
                held(x_read, NX * b + n + 1)
                cols = x_sb[:, n // 4, 8 * D * (n % 4):8 * D * (n % 4 + 1)]
                nc.gpsimd.tensor_tensor(cols, o32[:, n % 2, :, :, :].rearrange("p q a d -> p (q a d)"), cols, ALU.add)\
                    .then_inc(x_added, 1)

            def batch(b, last):
                for n in range(NP):
                    for k in range(CHUNKS):
                        if k not in BY_VECTOR:
                            low_parts(b, CHUNKS * n + k)
                    if not last:
                        for i in {PAIRS * (UNITS - 2) + 1: (0, 1), PAIRS * (UNITS - 1): (2,),
                                  PAIRS * (UNITS - 1) + 1: (3,)}.get(n, ()):
                            ln_root(ln_first(b + 1, False) + i, i % 2)
                    if n >= 1:
                        add_pair(b, n - 1)
                add_pair(b, NP - 1)
                ln_root(ln_cross(b, last), 0)
                ln_root(ln_cross(b, last) + 1, 1)
                for n in range(NX + 2):
                    if n in (2, 6):
                        ln_root(ln_cross(b, last) + 2 + n // 4, n // 4)
                    if n < NX:
                        shift(b, n)
                    if n >= 2:
                        add_cross(b, n - 2)

            nc.gpsimd.memset(t.minus_half[:], -0.5).then_inc(zeroed, 1)
            nc.gpsimd.memset(t.ident[:], 0.0).then_inc(zeroed, 1)
            pool.wait_ge(zeroed, 2)
            nc.gpsimd.affine_select(out=t.ident[:, :], in_=t.ident[:, :], compare_op=ALU.not_equal, fill=1.0, base=0,
                                    pattern=[[-1, P]], channel_multiplier=1).then_inc(selected, 1)
            for i in range(4):
                ln_root(i, i % 2)
            cleared = [t.ident_b, t.mask_qk, t.mask_kq, t.v_parts, t.kx_h, t.kx_l, t.vx_h, t.vx_l]
            for buf in cleared:
                nc.gpsimd.memset(buf[:], 0.0).then_inc(zeroed, 1)
            pool.wait_ge(zeroed, len(cleared) + 2)
            nc.gpsimd.affine_select(out=t.ident_b[:, :], in_=t.ident_b[:, :], compare_op=ALU.not_equal, fill=1.0,
                                    base=0, pattern=[[-1, P]], channel_multiplier=1).then_inc(selected, 1)
            nc.gpsimd.affine_select(out=t.mask_qk[:, :], in_=t.mask_qk[:, :], compare_op=ALU.is_ge, fill=NEG, base=0,
                                    pattern=[[-1, P]], channel_multiplier=1).then_inc(selected, 1)
            nc.gpsimd.affine_select(out=t.mask_kq[:, :], in_=t.mask_kq[:, :], compare_op=ALU.is_ge, fill=NEG, base=0,
                                    pattern=[[1, P]], channel_multiplier=-1).then_inc(selected, 1)
            nc.gpsimd.memset(t.v_parts[:, :, :, :, D:D + 1], 1.0).then_inc(selected, 1)
            pool.wait_ge(selected, 5)
            nc.gpsimd.memset(t.k_rows[96:97, :, :, :], 1.0).then_inc(selected, 1)
            for j in range(2):
                pool.wait_ge(selected, 6 + j)
                nc.gpsimd.memset(t.vx_h[TC * j:TC * j + TC, :, (D + 1) * j + D:(D + 1) * j + D + 1], 1.0)\
                    .then_inc(selected, 1)
            pool.wait_ge(selected, 8)
            with pool.Fori(0, B - 1) as b:
                batch(b, False)
            batch(B - 1, True)

        @block.tensor
        def _(pe):
            def ln_turn(at, i, first=False):
                pe.wait_ge(ln_xn, at + 1)
                for half in range(2):
                    if not (first and i == 0):
                        pe.wait_ge(ln_low, 2 * at + half - 1)
                    for c in range(4):
                        mm = nc.tensor.transpose(bank[LN_BANK + half][:, P * c:P * c + P],
                                                 xn[:, i % 2, P * (4 * half + c):P * (4 * half + c + 1)],
                                                 t.ident[:, :])
                    mm.then_inc(ln_turned, 1)

            def project(b, g, kind, pieces=range(4), first=False):
                dst = bank[PROJ_BANK + kind % 2]
                cols = slice(HALF * g + P * kind, HALF * g + P * kind + P)
                if 0 in pieces:
                    if kind == 0 and g == 0:
                        pe.wait_ge(ln_low, 2 * ln_first(b, first) + 8)
                    if kind == 0 and not first:
                        pe.wait_ge(proj_out, 3 * (UNITS * b + g))
                    if kind == 1 and not first:
                        pe.wait_ge(v_out, UNITS * b + g)
                    if kind >= 2:
                        pe.wait_ge(proj_out, 3 * (UNITS * b + g) + kind - 1)
                for piece in pieces:
                    if kind < 3:
                        for c in (2 * piece, 2 * piece + 1):
                            if first and kind == 0:
                                pe.wait_ge(w_low, piece + 1)
                            for m, (w, x) in enumerate(((t.w_h, xT_h), (t.w_h, xT_l), (t.w_l, xT_h))):
                                mm = nc.tensor.matmul(dst[:, :], w[:, c, cols], x[:, c, :],
                                                      start=(c == 0 and m == 0), stop=(c == CT - 1 and m == 2))
                    else:
                        rows = slice(P * piece, P * piece + P)
                        for c in range(CT):
                            for m, (w, x) in enumerate(((t.w_h, xT_h), (t.w_h, xT_l), (t.w_l, xT_h))):
                                mm = nc.tensor.matmul(dst[:, rows], x[:, c, rows], w[:, c, cols],
                                                      start=(c == 0 and m == 0), stop=(c == CT - 1 and m == 2))
                if 3 in pieces:
                    mm.then_inc(proj_done, 1)

            def score(b, n, banks=range(CHUNKS)):
                g, j = n // PAIRS, n % PAIRS
                if j == 0 and banks[0] == 0:
                    pe.wait_ge(rows_stacked, 16 * STACKS * (UNITS * b + g + 1))
                for k in banks:
                    m = CHUNKS * n + k
                    if m >= 2:
                        pe.wait_ge(maxed, NCH * b + m - 1)
                    for col, hh, qt, keys in score_parts(k):
                        nc.tensor.matmul(bank[LN_BANK + m % 2][:, col:col + keys],
                                         t.q_rows[0:96, g % 2, 2 * j + hh, P * qt:P * qt + P],
                                         t.k_rows[0:96, g % 2, j, 0:keys], start=True, stop=False)
                        mm = nc.tensor.matmul(bank[LN_BANK + m % 2][:, col + P * qt:col + P * qt + P],
                                              t.ident_b[:, :], t.mask_qk[:, :], start=False, stop=True)
                    mm.then_inc(scored, 1)

            def turn_max(b, g, half, at=MAX_BANK):
                pe.wait_ge(rows_maxed, 4 * (2 * (UNITS * b + g) + half + 1))
                nc.tensor.transpose(bank[at][0:PAIRS * QT, P * half:P * half + P],
                                    row_max[:, 2 * half:2 * half + 2, :, :].rearrange("p j a q -> p (j a q)"),
                                    t.ident[:, :]).then_inc(max_turned, 1)

            def t_score(b, n, banks):
                g, j = n // PAIRS, n % PAIRS
                if j % 2 == 0 and banks[0] == 0:
                    pe.wait_ge(max_stacked, 16 * (2 * (UNITS * b + g) + j // 2 + 1))
                for k in banks:
                    m = CHUNKS * n + k
                    if m >= 2:
                        pe.wait_ge(t_exp, NCH * b + m - 1)
                    for col, hh, kt in t_parts(k):
                        nc.tensor.matmul(bank[T_BANK + m % 2][:, col:col + T - P * kt],
                                         t.k_rows[0:97, g % 2, j, P * kt:P * kt + P],
                                         t.q_rows[0:97, g % 2, 2 * j + hh, P * kt:T], start=True, stop=False)
                        mm = nc.tensor.matmul(bank[T_BANK + m % 2][:, col:col + P],
                                              t.ident_b[:, :], t.mask_kq[:, :], start=False, stop=True)
                    mm.then_inc(t_scored, 1)

            def weigh(b, n):
                g, j = n // PAIRS, n % PAIRS
                if j == 0:
                    pe.wait_ge(v_low, UNITS * b + g + 1)
                for k in (CHUNKS - 2, CHUNKS - 1):
                    pe.wait_ge(*low_cut(b, CHUNKS * n + k))
                if n >= 1:
                    pe.wait_ge(o_read, NP * b + n)
                for qt in range(QT):
                    for hh in range(2):
                        col = (D + 1) * (2 * qt + hh)
                        for kt in range(qt + 1):
                            k, at = t_place(hh, kt, qt)
                            high = p_h[:, n % 2, k, at:at + P]
                            low = p_l[:, n % 2, k, at:at + P]
                            v = t.v_parts[:, g % 2, kt, j, :]
                            out = bank[O_BANK]
                            nc.tensor.matmul(out[:, col:col + D + 1], high, v[:, 0:D + 1],
                                             start=(kt == 0), stop=False)
                            nc.tensor.matmul(out[:, col:col + D], high, v[:, D + 1:2 * D + 1],
                                             start=False, stop=False)
                            mm = nc.tensor.matmul(out[:, col:col + D + 1], low, v[:, 0:D + 1],
                                                  start=False, stop=(kt == qt))
                mm.then_inc(o_done, 1)

            def x_score(b, n, last):
                rt = n // 4
                if n % 4 == 0:
                    pe.wait_ge(ln_low, 2 * (ln_cross(b, last) + rt + 1))
                if n == 0:
                    pe.wait_ge(ctx_step, 13 * (b + 1))
                if n >= 2:
                    pe.wait_ge(x_masked, NX * b + n - 1)
                for part in range(2):
                    g = 2 * (n % 4) + part
                    for i, (x, k) in enumerate(((x2T_h, t.kx_h), (x2T_l, t.kx_h), (x2T_h, t.kx_l))):
                        mm = nc.tensor.matmul(bank[T_BANK + n % 2][:, 256 * part:256 * part + 256],
                                              x[:, rt % 2, g, :], k[:, g, :], start=(i == 0), stop=(i == 2))
                mm.then_inc(x_scored, 1)

            def x_weigh(b, n):
                pe.wait_ge(x_low, NX * b + n + 1)
                if n >= 1:
                    pe.wait_ge(x_read, NX * b + n)
                W = 2 * (D + 1)
                for i in range(4):
                    g = 2 * (n % 4) + i // 2
                    for m, (p, v) in enumerate(((px_h, t.vx_h), (px_h, t.vx_l), (px_l, t.vx_h))):
                        mm = nc.tensor.matmul(bank[O_BANK][:, W * i:W * i + W], p[:, n % 2, P * i:P * i + P],
                                              v[:, g, :], start=(m == 0), stop=(m == 2))
                mm.then_inc(x_done, 1)

            def x_turn(b, n):
                pe.wait_ge(x_exp, NX * b + n + 1)
                for i in range(4):
                    mm = nc.tensor.transpose(bank[MAX_BANK][:, P * i:P * i + P], e32[:, n % 2, P * i:P * i + P],
                                             t.ident[:, :])
                mm.then_inc(x_turned, 1)

            def unit(b, g, last):
                n, nn = PAIRS * g, PAIRS * (g + 1)
                more = g + 1 < UNITS
                turns = not more and not last
                at = ln_first(b + 1, False)
                if turns:
                    ln_turn(at, 0)
                    ln_turn(at + 1, 1)
                if more and g > 0:
                    project(b, g + 1, 0)
                for j in range(2):
                    for k in range(CHUNKS):
                        t_score(b, n + j, (k,))
                        if turns and j == 0 and k == 0:
                            pe.wait_ge(ln_low, 2 * at + 4)
                        score(b, n + 2 + j, (k,))
                        if more and k < 4:
                            project(b, g + 1, 1 + j, (k,))
                weigh(b, n)
                turn_max(b, g, 1)
                if turns:
                    ln_turn(at + 2, 2)
                if more:
                    project(b, g + 1, 3, (0, 1))
                for k in range(CHUNKS):
                    t_score(b, n + 2, (k,))
                    if more and 1 <= k < 3:
                        project(b, g + 1, 3, (k + 1,))
                weigh(b, n + 1)
                if turns:
                    ln_turn(at + 3, 3)
                for k in range(CHUNKS + 2):
                    if k < CHUNKS:
                        t_score(b, n + 3, (k,))
                    if k >= 2 and more:
                        score(b, nn, (k - 2,))
                weigh(b, n + 2)
                if more:
                    score(b, nn + 1)
                weigh(b, n + 3)
                if more:
                    turn_max(b, g + 1, 0)

            def tail(b, last):
                at = ln_cross(b, last)
                if not last:
                    project(b + 1, 0, 0)
                ln_turn(at, 0)
                ln_turn(at + 1, 1)
                for n in range(NX + 2):
                    if n in (3, 7):
                        ln_turn(at + 2 + n // 4, n // 4)
                    if n < NX:
                        x_score(b, n, last)
                        if n < 6 and not last:
                            project(b + 1, 0, 1 + n // 2, (2 * (n % 2), 2 * (n % 2) + 1))
                    if n >= NX - 2 and not last:
                        project(b + 1, 1, 0, (n - NX + 2,))
                    if n >= 2:
                        x_weigh(b, n - 2)
                    if 1 <= n <= NX:
                        x_turn(b, n - 1)
                    if 9 <= n < 14 and not last:
                        for m in (2 * (n - 9), 2 * (n - 9) + 1):
                            score(b + 1, m // CHUNKS, (m % CHUNKS,))
                    if n == NX and not last:
                        turn_max(b + 1, 0, 0, LN_BANK)

            pe.wait_ge(selected, 1)
            for i in range(4):
                ln_turn(i, i, True)
            for kind in range(4):
                project(0, 0, kind, first=True)
            pe.wait_ge(selected, 8)
            for j in range(2):
                score(0, j)
            turn_max(0, 0, 0)
            pe.wait_ge(w_low, LATE)
            project(0, 1, 0)
            pe.wait_ge(w_low, NW)
            with pe.Fori(0, B - 1) as b:
                for g in range(UNITS):
                    unit(b, g, False)
                tail(b, False)
            for g in range(UNITS):
                unit(B - 1, g, True)
            tail(B - 1, True)

        @block.scalar
        def _(act):
            def cut_w(n):
                act.wait_ge(w_loaded[n % QT], 16 * (n // QT + 1))
                g, c = n // 4, 2 * (n % 4)
                nc.scalar.activation(t.w_h[:, c:c + 2, HALF * g:HALF * g + HALF], w_raw[:, n % QT, :, :], ACT.Copy,
                                     scale=W_SCALE).then_inc(w_high, 1)

            def ln_high_parts(at, dst):
                for half in range(2):
                    act.wait_ge(ln_turned, 2 * at + half + 1)
                    nc.scalar.activation(dst[:, 4 * half:4 * half + 4, :],
                                         bank[LN_BANK + half][:, :].rearrange("p (c n) -> p c n", n=P), ACT.Copy)\
                        .then_inc(ln_high, 1)

            def first_high(b, i):
                ln_high_parts(ln_first(b, False) + i, xT_h[:, :, P * i:P * i + P])

            def proj_parts(b, g, kind, first=False):
                n = 3 * (UNITS * b + g) + kind
                slot = (3 * g + kind) % 2
                act.wait_ge(proj_done, 4 * (UNITS * b + g) + kind + 1)
                if not (first and kind < 2):
                    act.wait_ge(proj_low, n - 1)
                nc.scalar.activation(proj32[:, slot, :], bank[PROJ_BANK + kind % 2][:, :], ACT.Identity,
                                     bias=t.bias_qk[:, g, kind:kind + 1], scale=1.0 / W_SCALE)\
                    .then_inc(proj_out, 1)
                act.wait_ge(proj_out, n + 1)
                if kind == 0 and not first:
                    act.wait_ge(rows_stacked, 16 * STACKS * (UNITS * b + g))
                nc.scalar.activation(nat_h[:, kind, :], proj32[:, slot, :], ACT.Copy).then_inc(proj_high, 1)

            def v_parts(b, g):
                act.wait_ge(v_out, UNITS * b + g + 1)
                nc.scalar.activation(t.v_parts[:, g % 2, :, :, 0:D], v32[:, :, :, :], ACT.Copy).then_inc(v_high, 1)

            def max_rows(b, g, half, first=False, at=MAX_BANK):
                n = 2 * (UNITS * b + g) + half
                act.wait_ge(max_turned, n + 1)
                if not first:
                    act.wait_ge(max_stacked, 16 * (n - 1))
                nc.scalar.activation(neg_max[:, half, :],
                                     bank[at][0:PAIRS * QT, P * half:P * half + P],
                                     ACT.Copy, scale=-1.0).then_inc(max_out, 1)

            def exps(b, n):
                act.wait_ge(t_scored, NCH * b + n + 1)
                if n >= 4:
                    act.wait_ge(*low_cut(b, n - 4))
                nc.scalar.activation(p32[:, n % 4, :], bank[T_BANK + n % 2][:, :], ACT.Exp, scale=SELF_SCALE)\
                    .then_inc(t_exp, 1)

            def high_parts(b, n):
                act.wait_ge(t_exp, NCH * b + n + 1)
                if n % CHUNKS == 0 and n >= 2 * CHUNKS:
                    act.wait_ge(o_done, NP * b + n // CHUNKS - 1)
                nc.scalar.activation(p_h[:, n // CHUNKS % 2, n % CHUNKS, :], p32[:, n % 4, :], ACT.Copy)\
                    .then_inc(p_high, 1)

            def x_exps(b, n):
                act.wait_ge(x_shifted, NX * b + n + 1)
                if n >= 2:
                    act.wait_ge(x_turned, NX * b + n - 1)
                nc.scalar.activation(e32[:, n % 2, :], s32[:, n % 2, :, :].rearrange("p a t -> p (a t)"), ACT.Exp)\
                    .then_inc(x_exp, 1)

            def x_high_parts(b, n):
                act.wait_ge(x_turned, NX * b + n + 1)
                if n >= 2:
                    act.wait_ge(x_done, NX * b + n - 1)
                nc.scalar.activation(px_h[:, n % 2, :], bank[MAX_BANK][:, :], ACT.Copy).then_inc(x_high, 1)

            def unit(b, g, last):
                more = g + 1 < UNITS
                turns = not more and not last
                for j in range(PAIRS):
                    if more and j < 3:
                        proj_parts(b, g + 1, j)
                    if j == 2:
                        max_rows(b, g, 1)
                    if turns and j != 1:
                        for i in {0: (0, 1), 2: (2,), 3: (3,)}[j]:
                            first_high(b + 1, i)
                    first = CHUNKS * (PAIRS * g + j)
                    for n in range(first, first + CHUNKS):
                        exps(b, n)
                        if n > first:
                            high_parts(b, n - 1)
                    high_parts(b, first + CHUNKS - 1)
                    if more and j == 3:
                        v_parts(b, g + 1)
                if more:
                    max_rows(b, g + 1, 0)

            def tail(b, last):
                at = ln_cross(b, last)
                ln_high_parts(at, x2T_h[:, 0, :, :])
                ln_high_parts(at + 1, x2T_h[:, 1, :, :])
                for n in range(NX + 1):
                    if n >= 1:
                        x_high_parts(b, n - 1)
                    if n < NX:
                        x_exps(b, n)
                    if n in (3, 7):
                        act.wait_ge(x_scored, NX * b + n + 1)
                        ln_high_parts(at + 2 + n // 4, x2T_h[:, n // 4, :, :])
                    if n in (0, 2, 4) and not last:
                        proj_parts(b + 1, 0, n // 2)
                    if n == 8 and not last:
                        v_parts(b + 1, 0)
                if not last:
                    max_rows(b + 1, 0, 0, at=LN_BANK)

            for i in range(4):
                cut_w(i)
                ln_high_parts(i, xT_h[:, :, P * i:P * i + P])
            act.wait_ge(small_loaded, 48)
            for n in range(4, LATE):
                if n in CUTS_BEFORE:
                    proj_parts(0, 0, CUTS_BEFORE.index(n), True)
                cut_w(n)
            act.wait_ge(selected, 8)
            v_parts(0, 0)
            max_rows(0, 0, 0, True)
            for n in range(LATE, NW):
                cut_w(n)
            with act.Fori(0, B - 1) as b:
                for g in range(UNITS):
                    unit(b, g, False)
                tail(b, False)
            for g in range(UNITS):
                unit(B - 1, g, True)
            tail(B - 1, True)

        @block.vector
        def _(dve):
            def cut_w(n):
                g, c = n // 4, 2 * (n % 4)
                cols = (slice(None), slice(c, c + 2), slice(HALF * g, HALF * g + HALF))
                dve.wait_ge(w_high, n + 1)
                nc.vector.scalar_tensor_tensor(t.w_l[cols], w_raw[:, n % QT, :, :], W_SCALE, t.w_h[cols],
                                               ALU.mult, ALU.subtract).then_inc(w_low, 1)

            def lay_context(b):
                dve.wait_ge(ctx_loaded, 16 * 6 * (b + 1))
                base = 13 * b
                nc.vector.tensor_scalar(k_raw[:, :, :], k_raw[:, :, :], CROSS_SCALE, None, ALU.mult)\
                    .then_inc(ctx_step, 1)
                dve.wait_ge(ctx_step, base + 1)
                for r in range(4):
                    rows, cols = slice(D * r, D * r + D), slice(TC * r, TC * r + TC)
                    nc.vector.tensor_copy(t.kx_h[rows, :, cols], k_raw[rows, :, :]).then_inc(ctx_step, 1)
                for j in range(2):
                    rows, cols = slice(TC * j, TC * j + TC), slice((D + 1) * j, (D + 1) * j + D)
                    nc.vector.tensor_copy(t.vx_h[rows, :, cols], v_raw[rows, :, :]).then_inc(ctx_step, 1)
                dve.wait_ge(ctx_step, base + 7)
                for r in range(4):
                    rows, cols = slice(D * r, D * r + D), slice(TC * r, TC * r + TC)
                    nc.vector.tensor_tensor(t.kx_l[rows, :, cols], k_raw[rows, :, :], t.kx_h[rows, :, cols],
                                            ALU.subtract).then_inc(ctx_step, 1)
                for j in range(2):
                    rows, cols = slice(TC * j, TC * j + TC), slice((D + 1) * j, (D + 1) * j + D)
                    nc.vector.tensor_tensor(t.vx_l[rows, :, cols], v_raw[rows, :, :], t.vx_h[rows, :, cols],
                                            ALU.subtract).then_inc(ctx_step, 1)

            def ln_stats(at, s, row):
                for half in range(2):
                    nc.vector.bn_stats(stats[:, s, half, :], row[:, HALF * half:HALF * half + HALF])\
                        .then_inc(ln_stat, 1)
                dve.wait_ge(ln_stat, 4 * at + 2)
                dve.sem_inc(dve_tick, 1)
                nc.vector.bn_aggr(mean_var[:, s, :], stats[:, s, :, :]).then_inc(ln_stat, 1)
                dve.wait_ge(ln_stat, 4 * at + 3)
                nc.vector.tensor_scalar(var_eps[:, s:s + 1], mean_var[:, s, 1:2], EPS, None, ALU.add)\
                    .then_inc(ln_stat, 1)

            def ln_normal(at, s, row):
                dve.wait_ge(ln_rstd, at + 1)
                nc.vector.tensor_scalar(xn[:, s, :], row, mean_var[:, s, 0:1], rstd[:, s:s + 1],
                                        ALU.subtract, ALU.mult).then_inc(ln_xn, 1)

            def ln_low_parts(at, dst_h, dst_l):
                for half in range(2):
                    dve.wait_ge(ln_high, 2 * at + half + 1)
                    cols = (slice(None), slice(4 * half, 4 * half + 4), slice(None))
                    nc.vector.tensor_tensor(dst_l[cols], bank[LN_BANK + half][:, :].rearrange("p (c n) -> p c n", n=P),
                                            dst_h[cols], ALU.subtract).then_inc(ln_low, 1)

            def first_stats(b, i, first=False):
                dve.wait_ge(row_loaded[i % 2], 16 * (2 * b + i // 2 + 1))
                ln_stats(ln_first(b, first) + i, i % 2, xn[:, i % 2, :])

            def first_normal(b, i, first=False):
                ln_normal(ln_first(b, first) + i, i % 2, xn[:, i % 2, :])

            def first_low(b, i, first=False):
                cols = slice(P * i, P * i + P)
                ln_low_parts(ln_first(b, first) + i, xT_h[:, :, cols], xT_l[:, :, cols])

            def cross_normal(b, i, last):
                at = ln_cross(b, last) + i
                ln_stats(at, i % 2, x_sb[:, i, :])
                dve.wait_ge(ln_turned, 2 * at - 2)
                ln_normal(at, i % 2, x_sb[:, i, :])

            def cross_low(b, i, last):
                ln_low_parts(ln_cross(b, last) + i, x2T_h[:, i % 2, :, :], x2T_l[:, i % 2, :, :])

            def proj_low_parts(b, g, kind):
                dve.wait_ge(proj_high, 3 * (UNITS * b + g) + kind + 1)
                nc.vector.tensor_tensor(nat_l[:, kind, :], proj32[:, (3 * g + kind) % 2, :], nat_h[:, kind, :],
                                        ALU.subtract).then_inc(proj_low, 1)

            def v_biased(b, g):
                dve.wait_ge(proj_done, 4 * (UNITS * b + g + 1))
                bias = t.bias_v[:, P * g:P * g + P].unsqueeze(1).broadcast_to([P, QT, P])
                nc.vector.scalar_tensor_tensor(v32[:, :, :, :].rearrange("p q j d -> p q (j d)"),
                                               bank[PROJ_BANK + 1][:, :]
                                               .rearrange("p (q n) -> p q n", n=P),
                                               1.0 / W_SCALE, bias, ALU.mult, ALU.add).then_inc(v_out, 1)

            def v_low_parts(b, g):
                dve.wait_ge(v_high, UNITS * b + g + 1)
                nc.vector.tensor_tensor(t.v_parts[:, g % 2, :, :, D + 1:2 * D + 1], v32[:, :, :, :],
                                        t.v_parts[:, g % 2, :, :, 0:D], ALU.subtract).then_inc(v_low, 1)

            def low_parts(b, n, banks=BY_VECTOR):
                for k in banks:
                    m = CHUNKS * n + k
                    dve.wait_ge(p_high, NCH * b + m + 1)
                    nc.vector.tensor_tensor(p_l[:, n % 2, k, :], p32[:, m % 4, :], p_h[:, n % 2, k, :],
                                            ALU.subtract).then_inc(p_low_v, 1)

            def maxima(b, n, banks=range(CHUNKS)):
                for k in banks:
                    m = CHUNKS * n + k
                    dve.wait_ge(scored, NCH * b + m + 1)
                    nc.vector.reduce_max(block_max[:, n % PAIRS, k, :],
                                         bank[LN_BANK + m % 2][:, :].rearrange("p (a n) -> p a n", n=P), AX_X)\
                        .then_inc(maxed, 1)

            def row_maxima(b, g, half):
                dve.wait_ge(maxed, NCH * b + CHUNKS * (PAIRS * g + 2 * half + 2))
                rows, blocks = row_max[:, 2 * half:2 * half + 2, :, :], block_max[:, 2 * half:2 * half + 2, :, :]
                nc.vector.reduce_max(rows[:, :, :, 3], blocks[:, :, 0:2, :], AX_X).then_inc(rows_maxed, 1)
                nc.vector.reduce_max(rows[:, :, :, 2], blocks[:, :, 2:4, 1:4], AX_X).then_inc(rows_maxed, 1)
                nc.vector.tensor_copy(rows[:, :, :, 0], blocks[:, :, 2:4, 0]).then_inc(rows_maxed, 1)
                nc.vector.reduce_max(rows[:, :, :, 1],
                                     blocks[:, :, 4, :].rearrange("p j (a n) -> p j a n", n=2), AX_X)\
                    .then_inc(rows_maxed, 1)

            def pair_out(b, n):
                dve.wait_ge(o_done, NP * b + n + 1)
                out = bank[O_BANK][:, 0:(D + 1) * 2 * QT].rearrange("p (s d) -> p s d", d=D + 1)
                nc.vector.reciprocal(r_sum[:, n % 2, :], out[:, :, D]).then_inc(o_recip, 1)
                dve.wait_ge(o_recip, NP * b + n + 1)
                if n >= 2:
                    dve.wait_ge(o_added, NP * b + n - 1)
                nc.vector.tensor_tensor(o32[:, n % 2, :, :, :].rearrange("p q a d -> p (q a) d"), out[:, :, 0:D],
                                        r_sum[:, n % 2, :].unsqueeze(2).broadcast_to([P, 2 * QT, D]), ALU.mult)\
                    .then_inc(o_read, 1)

            def x_soft(b, n):
                s = s32[:, n % 2, :, :]
                dve.wait_ge(x_scored, NX * b + n + 1)
                if n >= 2:
                    dve.wait_ge(x_exp, NX * b + n - 1)
                nc.vector.tensor_tensor(s, bank[T_BANK + n % 2][:, :].rearrange("p (a t) -> p a t", t=TC),
                                        t.mask[:, n // 4, :].unsqueeze(1).broadcast_to([P, 8, TC]), ALU.add)\
                    .then_inc(x_masked, 1)
                dve.wait_ge(x_masked, NX * b + n + 1)
                nc.vector.reduce_max(s_top[:, n % 2, :], s, AX_X).then_inc(x_topped, 1)

            def x_low_parts(b, n):
                dve.wait_ge(x_high, NX * b + n + 1)
                nc.vector.tensor_tensor(px_l[:, n % 2, :], bank[MAX_BANK][:, :], px_h[:, n % 2, :],
                                        ALU.subtract).then_inc(x_low, 1)

            def x_out(b, n):
                dve.wait_ge(x_done, NX * b + n + 1)
                out = bank[O_BANK][:, 0:(D + 1) * 8].rearrange("p (s d) -> p s d", d=D + 1)
                nc.vector.reciprocal(r_sum[:, n % 2, :], out[:, :, D]).then_inc(x_recip, 1)
                dve.wait_ge(x_recip, NX * b + n + 1)
                if n >= 2:
                    dve.wait_ge(x_added, NX * b + n - 1)
                nc.vector.tensor_tensor(o32[:, n % 2, :, :, :].rearrange("p q a d -> p (q a) d"), out[:, :, 0:D],
                                        r_sum[:, n % 2, :].unsqueeze(2).broadcast_to([P, 8, D]), ALU.mult)\
                    .then_inc(x_read, 1)

            def unit(b, g, last):
                n, nn = PAIRS * g, PAIRS * (g + 1)
                if g == 1:
                    lay_context(b)
                more = g + 1 < UNITS
                turns = not more and not last
                early = g == UNITS - 2 and not last
                if turns:
                    first_low(b + 1, 0)
                    first_low(b + 1, 1)
                for j in range(2):
                    if more:
                        proj_low_parts(b, g + 1, j)
                    maxima(b, n + 2 + j, (0, 1, 2))
                    low_parts(b, n + j, (1,))
                    maxima(b, n + 2 + j, (3, 4))
                    low_parts(b, n + j, (3,))
                    if turns:
                        first_stats(b + 1, 2 + j)
                    if early:
                        first_stats(b + 1, j)
                row_maxima(b, g, 1)
                if turns:
                    first_normal(b + 1, 2)
                    first_normal(b + 1, 3)
                pair_out(b, n)
                if more:
                    proj_low_parts(b, g + 1, 2)
                if early:
                    first_normal(b + 1, 0)
                    first_normal(b + 1, 1)
                low_parts(b, n + 2)
                if more:
                    v_biased(b, g + 1)
                if turns:
                    first_low(b + 1, 2)
                pair_out(b, n + 1)
                if more:
                    maxima(b, nn, (0, 1))
                low_parts(b, n + 3, (1,))
                if more:
                    maxima(b, nn, (2, 3, 4))
                low_parts(b, n + 3, (3,))
                if turns:
                    first_low(b + 1, 3)
                pair_out(b, n + 2)
                if more:
                    maxima(b, nn + 1)
                    row_maxima(b, g + 1, 0)
                pair_out(b, n + 3)
                if more:
                    v_low_parts(b, g + 1)

            def tail(b, last):
                dve.wait_ge(o_added, NP * (b + 1))
                cross_normal(b, 0, last)
                cross_normal(b, 1, last)
                cross_low(b, 0, last)
                cross_low(b, 1, last)
                for n in range(NX + 2):
                    if n in (2, 6):
                        cross_normal(b, 2 + n // 4, last)
                    if n < NX:
                        x_soft(b, n)
                    if 1 <= n <= NX:
                        x_low_parts(b, n - 1)
                    if n >= 2:
                        x_out(b, n - 2)
                    if n in (3, 7):
                        cross_low(b, 2 + n // 4, last)
                    if n in (0, 2, 4) and not last:
                        proj_low_parts(b + 1, 0, n // 2)
                    if n == 8 and not last:
                        v_biased(b + 1, 0)
                        v_low_parts(b + 1, 0)
                    if 9 <= n < 14 and not last:
                        for m in (2 * (n - 9), 2 * (n - 9) + 1):
                            maxima(b + 1, m // CHUNKS, (m % CHUNKS,))
                    if n == 14 and not last:
                        row_maxima(b + 1, 0, 0)

            for i in range(4):
                first_stats(0, i, True)
                first_normal(0, i, True)
                if i:
                    cut_w(i - 1)
                    first_low(0, i - 1, True)
            cut_w(3)
            first_low(0, 3, True)
            for n in range(4, LATE):
                if n in CUTS_BEFORE:
                    proj_low_parts(0, 0, CUTS_BEFORE.index(n))
                cut_w(n)
            dve.wait_ge(small_loaded, 48)
            v_biased(0, 0)
            v_low_parts(0, 0)
            for j in range(2):
                maxima(0, j)
            row_maxima(0, 0, 0)
            for n in range(LATE, NW):
                cut_w(n)
            dve.wait_ge(selected, 8)
            with dve.Fori(0, B - 1) as b:
                for g in range(UNITS):
                    unit(b, g, False)
                tail(b, False)
            for g in range(UNITS):
                unit(B - 1, g, True)
            tail(B - 1, True)


def feed_forward(nc, dram):
    with ExitStack() as ctx:
        def sb(name, shape, dt):
            return ctx.enter_context(nc.sbuf_tensor(name, shape, dt))

        def sem(name):
            return ctx.enter_context(nc.semaphore(name))

        SLOTS = 4
        LEAD = 3
        y = sb("y", [P, RT, C], FP32)
        xT_h = sb("fT_h", [P, CT, B * T], FP16)
        xT_l = sb("fT_l", [P, CT, B * T], FP16)
        hT_h = sb("hT_h", [P, 2, B * T], FP16)
        hT_l = sb("hT_l", [P, 2, B * T], FP16)
        up_h = sb("up_h", [P, 2, 2, C], FP16)
        up_l = sb("up_l", [P, 2, 2, C], FP16)
        dn_h = sb("dn_h", [P, 2, C], FP16)
        dn_l = sb("dn_l", [P, 2, C], FP16)
        codes = sb("codes", [P, 2, HALF], INT32)
        scales = sb("scales", [P, 2, HALF], FP32)
        line = sb("line", [P, NL, HALF], FP32)
        w32 = sb("w32", [P, 2, HALF], FP32)
        h32 = sb("h32", [P, 2, HALF], FP32)
        xn = sb("f_xn", [P, 2, HALF], FP32)
        ident = sb("f_ident", [P, P], FP32)
        minus_half = sb("f_minus_half", [P, 1], FP32)
        stats = sb("f_stats", [P, SLOTS, 2, 6], FP32)
        mean_var = sb("f_mean_var", [P, SLOTS, 2], FP32)
        var_eps = sb("f_var_eps", [P, SLOTS], FP32)
        rstd = sb("f_rstd", [P, SLOTS], FP32)
        neg_mean = sb("f_neg_mean", [P, SLOTS], FP32)
        shift = sb("f_shift", [P, SLOTS], FP32)
        zero = sb("f_zero", [P, 1], FP32)
        bank = [ctx.enter_context(nc.psum_tensor(f"f_bank{i}", [P, HALF], FP32)) for i in range(8)]
        GATE, UP, DOWN = 0, 2, 4

        y_loaded = [sem(f"y_loaded{i}") for i in range(4)]
        consts = sem("consts")
        ln_stat = sem("f_ln_stat")
        ln_rstd = sem("f_ln_rstd")
        ln_xn = sem("f_ln_xn")
        ln_turned = sem("f_ln_turned")
        ln_high = sem("f_ln_high")
        ln_low = sem("f_ln_low")
        codes_loaded = [sem(f"codes_loaded{i}") for i in range(2)]
        scales_loaded = [sem(f"scales_loaded{i}") for i in range(2)]
        lined = sem("lined")
        lut = sem("lut")
        scaled = sem("scaled")
        w_high = sem("fw_high")
        w_low = sem("fw_low")
        gate_done = sem("gate_done")
        up_done = sem("up_done")
        silu_done = sem("silu_done")
        h_done = sem("h_done")
        h_high = sem("h_high")
        h_low = sem("h_low")
        down_done = sem("down_done")
        y_added = sem("y_added")
        stored = sem("y_stored")
        sp_tick = sem("f_sp_tick")
        pool_tick = sem("f_pool_tick")
        block = ctx.enter_context(nc.Block())

        NB = B
        NQ = 2 * NB
        ND = 2 * RT
        AHEAD = 4
        PER = 12
        FREE = 2

        def tile_of(k):
            if k < 0:
                return 0, (k + 4) // 2, k % 2
            if k < 4:
                return 1, k // 2, k % 2
            if k < 8:
                return (k - 4) // 2, 2, k % 2
            return 2, (k - 8) // 2, k % 2

        STEPS = [[0, 1], [2, 3], [4], [5], [6], [7], [8], [9], [10, 11]]
        FIRST_STEPS = [[0], [1], [2], [3], [4, 5], [6, 7], [8], [9], [10, 11]]

        def rows_of_step(q):
            return range(4 * (q + 2), 4 * (q + 3)) if q < 2 else ()

        def last_k(last):
            return 8 if last else PER

        def cut_with(k, last):
            if k >= last_k(last):
                return []
            return ([k - 1] if k % 4 else []) + ([k] if k % 4 == 3 else [])

        def weights(chunk, kind, half):
            cols = slice(HALF * half, HALF * half + HALF)
            if kind == 2:
                return dn_h[:, chunk % 2, cols], dn_l[:, chunk % 2, cols]
            return up_h[:, chunk % 2, kind, cols], up_l[:, chunk % 2, kind, cols]

        @block.sync
        def _(sp):
            def load(i, k, t):
                chunk, kind, half = tile_of(k)
                cols = slice(HALF * half, HALF * half + HALF)
                code = dram["codes"][bass.ds(2 * i + chunk, 1), kind, :, cols].rearrange("a p n -> p (a n)")
                scale = [dram["scales"][bass.ds(2 * i + chunk, 1), kind, s, cols].broadcast_to([P // 2, HALF])
                         for s in range(2)]
                slot = k % 2
                if k > -3:
                    sp.wait_ge(lined, NL * (t - 1))
                    sp.sem_inc(sp_tick, 1)
                sp.dma_start(codes[:, slot, :], code).then_inc(codes_loaded[slot], 16)
                if k > -3:
                    sp.wait_ge(scaled, t - 1)
                    sp.sem_inc(sp_tick, 1)
                for s in range(2):
                    sp.dma_start(scales[P // 2 * s:P // 2 * (s + 1), slot, :], scale[s])\
                        .then_inc(scales_loaded[slot], 16)

            def group(i, last, first=False):
                for k in range(last_k(last)):
                    load(i, k, AHEAD + PER * i + k)

            for k in range(-4, 0):
                load(0, k, AHEAD + k)
                if k in (-3, -1):
                    for q in ((0,) if k == -3 else (1, 2, 3)):
                        sp.dma_start(y[:, 4 * q:4 * q + 4, :], dram["x2"][q, :, :].rearrange("(r p) c -> p r c", p=P))\
                            .then_inc(y_loaded[q], 16)
            group(0, False, True)
            with sp.Fori(1, GROUPS - 1) as i:
                group(i, False)
            group(GROUPS - 1, True)
            for r in range(RT):
                sp.wait_ge(y_added, ND * (GROUPS - 1) + 2 * (r + 1))
                sp.dma_start(dram["out"][P * r:P * r + P, :], y[:, r, :]).then_inc(stored, 16)
            sp.wait_ge(stored, 16 * RT)

        @block.gpsimd
        def _(pool):
            nc.gpsimd.memset(ident[:, :], 0.0).then_inc(consts, 1)
            nc.gpsimd.memset(minus_half[:, :], -0.5).then_inc(consts, 1)
            nc.gpsimd.memset(zero[:, :], 0.0).then_inc(consts, 1)
            pool.wait_ge(consts, 3)
            nc.gpsimd.affine_select(out=ident[:, :], in_=ident[:, :], compare_op=ALU.not_equal, fill=1.0, base=0,
                                    pattern=[[-1, P]], channel_multiplier=1).then_inc(consts, 1)

            def held(ge_sem, value):
                pool.wait_ge(ge_sem, value)
                pool.sem_inc(pool_tick, 1)

            def scale(i, k):
                t, w = AHEAD + PER * i + k, w32[:, k % 2, :]
                held(scales_loaded[k % 2], 32 * (PER // 2 * i + (AHEAD + k) // 2 + 1))
                held(lut, LUT * (t + 1))
                nc.gpsimd.tensor_tensor(w, w, scales[:, k % 2, :], ALU.mult).then_inc(scaled, 1)

            def cut_low(i, k):
                w_h, w_l = weights(*tile_of(k))
                held(w_high, AHEAD + PER * i + k + 1)
                nc.gpsimd.tensor_tensor(w_l, w32[:, k % 2, :], w_h, ALU.subtract).then_inc(w_low, 1)

            def ln_root(r):
                s = slice(r % SLOTS, r % SLOTS + 1)
                pool.wait_ge(ln_stat, 4 * r + 4)
                nc.gpsimd.tensor_tensor(rstd[:, s], var_eps[:, s], minus_half[:, :], ALU.pow).then_inc(ln_rstd, 1)
                nc.gpsimd.tensor_tensor(neg_mean[:, s], zero[:, :], mean_var[:, r % SLOTS, 0:1], ALU.subtract)\
                    .then_inc(ln_rstd, 1)
                pool.wait_ge(ln_rstd, 3 * r + 2)
                nc.gpsimd.tensor_tensor(shift[:, s], neg_mean[:, s], rstd[:, s], ALU.mult).then_inc(ln_rstd, 1)

            def hidden_low(i, q):
                cols = slice(T * (q % NB), T * (q % NB) + T)
                held(h_high, NQ * i + q + 1)
                nc.gpsimd.tensor_tensor(hT_l[:, q // NB, cols], h32[:, q % 2, :], hT_h[:, q // NB, cols],
                                        ALU.subtract).then_inc(h_low, 1)

            def group(i, last, first=False):
                for q, ks in enumerate(FIRST_STEPS if first else STEPS):
                    early = first and q < NB
                    if q < NQ and not early:
                        hidden_low(i, q)
                    for k in ks:
                        if k < last_k(last):
                            scale(i, k)
                        for c in cut_with(k, last):
                            cut_low(i, c)
                    if early:
                        for r in rows_of_step(q):
                            if r + LEAD < RT:
                                ln_root(r + LEAD)
                        hidden_low(i, q)

            pool.sem_inc(h_low, FREE)
            for k in range(-4, 0):
                scale(0, k)
                cut_low(0, k)
            for r in range(8 + LEAD):
                ln_root(r)
            group(0, False, True)
            with pool.Fori(1, GROUPS - 1) as i:
                group(i, False)
            group(GROUPS - 1, True)

        @block.tensor
        def _(pe):
            def ln_turn(r):
                for half in range(2):
                    pe.wait_ge(ln_xn, 2 * r + half + 1)
                    if r >= 2:
                        pe.wait_ge(ln_low, 2 * (r - 2) + half + 1)
                    for c in range(4):
                        mm = nc.tensor.transpose(bank[DOWN + 2 * (r % 2) + half][:, P * c:P * c + P],
                                                 xn[:, half, P * c:P * c + P], ident[:, :])
                    mm.then_inc(ln_turned, 1)

            def gate_up(i, chunk, first=False):
                pe.wait_ge(w_low, AHEAD + PER * i + 4 * chunk)
                for nb in range(NB):
                    n = NB * chunk + nb
                    cols = slice(T * nb, T * nb + T)
                    if first:
                        pe.wait_ge(ln_low, 8 * (nb + 1))
                    for kind in range(2):
                        if n >= 2:
                            pe.wait_ge((silu_done, h_done)[kind], NQ * i + n - 1)
                        for m in range(3 * CT):
                            c = m // 3
                            w, x = ((up_h, xT_h), (up_h, xT_l), (up_l, xT_h))[m % 3]
                            mm = nc.tensor.matmul(bank[(GATE, UP)[kind] + n % 2][:, :],
                                                  w[:, chunk, kind, P * c:P * c + P], x[:, c, cols],
                                                  start=(m == 0), stop=(m == 3 * CT - 1))
                            if m == 3 * CT - 1:
                                mm.then_inc((gate_done, up_done)[kind], 1)
                            if first and nb < NB - 1 and kind == 0 and m % 6 == 5:
                                ln_turn(4 * (nb + 1) + m // 6)

            def down(i):
                pe.wait_ge(w_low, AHEAD + PER * i + 8)
                for d in range(ND):
                    r, half = d // 2, d % 2
                    if d % 8 == 0:
                        pe.wait_ge(h_low, FREE + NQ * i + NB + d // 8 + 1)
                    if d >= 4:
                        pe.wait_ge(y_added, ND * i + d - 3)
                    rows, cols = slice(P * r, P * r + P), slice(HALF * half, HALF * half + HALF)
                    for m in range(6):
                        h, w = ((hT_h, dn_h), (hT_h, dn_l), (hT_l, dn_h))[m % 3]
                        mm = nc.tensor.matmul(bank[DOWN + d % 4][:, :], h[:, m // 3, rows], w[:, m // 3, cols],
                                              start=(m == 0), stop=(m == 5))
                    mm.then_inc(down_done, 1)

            pe.wait_ge(consts, 4)
            for r in range(4):
                ln_turn(r)
            gate_up(0, 0, True)
            gate_up(0, 1)
            down(0)
            with pe.Fori(1, GROUPS) as i:
                gate_up(i, 0)
                gate_up(i, 1)
                down(i)

        @block.scalar
        def _(act):
            def draw_lines(i, k):
                t, slot = AHEAD + PER * i + k, k % 2
                act.wait_ge(codes_loaded[slot], 16 * (PER // 2 * i + (AHEAD + k) // 2 + 1))
                for m, (slope, intercept) in enumerate(LINES):
                    if k > -4:
                        act.wait_ge(lut, LUT * (t - 1) + USED_BY[m])
                    nc.scalar.activation(line[:, m, :], codes[:, slot, :], ACT.Copy, scale=slope, bias=intercept)\
                        .then_inc(lined, 1)

            def cut_high(i, k):
                act.wait_ge(scaled, AHEAD + PER * i + k + 1)
                nc.scalar.activation(weights(*tile_of(k))[0], w32[:, k % 2, :], ACT.Copy).then_inc(w_high, 1)

            def ln_normal(r, half):
                s = r % SLOTS
                if half == 0:
                    act.wait_ge(ln_rstd, 3 * r + 3)
                nc.scalar.activation(xn[:, half, :], y[:, r, HALF * half:HALF * half + HALF], ACT.Identity,
                                     bias=shift[:, s:s + 1], scale=rstd[:, s:s + 1])\
                    .then_inc(ln_xn, 1)

            def ln_rows(rows):
                for r in rows:
                    for half in range(2):
                        act.wait_ge(ln_turned, 2 * r + half + 1)
                        nc.scalar.activation(xT_h[:, 4 * half:4 * half + 4, P * r:P * r + P],
                                             bank[DOWN + 2 * (r % 2) + half][:, :].rearrange("p (c n) -> p c n", n=P),
                                             ACT.Copy).then_inc(ln_high, 1)
                        if r + 1 < RT:
                            ln_normal(r + 1, half)

            def gate_silu(i, q):
                act.wait_ge(gate_done, NQ * i + q + 1)
                act.wait_ge(h_low, FREE + NQ * i + q - 1)
                nc.scalar.activation(h32[:, q % 2, :], bank[GATE + q % 2][:, :], ACT.Silu, scale=1.0 / F_SCALE)\
                    .then_inc(silu_done, 1)

            def hidden_high(i, q):
                act.wait_ge(h_done, NQ * i + q + 1)
                nc.scalar.activation(hT_h[:, q // NB, T * (q % NB):T * (q % NB) + T], h32[:, q % 2, :],
                                     ACT.Copy).then_inc(h_high, 1)

            def group(i, last, first=False):
                for q, ks in enumerate(FIRST_STEPS if first else STEPS):
                    early = first and q < NB
                    if q < NQ and not early:
                        gate_silu(i, q)
                    for n, k in enumerate(ks):
                        if k + 1 < (last_k(last) if last else PER + 1):
                            draw_lines(i, k + 1)
                        if n == 0 and q < NQ and not early:
                            hidden_high(i, q)
                        for c in cut_with(k, last):
                            cut_high(i, c)
                    if early:
                        gate_silu(i, q)
                        ln_rows(rows_of_step(q))
                        hidden_high(i, q)

            draw_lines(0, -4)
            for k in range(-4, 0):
                if k < -1:
                    draw_lines(0, k + 1)
                cut_high(0, k)
            for half in range(2):
                ln_normal(0, half)
            ln_rows(range(8))
            draw_lines(0, 0)
            group(0, False, True)
            with act.Fori(1, GROUPS - 1) as i:
                group(i, False)
            group(GROUPS - 1, True)

        @block.vector
        def _(dve):
            def look_up(i, k, steps=range(LUT)):
                t = AHEAD + PER * i + k
                for n in steps:
                    if n in (0, 4):
                        dve.wait_ge(lined, NL * t + (6, NL)[n // 4])
                    if n >= 7:
                        dve.wait_ge(lut, LUT * t + n)
                    elif n >= 2:
                        dve.wait_ge(lut, LUT * t + n - 1)
                    w = w32[:, k % 2, :]
                    if n < 2:
                        op = nc.vector.scalar_tensor_tensor(line[:, 2 * n + 1, :], line[:, 2 * n, :], 0.0,
                                                            line[:, 2 * n + 1, :], *((ALU.max,) * 2, (ALU.min,) * 2)[n])
                    elif n < 7:
                        op = nc.vector.tensor_tensor(line[:, n + 2, :], line[:, (1, 3)[n - 2] if n < 4 else n, :],
                                                     line[:, n + 2, :], (ALU.max, ALU.min)[n % 2])
                    else:
                        if k >= -2:
                            dve.wait_ge(w_low, t - 1)
                        op = nc.vector.tensor_tensor(w, line[:, NL - 1, :], line[:, NL - 2, :], ALU.add)
                    op.then_inc(lut, 1)

            def ln_stats(r):
                s = r % SLOTS
                if r % 4 == 0:
                    dve.wait_ge(y_loaded[r // 4], 16)
                for half in range(2):
                    nc.vector.bn_stats(stats[:, s, half, :], y[:, r, HALF * half:HALF * half + HALF])\
                        .then_inc(ln_stat, 1)
                dve.wait_ge(ln_stat, 4 * r + 2)
                nc.vector.bn_aggr(mean_var[:, s, :], stats[:, s, :, :]).then_inc(ln_stat, 1)
                dve.wait_ge(ln_stat, 4 * r + 3)
                nc.vector.tensor_scalar(var_eps[:, s:s + 1], mean_var[:, s, 1:2], EPS, None, ALU.add)\
                    .then_inc(ln_stat, 1)

            def ln_rows(rows):
                for r in rows:
                    for half in range(2):
                        dve.wait_ge(ln_high, 2 * r + half + 1)
                        cols = (slice(None), slice(4 * half, 4 * half + 4), slice(P * r, P * r + P))
                        nc.vector.tensor_tensor(xT_l[cols], bank[DOWN + 2 * (r % 2) + half][:, :]
                                                .rearrange("p (c n) -> p c n", n=P), xT_h[cols], ALU.subtract)\
                            .then_inc(ln_low, 1)
                    if r + LEAD < RT:
                        ln_stats(r + LEAD)

            def hidden(i, q):
                dve.wait_ge(silu_done, NQ * i + q + 1)
                dve.wait_ge(up_done, NQ * i + q + 1)
                nc.vector.scalar_tensor_tensor(h32[:, q % 2, :], bank[UP + q % 2][:, :], H_SCALE / F_SCALE,
                                               h32[:, q % 2, :], ALU.mult, ALU.mult).then_inc(h_done, 1)

            def add_down(i, d):
                cols = y[:, d // 2, HALF * (d % 2):HALF * (d % 2) + HALF]
                dve.wait_ge(down_done, ND * i + d + 1)
                nc.vector.scalar_tensor_tensor(cols, bank[DOWN + d % 4][:, :], 1.0 / (H_SCALE * F_SCALE),
                                               cols, ALU.mult, ALU.add).then_inc(y_added, 1)

            def group(i, last, first=False):
                for q, ks in enumerate(FIRST_STEPS if first else STEPS):
                    if q == NQ:
                        for d in range(ND):
                            add_down(i, d)
                            if d < LUT * len(ks) and not last:
                                look_up(i, ks[d // LUT], (d % LUT,))
                        continue
                    early = first and q < NB
                    if not early:
                        hidden(i, q)
                    for k in ks:
                        if k < last_k(last):
                            look_up(i, k)
                    if early:
                        hidden(i, q)
                        ln_rows(rows_of_step(q))

            for k in range(-4, 0):
                look_up(0, k)
            for r in range(LEAD):
                ln_stats(r)
            ln_rows(range(8))
            group(0, False, True)
            with dve.Fori(1, GROUPS - 1) as i:
                group(i, False)
            group(GROUPS - 1, True)


def decoder_layer(nc, dram):
    with ExitStack() as ctx:
        t = Attention(nc, ctx)
        attention(nc, t, dram)
    feed_forward(nc, dram)


def kernel(x, ctx_1024, mask_SxS2_ff0, L0_attn_Wq, L0_attn_bq, L0_attn_Wk, L0_attn_bk, L0_attn_Wv, L0_attn_bv,
           L0_ffn_gate_q, L0_ffn_gate_absmax, L0_ffn_up_q, L0_ffn_up_absmax, L0_ffn_down_q, L0_ffn_down_absmax):
    import concourse.bacc as bacc
    from concourse.bass_utils import run_bass_kernel_spmd

    def arr(a):
        return np.asarray(a)

    wk = arr(L0_attn_Wk).T.reshape(CT, P, UNITS, 1, P)
    wv = arr(L0_attn_Wv).T.reshape(CT, P, UNITS, 1, P)
    wq = arr(L0_attn_Wq).T.reshape(CT, P, 2, UNITS, P).transpose(0, 1, 3, 2, 4)
    w = np.concatenate([wk, wq, wv], axis=3).reshape(CT, P, 4 * HALF)
    bq = arr(L0_attn_bq).reshape(2, UNITS, P)
    bias_qk = np.stack([arr(L0_attn_bk).reshape(UNITS, P), bq[0], bq[1]], axis=2).transpose(1, 0, 2)
    ctx4 = arr(ctx_1024).reshape(B, TC, KVX, D)

    def gate_codes(q):
        return arr(q).reshape(MC, P, CT, P).transpose(0, 3, 2, 1).reshape(MC, P, C)

    def gate_scales(s):
        return arr(s).reshape(MC, P, CT, 2).transpose(0, 3, 2, 1).reshape(MC, 2, C)

    codes = np.stack([gate_codes(L0_ffn_gate_q), gate_codes(L0_ffn_up_q),
                      arr(L0_ffn_down_q).reshape(C, MC, P).transpose(1, 2, 0)], axis=1)
    scales = np.stack([gate_scales(L0_ffn_gate_absmax), gate_scales(L0_ffn_up_absmax),
                       arr(L0_ffn_down_absmax).reshape(C, MC, 2).transpose(1, 2, 0)], axis=1)
    arrays = {
        "x": arr(x),
        "w": w,
        "bias_qk": bias_qk,
        "bias_v": arr(L0_attn_bv).reshape(1, KV * D),
        "mask": arr(mask_SxS2_ff0),
        "ctx_kT": ctx4.transpose(0, 3, 2, 1).reshape(B, D, KVX * TC),
        "ctx_v": ctx4.reshape(B, TC, KVX * D),
        "codes": codes,
        "scales": scales,
    }
    arrays = {name: np.ascontiguousarray(a) for name, a in arrays.items()}
    nc = bacc.Bacc("TRN2", target_bir_lowering=False, num_devices=1)
    dram = {name: nc.dram_tensor("in_" + name, a.shape, mybir.dt.from_np(a.dtype), kind="ExternalInput").ap()
            for name, a in arrays.items()}
    dram["x2"] = nc.dram_tensor("x2", [B, T, C], FP32, kind="Internal").ap()
    dram["out"] = nc.dram_tensor("out", [B * T, C], FP32, kind="ExternalOutput").ap()
    decoder_layer(nc, dram)
    result = run_bass_kernel_spmd(nc, [{"in_" + name: a for name, a in arrays.items()}], core_ids=[0])
    return result.results[0]["out"].reshape(B, T, C)
```
